# Optimizing a Trainium2 kernel written in Bass

```python
import numpy as np
import jax
import jax.numpy as jnp

def _softmax(x, axis=-1):
    return jax.nn.softmax(x, axis=axis)

def _gelu(x):
    return jax.nn.gelu(x, approximate=True)

def _silu(x):
    return jax.nn.silu(x)

def _sigmoid(x):
    return jax.nn.sigmoid(x)

def _layernorm(x, axis=-1, eps=1e-05):
    m = jnp.mean(x, axis=axis, keepdims=True)
    v = jnp.var(x, axis=axis, keepdims=True)
    return (x - m) / jnp.sqrt(v + eps)

def _scatter_add(tgt, idx, src, axis=0):
    return tgt.at[idx].add(src)

def _segment_sum(src, seg, n):
    return jax.ops.segment_sum(src, seg, n)
kernel_name = 'mk_metaformer_d1_conv_nchw256_r4_fcadaa'

def setup_inputs(seed: int=0):
    np.random.seed(seed)
    _w = jnp.asarray

    def _rec_inputs():
        import jax
        import jax.numpy as jnp
        _gk = jax.random.key(seed)
        x = -0.0003929 + 0.9999 * jax.random.normal(jax.random.fold_in(_gk, 1), (64, 64, 16, 16), jnp.float32)
        return x
    x = _rec_inputs()

    def _L0_conv_setup():
        import jax, jax.numpy as jnp
        import numpy as np
        A_BIT = 4
        W_BIT = 4
        EPS = 1e-05

        def _ste_round(x, n):
            return x + jax.lax.stop_gradient(jnp.round(x * n) / n - x)

        def quant_act(x):
            n = float(2 ** A_BIT - 1)
            return _ste_round(jnp.clip(x, 0.0, 1.0), n)

        def quant_weight(w):
            n = float(2 ** W_BIT - 1)
            t = jnp.tanh(w)
            t = t / (2.0 * jnp.max(jnp.abs(t))) + 0.5
            return 2.0 * _ste_round(t, n) - 1.0

        def batchnorm(x, gamma, beta):
            mean = jnp.mean(x, axis=(0, 2, 3), keepdims=True)
            var = jnp.var(x, axis=(0, 2, 3), keepdims=True)
            xn = (x - mean) * jax.lax.rsqrt(var + EPS)
            return xn * gamma[None, :, None, None] + beta[None, :, None, None]

        def conv3x3(x, w):
            return jax.lax.conv_general_dilated(x, w, window_strides=(1, 1), padding=((1, 1), (1, 1)), dimension_numbers=('NCHW', 'OIHW', 'NCHW'))
        key = jax.random.key(seed)
        kx, kw1, kw2 = jax.random.split(key, 3)
        N, C, H, W = (64, 64, 16, 16)
        fan = C * 9
        inp = {'x': jax.random.normal(kx, (N, C, H, W), dtype=jnp.float32), 'gamma1': jnp.ones((C,), jnp.float32), 'beta1': jnp.zeros((C,), jnp.float32), 'w1': jax.random.normal(kw1, (C, C, 3, 3), jnp.float32) / np.sqrt(fan), 'gamma2': jnp.ones((C,), jnp.float32), 'beta2': jnp.zeros((C,), jnp.float32), 'w2': jax.random.normal(kw2, (C, C, 3, 3), jnp.float32) / np.sqrt(fan), 'pat': jnp.array([[0, 1, 0], [1, 1, 1], [0, 1, 0]], dtype=jnp.int32)}
        return inp
    _L0_conv_all = _L0_conv_setup()
    _L0_conv_in = {k: v for k, v in _L0_conv_all.items() if k in ('gamma1', 'beta1', 'w1', 'gamma2', 'beta2', 'w2', 'pat')}
    del _L0_conv_all

    def _L0_ffn_setup():
        import jax, jax.numpy as jnp
        import numpy as np
        N_EXPERTS = 8
        TOP_K = 2
        key = jax.random.key(seed)
        ks = jax.random.split(key, 5)
        B, T, C, E, H = (8, 512, 64, 8, 682)
        scale = 1.0 / np.sqrt(C)
        return {'x': jax.random.normal(ks[0], (B, T, C), dtype=jnp.float32), 'router_w': jax.random.normal(ks[1], (E, C), dtype=jnp.float32) * scale, 'w1': jax.random.normal(ks[2], (E, H, C), dtype=jnp.float32) * scale, 'w2': jax.random.normal(ks[3], (E, C, H), dtype=jnp.float32) * (1.0 / np.sqrt(H)), 'w3': jax.random.normal(ks[4], (E, H, C), dtype=jnp.float32) * scale}
    _L0_ffn_all = _L0_ffn_setup()
    _L0_ffn_in = {k: v for k, v in _L0_ffn_all.items() if k in ('router_w', 'w1', 'w2', 'w3')}
    del _L0_ffn_all
    return {'x': x, 'L0_conv_gamma1': _L0_conv_in['gamma1'], 'L0_conv_beta1': _L0_conv_in['beta1'], 'L0_conv_w1': _L0_conv_in['w1'], 'L0_conv_gamma2': _L0_conv_in['gamma2'], 'L0_conv_beta2': _L0_conv_in['beta2'], 'L0_conv_w2': _L0_conv_in['w2'], 'L0_conv_pat': _L0_conv_in['pat'], 'L0_ffn_router_w': _L0_ffn_in['router_w'], 'L0_ffn_w1': _L0_ffn_in['w1'], 'L0_ffn_w2': _L0_ffn_in['w2'], 'L0_ffn_w3': _L0_ffn_in['w3']}

def reference(x, L0_conv_gamma1, L0_conv_beta1, L0_conv_w1, L0_conv_gamma2, L0_conv_beta2, L0_conv_w2, L0_conv_pat, L0_ffn_router_w, L0_ffn_w1, L0_ffn_w2, L0_ffn_w3):
    import jax
    import jax.numpy as jnp

    def _L0_conv_ref(x, gamma1, beta1, w1, gamma2, beta2, w2, pat):
        import jax, jax.numpy as jnp
        import numpy as np
        A_BIT = 4
        W_BIT = 4
        EPS = 1e-05

        def _ste_round(x, n):
            return x + jax.lax.stop_gradient(jnp.round(x * n) / n - x)

        def quant_act(x):
            n = float(2 ** A_BIT - 1)
            return _ste_round(jnp.clip(x, 0.0, 1.0), n)

        def quant_weight(w):
            n = float(2 ** W_BIT - 1)
            t = jnp.tanh(w)
            t = t / (2.0 * jnp.max(jnp.abs(t))) + 0.5
            return 2.0 * _ste_round(t, n) - 1.0

        def batchnorm(x, gamma, beta):
            mean = jnp.mean(x, axis=(0, 2, 3), keepdims=True)
            var = jnp.var(x, axis=(0, 2, 3), keepdims=True)
            xn = (x - mean) * jax.lax.rsqrt(var + EPS)
            return xn * gamma[None, :, None, None] + beta[None, :, None, None]

        def conv3x3(x, w):
            return jax.lax.conv_general_dilated(x, w, window_strides=(1, 1), padding=((1, 1), (1, 1)), dimension_numbers=('NCHW', 'OIHW', 'NCHW'))
        m = pat.astype(jnp.float32)
        out = conv3x3(quant_act(batchnorm(x, gamma1, beta1)), quant_weight(w1) * m)
        out = conv3x3(quant_act(batchnorm(out, gamma2, beta2)), quant_weight(w2) * m)
        return out + x

    def _L0_ffn_ref(x, router_w, w1, w2, w3):
        import jax, jax.numpy as jnp
        import numpy as np
        N_EXPERTS = 8
        TOP_K = 2
        B, T, C = x.shape
        flat = x.reshape(-1, C)
        logits = flat @ router_w.T
        probs = jax.nn.softmax(logits, axis=-1)
        topk_probs, topk_idx = jax.lax.top_k(probs, TOP_K)
        topk_probs = topk_probs / (jnp.sum(topk_probs, axis=-1, keepdims=True) + 1e-09)
        onehot = jax.nn.one_hot(topk_idx, N_EXPERTS, dtype=flat.dtype)
        gates = jnp.einsum('nk,nke->ne', topk_probs, onehot)
        h1 = jnp.einsum('nc,ehc->neh', flat, w1)
        h3 = jnp.einsum('nc,ehc->neh', flat, w3)
        h = jax.nn.silu(h1) * h3
        y = jnp.einsum('neh,ech->nec', h, w2)
        out = jnp.einsum('ne,nec->nc', gates, y)
        return out.reshape(B, T, C)

    def _gn(v, G=32, eps=1e-05):
        B_, C_, H_, W_ = v.shape
        g = v.reshape(B_, G, C_ // G, H_, W_)
        m = jnp.mean(g, axis=(2, 3, 4), keepdims=True)
        s = jnp.var(g, axis=(2, 3, 4), keepdims=True)
        return ((g - m) / jnp.sqrt(s + eps)).reshape(v.shape)

    def _ln_c(v, eps=1e-06):
        m = jnp.mean(v, axis=1, keepdims=True)
        s = jnp.var(v, axis=1, keepdims=True)
        return (v - m) / jnp.sqrt(s + eps)

    def _ln_t(v, eps=1e-05):
        m = jnp.mean(v, axis=-1, keepdims=True)
        s = jnp.var(v, axis=-1, keepdims=True)
        return (v - m) / jnp.sqrt(s + eps)

    def _to_tokens(v):
        B_, C_, H_, W_ = v.shape
        return v.reshape(B_, C_, H_ * W_).transpose(0, 2, 1)

    def _from_tokens(t, like):
        B_, C_, H_, W_ = like.shape
        return t.transpose(0, 2, 1).reshape(B_, C_, H_, W_)
    x = x + _L0_conv_ref(_ln_c(x), L0_conv_gamma1, L0_conv_beta1, L0_conv_w1, L0_conv_gamma2, L0_conv_beta2, L0_conv_w2, L0_conv_pat)
    t = _to_tokens(x)
    t = t + _L0_ffn_ref(_ln_t(t), L0_ffn_router_w, L0_ffn_w1, L0_ffn_w2, L0_ffn_w3)
    x = _from_tokens(t, x)
    return x

_drawn_inputs = setup_inputs


def setup_inputs(seed=0):
    import zlib

    import numpy as np

    out = dict(_drawn_inputs(seed))
    spreads = {'L0_conv_gamma1': (1.0, 0.2),
     'L0_conv_beta1': (0.0, 0.1),
     'L0_conv_gamma2': (1.0, 0.2),
     'L0_conv_beta2': (0.0, 0.1)}
    factors = {}
    for name, (base, spread) in spreads.items():
        noise = np.random.default_rng([zlib.crc32(name.encode()), seed]).standard_normal(out[name].shape)
        drawn = base * np.exp(spread * noise) if base else spread * noise
        out[name] = jnp.asarray(drawn.astype(out[name].dtype))
    for name, factor in factors.items():
        out[name] = (out[name] * factor).astype(out[name].dtype)
    return out
```

```python
from contextlib import ExitStack

import concourse.bass as bass
from concourse import mybir

ALU = mybir.AluOpType
ACT = mybir.ActivationFunctionType
AX = mybir.AxisListType
F32 = mybir.dt.float32
F32R = mybir.dt.float32r
BF16 = mybir.dt.bfloat16
I32 = mybir.dt.int32
RED_MAX = bass.bass_isa.ReduceOp.max

ROUND = 1.5 * 2.0 ** 23
LEVELS = 15.0
NOT_CHOSEN = -1e30


def conv_moe_kernel(nc, x, gamma1, beta1, w1, gamma2, beta2, w2, pat, router_w, ew1, ew2, ew3, out):
    N, C, H, W = x.shape
    E, HID, _ = ew1.shape
    HW = H * W
    HALF = N // 2
    S = 512
    IMG = S // HW
    NS = HALF * HW // S
    G = S // 128
    GH = 2 * G
    TOK = N * HW
    TAPS = 9
    ROW = C + 1
    T = 512
    REG = TOK + T
    DUMMY = E * REG
    NT = 2 * TOK // T + E
    FULL = (2 * TOK - E * (T - 1)) // T // 2 * 2
    NPAD = E * (T // 128)
    HT = HID // 128
    HR = HID - HT * 128
    KT = HT + 1
    WST = (2 * HT + 1) * 128
    TAIL3 = 64
    assert C == 64 and E == 8 and KT == 6 and HR <= 64 and NT % 2 == 0 and NPAD % 2 == 0

    xv = x.rearrange("(h s i) c a b -> h s c i (a b)", h=2, i=IMG)
    outv = out.rearrange("(h s i) c a b -> h s c i (a b)", h=2, i=IMG)
    xs = nc.dram_tensor("expert_rows", [E * REG + T, ROW], F32).ap()
    yout = nc.dram_tensor("result_rows", [2 * TOK, C], F32).ap()
    wsc = nc.dram_tensor("expert_w13", [E * 128, WST], F32).ap()
    w2sc = nc.dram_tensor("expert_w2", [E * 128, KT * C], F32).ap()

    with ExitStack() as ctx:
        def sb(name, shape, dt=F32):
            return ctx.enter_context(nc.sbuf_tensor(name, shape, dt))

        def sem(name):
            return ctx.enter_context(nc.semaphore(name))

        bank = [ctx.enter_context(nc.psum_tensor(f"bank{i}", [128, 512], F32)) for i in range(8)]

        ident = sb("ident", [128, 128])
        same_half = sb("same_half", [128, 128])
        pair = sb("pair", [128, 128])
        half_col = sb("half_col", [128, 2])
        fold = sb("fold", [128, C])
        before = sb("before", [128, 128], BF16)
        ident_bf = sb("ident_bf", [128, 128], BF16)
        ones_bf = sb("ones_bf", [128, 128], BF16)
        first_pref = sb("first_pref", [128, GH, E])
        expert_no = sb("expert_no", [128, E])
        region = sb("region", [128, E])
        earlier = sb("earlier", [128, E, E])
        tile_no = sb("tile_no", [128, 1])
        pad_off = sb("pad_off", [128, T // 128, E])
        dest0 = sb("dest0", [128, 2, GH])
        zero_i = sb("zero_i", [128, 4 * ROW], I32)
        pad_rows = sb("pad_rows", [128, 4, ROW])
        eps6 = sb("eps6", [128, 1])
        eps5 = sb("eps5", [128, 1])

        xb = sb("x_all", [128, NS * S])
        yb = sb("y_all", [128, NS * S])
        cb = sb("conv1_all", [128, NS * S])
        gb = sb("gamma_beta", [128, 4])
        bn = sb("bn_stats", [128, 2, NS, 6])
        mv = sb("bn_mean_var", [128, 2, 2])
        mv2 = sb("bn_moments", [128, 2, 2])
        bt = sb("bn_tmp", [128, 2, 4])
        aff = sb("bn_affine", [128, 2, 2])
        wc = sb("conv_w", [C, 2, C * TAPS])
        wmax = sb("conv_w_max", [C, 2])
        wmax_all = sb("conv_w_max_all", [C, 2])
        wrec = sb("conv_w_rec", [C, 2])
        patf = sb("pat_f", [C, TAPS])
        pati = sb("pat_i", [C, TAPS], I32)
        wdup = sb("conv_w_dup", [C, 2, TAPS, 2, C], BF16)
        wblk = sb("conv_w_blocks", [128, 2, TAPS, 128], BF16)
        qt = [sb(f"quant_tmp{u}", [128, S]) for u in range(2)]
        qpad = [sb(f"quant_padded{u}", [128, IMG, H + 2, W + 2], BF16) for u in range(2)]
        sq = [sb(f"squares{u}", [128, S]) for u in range(2)]
        wide = [sb(f"rstd_wide{u}", [128, GH, C]) for u in range(2)]
        st = [sb(f"row_stats{u}", [128, 6, GH]) for u in range(2)]

        x1 = [sb(f"x1_{u}", [128, S]) for u in range(2)]
        cen = sb("centred_rows", [128, GH, C])
        rows = [sb(f"rows{u}", [128, 2, GH, ROW]) for u in range(2)]
        slot_f = sb("slot_f", [128, 2, GH])
        slot = [sb(f"slot{u}", [128, 2, GH], I32) for u in range(2)]
        dest_f = sb("dest_f", [128, 2, GH])
        rw = sb("router_rows", [E, C])
        rwm = sb("router_mean", [E, 1])
        rwc = sb("router_centred", [E, 2, C])
        rwt = sb("router_T", [128, 2 * E])
        lg = sb("logits", [128, NS, GH, E])
        top2 = sb("second_minus_first", [128, NS, GH])
        ra = sb("route_a", [128, GH, E])
        rb = sb("route_b", [128, GH, E])
        m1 = sb("route_max", [128, GH])
        m2 = sb("route_second", [128, GH])
        mm = sb("route_pref", [128, GH])
        oh = [sb(f"one_hot{k}", [128, GH, E]) for k in range(2)]
        chosen = sb("chosen", [128, GH + 1, E], BF16)
        pos = sb("positions", [128, GH + 1, E])
        base = sb("base", [128, E])
        gate = sb("gates", [128, 2, NS, GH])
        gsum = sb("gate_sum", [128, NS, GH])
        tm = sb("tile_map_work", [128, 12, E])
        tcol = sb("tile_map_col", [128, 4])
        tmap = sb("tile_map", [1, 2, 128], I32)
        padf = sb("pad_slot_f", [128, T // 128, E])
        padi = sb("pad_slot", [128, T // 128, E], I32)
        pads = [sb(f"pad_now{u}", [128, 1], I32) for u in range(2)]

        wr = sb("w13_rows", [128, 2, HT, C])
        wt = sb("w13_tail", [128, C])
        wr2 = sb("w2_rows", [C, HID])
        wsp = sb("w13_split", [128, 2 * HT + 1, 2, C])
        wstk = sb("w13_stacked", [128, WST])
        w2s = sb("w2_stacked", [128, KT, C])

        wbuf = [sb(f"w13_{u}", [128, WST], F32R) for u in range(2)]
        w2buf = [sb(f"w2_{u}", [128, KT, C]) for u in range(2)]
        free = [0]

        def carve(*shape):
            n = 1
            for d in shape:
                n *= d
            v = cb[:, free[0]:free[0] + n]
            free[0] += n
            assert free[0] <= NS * S
            if len(shape) == 1:
                return v
            names = "abc"[:len(shape)]
            return v.rearrange(f"p ({' '.join(names)}) -> p {' '.join(names)}",
                               **{names[i]: shape[i] for i in range(1, len(shape))})

        xrow = [carve(4, ROW) for u in range(2)]
        hl = [carve(4, 3, C) for u in range(2)]
        sbuf = [carve(T) for u in range(2)]
        hbuf = [carve(T) for u in range(2)]
        ysb = [carve(T) for u in range(2)]
        yrow = [carve(4, C) for u in range(2)]
        dest_all = sb("dest_all", [128, NT, 4], I32)
        destc = [sb(f"dest_now{u}", [128, 4], I32) for u in range(2)]
        xT = [[sb(f"xT_{p}_{u}", [128, T], F32R) for u in range(2)] for p in ("hi_lo", "lo_hi")]
        yk = [[yb[:, (2 * k + u) * GH * C:(2 * k + u + 1) * GH * C] for u in range(2)] for k in range(2)]

        x_in = [sem(f"x_in{u}") for u in range(2)]
        small_in = sem("small_in")
        const_p = sem("const_pool")
        const_v = sem("const_vector")
        p_step = sem("pool_step")
        v_step = sem("vector_step")
        mean_rdy = sem("mean_ready")
        cen_rdy = sem("centred_ready")
        sq_rdy = sem("squares_ready")
        var_rdy = sem("var_ready")
        sd_rdy = sem("sd_ready")
        rstd_rdy = sem("rstd_ready")
        bc_rdy = sem("rstd_spread_ready")
        y_rdy = sem("y_ready")
        x_res = sem("x_plus_y_done")
        th_rdy = sem("tanh_ready")
        wm_rdy = sem("wmax_ready")
        wma_rdy = sem("wmax_all_ready")
        wd_rdy = sem("conv_w_dup_ready")
        wT_rdy = sem("conv_w_turned")
        wb_rdy = sem("conv_w_blocks_ready")
        agg_rdy = sem("moments_ready")
        pr_rdy = sem("moments_paired")
        bsd_rdy = sem("bn_sd_ready")
        bva_rdy = sem("bn_var_ready")
        aff_rdy = sem("affine_ready")
        q_rdy = sem("quant_affine_ready")
        qp_rdy = sem("quant_padded_ready")
        cv_rdy = sem("conv_ready")
        c1_rdy = sem("conv1_copied")
        x1_rdy = sem("x1_ready")
        x1_kept = sem("x1_kept")
        rT_rdy = sem("rows_turned")
        lg_rdy = sem("logits_ready")
        rc_rdy = sem("rows_centred")
        rs_rdy = sem("row_squares_ready")
        rv_rdy = sem("row_var_ready")
        rsd_rdy = sem("row_sd_ready")
        row_rdy = sem("row_ready")
        row2_rdy = sem("row_copy_ready")
        ch_rdy = sem("chosen_ready")
        pos_rdy = sem("positions_ready")
        slot_rdy = sem("slots_ready")
        scat = [sem(f"row_scatter{u}") for u in range(2)]
        rr_rdy = sem("router_rows_centred")
        rT2 = sem("router_turned")
        rwt_rdy = sem("router_T_ready")
        w_in = sem("w_in")
        w_zero = sem("w_zeroed")
        ws_rdy = sem("w_split_ready")
        wt_ps = sem("w_turned")
        wt_sb = sem("w_stacked")
        w_out = sem("w_out")
        ex_rdy = sem("exp_ready")
        ex_go = sem("exp_go")
        dummy_out = sem("dummy_out")
        map_rdy = sem("map_cols_ready")
        mapT_rdy = sem("map_turned")
        tmap_rdy = sem("tile_map_ready")
        padi_rdy = sem("pad_slots_ready")
        pad_cp = sem("pad_slot_copied")
        pad_out = [sem(f"pad_out{u}") for u in range(2)]
        xr_in = [sem(f"tile_rows_in{u}") for u in range(2)]
        wt_in = [sem(f"tile_w_in{u}") for u in range(2)]
        split_rdy = sem("split_ready")
        xt_rdy = sem("xT_ready")
        xt_sb = sem("xT_copied")
        h1_rdy = sem("h1_ready")
        h3_rdy = sem("h3_ready")
        silu_rdy = sem("silu_ready")
        mul_rdy = sem("hidden_ready")
        w2_rdy = sem("w2_done")
        y_sb = sem("y_copied")
        ro_rdy = sem("rows_out_ready")
        yr_sb = sem("y_rows_ready")
        y_out = [sem(f"y_scatter{u}") for u in range(2)]
        yk_in = [sem(f"results_in{u}") for u in range(2)]
        g1_rdy = sem("gated_ready")
        g2_rdy = sem("gated2_ready")
        fin_rdy = sem("sum_ready")
        o_rdy = sem("out_ready")
        o_out = sem("out_stored")
        passed = sem("passed")

        def wait_apart(eng, sem_, value):
            eng.wait_ge(sem_, value)
            eng.sem_inc(passed, 1)

        def stripe(t, s):
            return t[:, bass.ds(s * S, S)]

        def pipelined(eng, front, back, n):
            front(0, 0)
            front(1, 1)
            back(0, 0)
            front(2, 0)
            back(1, 1)
            with eng.Fori(1, n // 2 - 1) as turn:
                i = 2 * turn
                front(i + 1, 1)
                back(i, 0)
                front(i + 2, 0)
                back(i + 1, 1)
            front(n - 1, 1)
            back(n - 2, 0)
            back(n - 1, 1)

        def tiles(eng, tile):
            tile(0, 0, first=True)
            tile(1, 1)
            tile(2, 0)
            tile(3, 1)
            with eng.Fori(2, NT // 2 - 1) as pair_:
                j = 2 * pair_
                tile(j, 0)
                tile(j + 1, 1)
            tile(NT - 2, 0)
            tile(NT - 1, 1, last=True)

        conv_ps = [bank[0], bank[1]]
        w_bf = bank[2][:, :].bitcast(BF16)

        h1_ps, h3_ps, y_ps = bank[0:2], bank[2:4], bank[4:6]
        xt_ps, ro_ps = bank[6], bank[7]

        def w_bank(b):
            return bank[6 + b % 2]

        mean_ps, var_ps, bc_ps = bank[0:2], [bank[4], bank[5]], bank[6:8]
        rT_ps, lg_ps, pos_ps = bank[2][:, :], bank[3][:, 0:GH * E], bank[4][:, 0:(GH + 1) * E]
        fin_ps = bank[0:2]

        def gate_of(k, s):
            return gate[:, k, bass.ds(s, 1), :].rearrange("p a g -> p (a g)").unsqueeze(2).broadcast_to([128, GH, C])

        NSMALL = 8 + 2 + 1 + 1
        block = ctx.enter_context(nc.Block())

        @block.sync
        def _(sp):
            for k, w in enumerate((w1, w2)):
                sp.dma_start(wc[:, k, :], w.rearrange("o i a b -> o (i a b)")).then_inc(small_in, 16)
            sp.dma_start(pati[:], pat.rearrange("a b -> (a b)").partition_broadcast(C)).then_inc(small_in, 16)
            sp.dma_start(rw[:], router_w).then_inc(small_in, 16)
            for k, v in enumerate((gamma1, beta1, gamma2, beta2)):
                for h in range(2):
                    sp.dma_start(gb[64 * h:64 * h + 64, k:k + 1],
                                 v.rearrange("(c a) -> c a", a=1)).then_inc(small_in, 16)
            for s in range(NS):
                if s >= 2:
                    sp.wait_ge(x_in[s % 2], 32 * (s // 2))
                for h in range(2):
                    sp.dma_start(xb[64 * h:64 * h + 64, s * S:(s + 1) * S].rearrange("c (i p) -> c i p", i=IMG),
                                 xv[h, s]).then_inc(x_in[s % 2], 16)
            sp.wait_ge(const_v, 1)
            sp.dma_start(xs[DUMMY:DUMMY + T, :].rearrange("(p g) c -> p g c", g=4),
                         pad_rows[:]).then_inc(dummy_out, 16)
            sp.wait_ge(w_zero, 1)
            with sp.Fori(0, E) as e:
                for k, w in enumerate((ew1, ew3)):
                    we = w.rearrange("e h c -> e (h c)")
                    sp.dma_start(wr[:, k, :, :].rearrange("p t c -> p (t c)"),
                                 we[bass.ds(e, 1), 0:HT * 128 * C].rearrange("a (p n) -> (a p) n", p=128)
                                 ).then_inc(w_in, 16)
                    sp.dma_start(wt[TAIL3 * k:TAIL3 * k + HR, :],
                                 we[bass.ds(e, 1), HT * 128 * C:HID * C].rearrange("a (p n) -> (a p) n", p=HR)
                                 ).then_inc(w_in, 16)
                sp.dma_start(wr2[:], ew2[bass.ds(e, 1), :, :].rearrange("a c h -> (a c) h")).then_inc(w_in, 16)
                sp.wait_ge(wt_sb, 4 * e + 4)
                sp.dma_start(wsc[bass.ds(e * 128, 128), :], wstk[:]).then_inc(w_out, 16)
                sp.dma_start(w2sc[bass.ds(e * 128, 128), :], w2s[:].rearrange("p k c -> p (k c)")).then_inc(w_out, 16)
                wait_apart(sp, w_out, 32 * e + 32)

            sp.wait_ge(dummy_out, 16)
            sp.wait_ge(tmap_rdy, 1)
            for u in range(2):
                sp.wait_ge(scat[u], 16 * 2 * GH * (NS // 2))

            def load(j, u):
                src = sp.value_load(tmap[0:1, 0, bass.ds(j, 1)], min_val=0, max_val=E * REG)
                exp = sp.value_load(tmap[0:1, 1, bass.ds(j, 1)], min_val=0, max_val=(E - 1) * 128)
                sp.wait_ge(split_rdy, j + 1)
                sp.dma_start(xrow[u], xs[bass.ds(src, T), :].rearrange("(p g) c -> p g c", g=4)
                             ).then_inc(xr_in[u], 16)
                if not isinstance(j, int):
                    sp.wait_ge(w2_rdy, KT * j - KT + 2)
                sp.dma_start(wbuf[u][:].bitcast(F32), wsc[bass.ds(exp, 128), :]).then_inc(wt_in[u], 16)
                sp.dma_start(w2buf[u][:].rearrange("p k c -> p (k c)"), w2sc[bass.ds(exp, 128), :]
                             ).then_inc(wt_in[u], 16)

            load(0, 0)
            load(1, 1)
            with sp.Fori(1, FULL // 2) as pair_:
                j = 2 * pair_
                load(j, 0)
                load(j + 1, 1)
            for u in range(2):
                sp.wait_ge(pad_out[u], 16 * NPAD // 2)
            with sp.Fori(FULL // 2, NT // 2) as pair_:
                j = 2 * pair_
                load(j, 0)
                load(j + 1, 1)

            for u in range(2):
                sp.wait_ge(y_out[u], 64 * (NT // 2))

            def results(s, u):
                sp.wait_ge(fin_rdy, s + 1)
                for k in range(2):
                    sp.dma_start(yk[k][u], yout[bass.ds(s * 2 * S + k * TOK, 2 * S), :]
                                 .rearrange("(p g) c -> p (g c)", g=GH)).then_inc(yk_in[u], 16)

            def store(s, u):
                sp.wait_ge(o_rdy, s + 3)
                for h in range(2):
                    sp.dma_start(outv[h, bass.ds(s, 1)].rearrange("a c i p -> (a c) i p"),
                                 stripe(xb, s)[64 * h:64 * h + 64, :].rearrange("c (i p) -> c i p", i=IMG)
                                 ).then_inc(o_out, 16)

            pipelined(sp, results, store, NS)
            sp.wait_ge(o_out, 32 * NS)

        @block.gpsimd
        def _(pool):
            def made(ins, n=[0]):
                n[0] += 1
                ins.then_inc(p_step, 1)
                pool.wait_ge(p_step, n[0])

            made(nc.gpsimd.memset(ident[:], 0.0))
            made(nc.gpsimd.affine_select(out=ident[:], in_=ident[:], compare_op=ALU.not_equal, fill=1.0,
                                         base=0, pattern=[[-1, 128]], channel_multiplier=1))
            made(nc.gpsimd.tensor_copy(ident_bf[:], ident[:]))
            made(nc.gpsimd.memset(before[:], 1.0))
            made(nc.gpsimd.affine_select(out=before[:], in_=before[:], compare_op=ALU.is_gt, fill=0.0,
                                         base=0, pattern=[[1, 128]], channel_multiplier=-1))
            iota = lambda t, pattern, base, cm: made(nc.gpsimd.iota(t, pattern=pattern, base=base,
                   channel_multiplier=cm, allow_small_or_imprecise_dtypes=True))
            iota(first_pref[:], [[0, GH], [-1, E]], E, 0)
            iota(expert_no[:], [[1, E]], 0, 0)
            iota(region[:], [[1, E]], 0, 0)
            iota(earlier[:], [[1, E], [-1, E]], 0, 0)
            iota(tile_no[:], [[0, 1]], 0, 1)
            iota(pad_off[:], [[128, T // 128], [0, E]], 0, 1)
            iota(dest0[:], [[TOK, 2], [1, GH]], 0, GH)
            nc.gpsimd.memset(ones_bf[:], 1.0).then_inc(const_p, 1)

            pool.wait_ge(wm_rdy, 1)
            nc.gpsimd.partition_all_reduce(wmax_all[:], wmax[:], C, RED_MAX).then_inc(wma_rdy, 1)

            with pool.Fori(0, NS) as s:
                pool.wait_ge(y_rdy, s + 1)
                nc.gpsimd.tensor_tensor(stripe(xb, s), stripe(xb, s), stripe(yb, s), ALU.add).then_inc(x_res, 1)

            def scatter(s, u):
                wait_apart(pool, slot_rdy, s + 1)
                wait_apart(pool, row_rdy, s + 1)
                wait_apart(pool, row2_rdy, s + 1)
                for k in range(2):
                    for g in range(GH):
                        nc.gpsimd.indirect_dma_start(
                            xs, bass.IndirectOffsetOnAxis(ap=slot[u][:, k, g:g + 1], axis=0),
                            rows[u][:, k, g, :], None).then_inc(scat[u], 16)

            with pool.Fori(0, NS // 2) as pair_:
                i = 2 * pair_
                scatter(i, 0)
                scatter(i + 1, 1)

            def scatter_y(j, u):
                wait_apart(pool, yr_sb, j + 2)
                for g in range(4):
                    nc.gpsimd.indirect_dma_start(
                        yout, bass.IndirectOffsetOnAxis(ap=destc[u][:, g:g + 1], axis=0),
                        yrow[u][:, g, :], None, bounds_check=2 * TOK - 1, oob_is_err=False
                    ).then_inc(y_out[u], 16)

            def scatter_pad(n, u):
                if not isinstance(n, int) or n >= 2:
                    pool.wait_ge(pad_out[u], (n - u) * 8)
                nc.gpsimd.tensor_copy(pads[u][:], padi_flat[:, bass.ds(n, 1)]).then_inc(pad_cp, 1)
                wait_apart(pool, pad_cp, n + 1)
                nc.gpsimd.indirect_dma_start(
                    xs, bass.IndirectOffsetOnAxis(ap=pads[u][:], axis=0),
                    pad_rows[:, 0, :], None).then_inc(pad_out[u], 16)

            padi_flat = padi[:].rearrange("p i e -> p (i e)")
            pool.wait_ge(padi_rdy, 1)
            for u in range(2):
                scatter_pad(u, u)
                scatter_y(u, u)
            with pool.Fori(1, NPAD // 2) as pair_:
                j = 2 * pair_
                for u in range(2):
                    scatter_pad(j + u, u)
                    scatter_y(j + u, u)
            with pool.Fori(NPAD // 2, NT // 2) as pair_:
                j = 2 * pair_
                for u in range(2):
                    scatter_y(j + u, u)

            def gate2(s, u):
                pool.wait_ge(yk_in[u], (s - u) * 16 + 32)
                v = yk[1][u].rearrange("p (g c) -> p g c", g=GH)
                nc.gpsimd.tensor_tensor(v, v, gate_of(1, s), ALU.mult).then_inc(g2_rdy, 1)

            with pool.Fori(0, NS // 2) as pair_:
                i = 2 * pair_
                gate2(i, 0)
                gate2(i + 1, 1)

        @block.scalar
        def _(act):
            act.sem_inc(c1_rdy, 2)
            act.sem_inc(x1_kept, 2)
            act.sem_inc(xt_sb, 1)
            act.sem_inc(y_sb, 2)
            act.wait_ge(small_in, 16 * NSMALL)
            nc.scalar.activation(wc[:], wc[:], ACT.Tanh).then_inc(th_rdy, 1)

            def square(s, u):
                act.wait_ge(cen_rdy, s + 3)
                act.wait_ge(var_rdy, s + 1)
                nc.scalar.activation(sq[u][:], stripe(yb, s), ACT.Square).then_inc(sq_rdy, 1)

            def sd(s, u):
                act.wait_ge(sd_rdy, 2 * s + 1)
                nc.scalar.activation(st[u][:, 1, :], st[u][:, 0, :], ACT.Sqrt).then_inc(sd_rdy, 1)

            pipelined(act, square, sd, NS)

            def affine(l, s, u):
                act.wait_ge(qp_rdy, s + l * NS + 1)
                nc.scalar.activation(qt[u][:], stripe(cb if l else yb, s), ACT.Relu,
                                     bias=aff[:, l, 1:2], scale=aff[:, l, 0:1]).then_inc(q_rdy, 1)

            def keep_conv1(s, u):
                act.wait_ge(cv_rdy, s + 3)
                nc.scalar.activation(stripe(cb, s), conv_ps[u][:], ACT.Copy).then_inc(c1_rdy, 1)

            act.wait_ge(bva_rdy, 1)
            nc.scalar.activation(bt[:, 0, 1:2], bt[:, 0, 0:1], ACT.Sqrt).then_inc(bsd_rdy, 1)
            act.wait_ge(aff_rdy, 1)
            pipelined(act, lambda s, u: affine(0, s, u), keep_conv1, NS)
            act.wait_ge(bva_rdy, 2)
            nc.scalar.activation(bt[:, 1, 1:2], bt[:, 1, 0:1], ACT.Sqrt).then_inc(bsd_rdy, 1)
            act.wait_ge(aff_rdy, 2)

            def route(s, u):
                act.wait_ge(x1_rdy, s + 3)
                nc.scalar.activation(stripe(xb, s), x1[u][:], ACT.Copy).then_inc(x1_kept, 1)
                act.wait_ge(rc_rdy, s + 2)
                nc.scalar.activation(sq[u][:], cen[:].rearrange("p g c -> p (g c)"), ACT.Square).then_inc(rs_rdy, 1)
                act.wait_ge(rsd_rdy, 2 * s + 1)
                nc.scalar.activation(st[u][:, 1, :], st[u][:, 0, :], ACT.Sqrt).then_inc(rsd_rdy, 1)
                act.wait_ge(row_rdy, s + 1)
                nc.scalar.activation(rows[u][:, 1, :, 0:C], rows[u][:, 0, :, 0:C], ACT.Copy).then_inc(row2_rdy, 1)
                if u == 1:
                    e = (s - 1) // 2
                    for b in range(3):
                        n = min(512, WST - 512 * b)
                        act.wait_ge(wt_ps, 4 * e + b + 1)
                        nc.scalar.activation(wstk[:, 512 * b:512 * b + n].bitcast(F32R), w_bank(b)[:, 0:n],
                                             ACT.Copy).then_inc(wt_sb, 1)
                    act.wait_ge(wt_ps, 4 * e + 4)
                    nc.scalar.activation(w2s[:, 0:HT, :].rearrange("p k c -> p (k c)"), w_bank(3)[:, 0:HT * C],
                                         ACT.Copy)
                    nc.scalar.activation(w2s[0:HR, HT, :], w_bank(3)[0:HR, HT * C:KT * C],
                                         ACT.Copy).then_inc(wt_sb, 1)

            pipelined(act, lambda s, u: affine(1, s, u), route, NS)

            act.wait_ge(ex_go, 1)
            nc.scalar.activation(lg[:], lg[:], ACT.Exp).then_inc(ex_rdy, 1)
            nc.scalar.activation(top2[:], top2[:], ACT.Exp).then_inc(ex_rdy, 1)

            def silu(j, k):
                m = 128 if k < HT else HR
                act.wait_ge(h1_rdy, KT * j + k + 1)
                nc.scalar.activation(sbuf[k % 2][0:m, :], h1_ps[k % 2][0:m, :], ACT.Silu).then_inc(silu_rdy, 1)

            def copy_xT(j, u, p):
                act.wait_ge(xt_rdy, 2 * j + p + 1)
                nc.scalar.activation(xT[p][u][:], xt_ps[:], ACT.Copy).then_inc(xt_sb, 1)

            def copy_y(j, u):
                act.wait_ge(w2_rdy, KT * j + KT + 2)
                act.wait_ge(ro_rdy, j + 1)
                nc.scalar.activation(ysb[u], y_ps[u][:], ACT.Copy).then_inc(y_sb, 1)

            def tile(j, u, first=False, last=False):
                silu(j, 0)
                if not first:
                    copy_y(j - 1, 1 - u)
                silu(j, 1)
                silu(j, 2)
                if not last:
                    copy_xT(j + 1, 1 - u, 0)
                silu(j, 3)
                if not last:
                    copy_xT(j + 1, 1 - u, 1)
                silu(j, 4)
                silu(j, 5)

            copy_xT(0, 0, 0)
            copy_xT(0, 0, 1)
            tiles(act, tile)
            copy_y(NT - 1, 1)

        @block.vector
        def _(dve):
            class Chain:
                base = 0

                def begin(self, n=0, per=0):
                    self.at, self.k, self.per = n, 0, per
                    return self

                def __call__(self, ins):
                    self.k += 1
                    ins.then_inc(self.sem, 1)
                    dve.wait_ge(self.sem, self.base + self.at * self.per + self.k)

                def end(self):
                    assert self.k == self.per, self.k

            def chain(name):
                c = Chain()
                c.sem = sem(name)
                return c

            V = nc.vector
            one = chain("vector_straight").begin()
            for s_ in (cen_rdy, qp_rdy, x1_rdy, split_rdy, mul_rdy, o_rdy):
                dve.sem_inc(s_, 2)
            for s_ in (rc_rdy, ch_rdy, yr_sb):
                dve.sem_inc(s_, 1)

            V.memset(wt[:], 0.0)
            V.memset(w2s[:], 0.0).then_inc(w_zero, 1)
            one(V.memset(zero_i[:], 0))
            one(V.tensor_copy(pad_rows[:].bitcast(I32).rearrange("p g c -> p (g c)"), zero_i[:]))
            one(V.memset(pad_rows[:].bitcast(I32)[:, :, C:ROW], 1 << 20))
            one(V.memset(same_half[:], 0.0))
            V.memset(same_half[0:64, 0:64], 1.0 / C)
            one(V.memset(same_half[64:128, 64:128], 1.0 / C))
            one(V.memset(half_col[:], 0.0))
            V.memset(half_col[0:64, 0:1], 1.0 / C)
            V.memset(half_col[64:128, 1:2], 1.0 / C)
            V.memset(chosen[:], 0.0)
            V.memset(rwt[:], 0.0)
            V.memset(wblk[:], 0.0)
            for u in range(2):
                V.memset(qpad[u][:], 0.0)
            one(V.memset(dest_f[:], 0.0))
            dve.wait_ge(const_p, 1)
            one(V.tensor_tensor(fold[:], ident[:, 0:C], ident[:, C:2 * C], ALU.add))
            for h in range(2):
                one(V.tensor_scalar(pair[:, C * h:C * h + C], fold[:], 0.5, None, ALU.mult))
            one(V.tensor_scalar(region[:], region[:], float(REG), None, ALU.mult))
            one(V.tensor_scalar(earlier[:], earlier[:], 0.0, None, ALU.is_gt))
            one(V.tensor_copy(base[:], region[:]))
            V.tensor_copy(dest_f[:], dest0[:]).then_inc(const_v, 1)

            dve.wait_ge(th_rdy, 1)
            V.tensor_reduce(wmax[:], wc[:], AX.X, ALU.max, apply_absolute_value=True).then_inc(wm_rdy, 1)
            one(V.tensor_copy(patf[:], pati[:]))
            one(V.tensor_reduce(rwm[:], rw[:], AX.X, ALU.add))
            one(V.tensor_scalar(rwm[:], rwm[:], -1.0 / C, None, ALU.mult))
            V.tensor_scalar(rwc[:, 0, :], rw[:], rwm[:, 0:1], None, ALU.add)
            V.tensor_scalar(rwc[:, 1, :], rw[:], rwm[:, 0:1], None, ALU.add).then_inc(rr_rdy, 1)
            dve.wait_ge(wma_rdy, 1)
            one(V.tensor_scalar(wrec[:], wmax_all[:], 2.0, None, ALU.mult))
            one(V.reciprocal(wrec[:], wrec[:]))
            for k in range(2):
                one(V.tensor_scalar(wc[:, k, :], wc[:, k, :], wrec[:, k:k + 1], 0.5, ALU.mult, ALU.add))
            one(V.tensor_scalar(wc[:], wc[:], LEVELS, ROUND, ALU.mult, ALU.add))
            one(V.tensor_scalar(wc[:], wc[:], -ROUND, 2.0, ALU.add, ALU.mult))
            one(V.tensor_scalar(wc[:], wc[:], -LEVELS, None, ALU.add))
            for k in range(2):
                for d in range(2):
                    ins = V.tensor_tensor(wdup[:, k, :, d, :], wc[:, k, :].rearrange("o (i t) -> o t i", t=TAPS),
                                          patf[:].unsqueeze(2).broadcast_to([C, TAPS, C]), ALU.mult)
            ins.then_inc(wd_rdy, 1)
            def rstd(c, t):
                var, sd_, r, w, _, _ = (t[:, k] for k in range(6))
                c(V.reciprocal(r, sd_))
                c(V.tensor_tensor(w, var, r, ALU.mult))
                c(V.tensor_tensor(w, w, r, ALU.mult))
                c(V.tensor_scalar(w, w, -0.5, 1.5, ALU.mult, ALU.add))
                c(V.tensor_tensor(r, r, w, ALU.mult))

            def centre(s, u):
                dve.wait_ge(mean_rdy, s + 1)
                V.tensor_tensor(stripe(yb, s), stripe(xb, s), mean_ps[u][:], ALU.subtract).then_inc(cen_rdy, 1)

            ln = chain("vector_layernorm")

            def norm(s, u):
                c = ln.begin(s, 6)
                dve.wait_ge(var_rdy, s + 3)
                V.tensor_scalar(st[u][:, 0, :], var_ps[u][:, 0:GH], 1e-6, None, ALU.add).then_inc(sd_rdy, 1)
                dve.wait_ge(sd_rdy, 2 * s + 2)
                rstd(c, st[u])
                dve.wait_ge(bc_rdy, s + 1)
                V.tensor_copy(wide[u][:], st[u][:, 2, :].unsqueeze(2).broadcast_to([128, GH, C])).then_inc(rstd_rdy, 1)
                dve.wait_ge(bc_rdy, s + 3)
                ins = V.tensor_tensor(stripe(yb, s), stripe(yb, s), bc_ps[u][:], ALU.mult)
                ins.then_inc(y_rdy, 1)
                dve.wait_ge(y_rdy, s + 1)
                c(V.bn_stats(bn[:, 0, bass.ds(s, 1), :].rearrange("p a n -> p (a n)"), stripe(yb, s)))
                c.end()

            pipelined(dve, centre, norm, NS)

            for k in range(2):
                dve.wait_ge(wT_rdy, k + 1)
                turned = w_bf[:, 0:TAPS * C].rearrange("p (t c) -> p t c", t=TAPS)
                V.tensor_copy(wblk[0:64, k, :, 0:64], turned[0:64])
                V.tensor_copy(wblk[64:128, k, :, 64:128], turned[64:128]).then_inc(wb_rdy, 1)
            dve.wait_ge(rT2, 1)
            V.tensor_copy(rwt[0:64, 0:E], bank[3][0:64, 0:E])
            V.tensor_copy(rwt[64:128, E:2 * E], bank[3][64:128, 0:E]).then_inc(rwt_rdy, 1)

            def batch_norm(l, of):
                one(V.bn_aggr(mv[:, l, :], bn[:, l].rearrange("p s n -> p (s n)")))
                V.tensor_copy(mv2[:, l, 0:1], mv[:, l, 0:1])
                V.scalar_tensor_tensor(mv2[:, l, 1:2], mv[:, l, 0:1], mv[:, l, 0:1], mv[:, l, 1:2],
                                       ALU.mult, ALU.add).then_inc(agg_rdy, 1)
                dve.wait_ge(pr_rdy, l + 1)
                t = bt[:, l, :]
                mean, m2_ = mv[:, l, 0:1], mv[:, l, 1:2]
                one(V.tensor_copy(mv[:, l, :], bank[2][:, 0:2]))
                one(V.tensor_tensor(t[:, 0:1], mean, mean, ALU.mult))
                one(V.tensor_tensor(t[:, 0:1], m2_, t[:, 0:1], ALU.subtract))
                V.tensor_scalar(t[:, 0:1], t[:, 0:1], of * of, 1e-5, ALU.mult, ALU.add).then_inc(bva_rdy, 1)
                dve.wait_ge(bsd_rdy, l + 1)
                one(V.reciprocal(t[:, 2:3], t[:, 1:2]))
                one(V.tensor_tensor(t[:, 3:4], t[:, 0:1], t[:, 2:3], ALU.mult))
                one(V.tensor_tensor(t[:, 3:4], t[:, 3:4], t[:, 2:3], ALU.mult))
                one(V.tensor_scalar(t[:, 3:4], t[:, 3:4], -0.5, 1.5, ALU.mult, ALU.add))
                one(V.tensor_tensor(t[:, 2:3], t[:, 2:3], t[:, 3:4], ALU.mult))
                one(V.tensor_scalar(t[:, 2:3], t[:, 2:3], gb[:, 2 * l:2 * l + 1], LEVELS * of, ALU.mult, ALU.mult))
                V.tensor_copy(aff[:, l, 0:1], t[:, 2:3])
                one(V.tensor_tensor(t[:, 3:4], mean, t[:, 2:3], ALU.mult))
                V.scalar_tensor_tensor(aff[:, l, 1:2], gb[:, 2 * l + 1:2 * l + 2], LEVELS, t[:, 3:4],
                                       ALU.mult, ALU.subtract).then_inc(aff_rdy, 1)

            q_chain = chain("vector_quant")

            def quantise(l, s, u):
                c = q_chain.begin(s + l * NS, 1)
                dve.wait_ge(q_rdy, s + l * NS + 1)
                c(V.tensor_scalar(qt[u][:], qt[u][:], LEVELS, ROUND, ALU.min, ALU.add))
                c.end()
                dve.wait_ge(cv_rdy, s + l * NS + 1)
                V.tensor_scalar(qpad[u][:, :, 1:H + 1, 1:W + 1],
                                qt[u][:].rearrange("p (i a b) -> p i a b", i=IMG, a=H), -ROUND, None,
                                ALU.add).then_inc(qp_rdy, 1)

            b_chain = chain("vector_conv1_stats")

            def stats1(s, u):
                dve.wait_ge(c1_rdy, s + 3)
                c = b_chain.begin(s, 1)
                c(V.bn_stats(bn[:, 1, bass.ds(s, 1), :].rearrange("p a n -> p (a n)"), stripe(cb, s)))
                c.end()

            batch_norm(0, 1.0)
            pipelined(dve, lambda s, u: quantise(0, s, u), stats1, NS)
            batch_norm(1, 1.0 / (LEVELS * LEVELS))

            r_chain = chain("vector_route")

            def route(s, u):
                c = r_chain.begin(s, 27)
                t = st[u]
                wideof = lambda a, n=C: a.unsqueeze(2).broadcast_to([128, GH, n])
                lgs = lg[:, bass.ds(s, 1)].rearrange("p a g e -> p (a g) e")
                m2s = top2[:, bass.ds(s, 1)].rearrange("p a g -> p (a g)")
                dve.wait_ge(cv_rdy, s + NS + 3)
                dve.wait_ge(x_res, NS)
                dve.wait_ge(x1_kept, s + 1)
                dve.wait_ge(lg_rdy, s + 1)
                V.scalar_tensor_tensor(x1[u][:], conv_ps[u][:], 1.0 / (LEVELS * LEVELS), stripe(xb, s),
                                       ALU.mult, ALU.add).then_inc(x1_rdy, 1)
                dve.wait_ge(rT_rdy, s + 1)
                c(V.tensor_reduce(t[:, 4], rT_ps.rearrange("p (g c) -> p g c", c=C), AX.X, ALU.add))
                c(V.tensor_scalar(t[:, 4], t[:, 4], 1.0 / C, None, ALU.mult))
                V.tensor_tensor(cen[:], rT_ps.rearrange("p (g c) -> p g c", c=C), wideof(t[:, 4]),
                                ALU.subtract).then_inc(rc_rdy, 1)
                dve.wait_ge(rs_rdy, s + 1)
                c(V.tensor_reduce(t[:, 0], sq[u][:].rearrange("p (g c) -> p g c", c=C), AX.X, ALU.add))
                V.tensor_scalar(t[:, 0], t[:, 0], 1.0 / C, 1e-5, ALU.mult, ALU.add).then_inc(rsd_rdy, 1)
                dve.wait_ge(rsd_rdy, 2 * s + 2)
                rstd(c, t)
                if not isinstance(s, int) or s >= 2:
                    dve.wait_ge(scat[u], (s - u) * 128)
                V.tensor_tensor(rows[u][:, 0, :, 0:C], cen[:], wideof(t[:, 2]), ALU.mult).then_inc(row_rdy, 1)
                V.tensor_copy(rows[u][:].bitcast(I32)[:, :, :, C], dest_f[:])
                dve.wait_ge(lg_rdy, s + 3)
                c(V.tensor_tensor(ra[:], lg_ps.rearrange("p (g e) -> p g e", e=E), wideof(t[:, 2], E), ALU.mult))
                c(V.tensor_scalar(dest_f[:], dest_f[:], float(2 * S), None, ALU.add))
                c(V.tensor_reduce(m1[:], ra[:], AX.X, ALU.max))
                c(V.tensor_tensor(lgs, ra[:], wideof(m1[:], E), ALU.subtract))
                c(V.scalar_tensor_tensor(rb[:], lgs, 0.0, first_pref[:], ALU.is_equal, ALU.mult))
                c(V.tensor_reduce(mm[:], rb[:], AX.X, ALU.max))
                c(V.tensor_tensor(oh[0][:], rb[:], wideof(mm[:], E), ALU.is_equal))
                c(V.scalar_tensor_tensor(ra[:], oh[0][:], NOT_CHOSEN, lgs, ALU.mult, ALU.add))
                c(V.tensor_reduce(m2[:], ra[:], AX.X, ALU.max))
                V.tensor_copy(m2s, m2[:])
                c(V.tensor_tensor(rb[:], ra[:], wideof(m2[:], E), ALU.is_equal))
                c(V.tensor_tensor(rb[:], rb[:], first_pref[:], ALU.mult))
                c(V.tensor_reduce(mm[:], rb[:], AX.X, ALU.max))
                c(V.tensor_tensor(oh[1][:], rb[:], wideof(mm[:], E), ALU.is_equal))
                V.tensor_tensor(chosen[:, 0:GH, :], oh[0][:], oh[1][:], ALU.add).then_inc(ch_rdy, 1)
                dve.wait_ge(pos_rdy, s + 1)
                c(V.tensor_tensor(pos[:], pos_ps.rearrange("p (g e) -> p g e", e=E),
                                  base[:].unsqueeze(1).broadcast_to([128, GH + 1, E]), ALU.add))
                c(V.tensor_copy(base[:], pos[:, GH, :]))
                for k in range(2):
                    c(V.tensor_tensor(ra[:], oh[k][:], pos[:, 0:GH, :], ALU.mult))
                    c(V.tensor_reduce(slot_f[:, k], ra[:], AX.X, ALU.add))
                V.tensor_copy(slot[u][:], slot_f[:]).then_inc(slot_rdy, 1)
                dve.wait_ge(slot_rdy, s + 1)
                if u == 1:
                    e = (s - 1) // 2
                    dve.wait_ge(w_in, 80 * e + 80)
                    V.tensor_copy(wsp[:, 0:2 * HT, 0, :].bitcast(F32R), wr[:].rearrange("p k t c -> p (k t) c"))
                    V.tensor_copy(wsp[:, 2 * HT, 0, :].bitcast(F32R), wt[:]).then_inc(ws_rdy, 1)
                    dve.wait_ge(ws_rdy, 2 * e + 1)
                    V.tensor_tensor(wsp[:, 0:2 * HT, 1, :], wr[:].rearrange("p k t c -> p (k t) c"),
                                    wsp[:, 0:2 * HT, 0, :], ALU.subtract)
                    V.tensor_tensor(wsp[:, 2 * HT, 1, :], wt[:], wsp[:, 2 * HT, 0, :], ALU.subtract
                                    ).then_inc(ws_rdy, 1)
                c.end()

            pipelined(dve, lambda s, u: quantise(1, s, u), route, NS)
            V.memset(mm[:], 0.0).then_inc(ex_go, 1)

            f, fl, r, F, P, a, b_, d, i1, i2 = (tm[:, k, :] for k in range(10))
            count = tm[:, 10, :]
            one(V.tensor_tensor(count, base[:], region[:], ALU.subtract))
            for n in range(T // 128):
                V.tensor_tensor(padf[:, n, :], pad_off[:, n, :], base[:], ALU.add)
            one(V.tensor_scalar(f, count, -(T / 2 - 0.5), 1.0 / T, ALU.add, ALU.mult))
            V.tensor_copy(padi[:], padf[:]).then_inc(padi_rdy, 1)
            one(V.tensor_scalar(f, f, ROUND, None, ALU.add))
            one(V.tensor_scalar(f, f, -ROUND, None, ALU.add))
            one(V.tensor_scalar(fl, f, float(T), None, ALU.mult))
            one(V.tensor_tensor(r, count, fl, ALU.is_gt))
            of_all = lambda v: v.unsqueeze(1).broadcast_to([128, E, E])
            one(V.tensor_tensor(ra[:], earlier[:], of_all(f), ALU.mult))
            one(V.tensor_reduce(F, ra[:], AX.X, ALU.add))
            one(V.tensor_reduce(tcol[:, 2:3], f, AX.X, ALU.add))
            one(V.tensor_tensor(ra[:], earlier[:], of_all(r), ALU.mult))
            one(V.tensor_reduce(P, ra[:], AX.X, ALU.add))
            one(V.tensor_scalar(P, P, tcol[:, 2:3], None, ALU.add))
            one(V.tensor_scalar(a, F, -1.0, tile_no[:, 0:1], ALU.mult, ALU.add))
            one(V.tensor_tensor(b_, a, f, ALU.is_lt))
            one(V.scalar_tensor_tensor(i1, a, 0.0, b_, ALU.is_ge, ALU.mult))
            one(V.scalar_tensor_tensor(a, a, float(T), region[:], ALU.mult, ALU.add))
            one(V.tensor_tensor(a, a, i1, ALU.mult))
            one(V.scalar_tensor_tensor(i2, P, tile_no[:, 0:1], r, ALU.is_equal, ALU.mult))
            one(V.tensor_tensor(d, fl, region[:], ALU.add))
            one(V.tensor_tensor(d, d, i2, ALU.mult))
            one(V.tensor_tensor(a, a, d, ALU.add))
            one(V.tensor_reduce(tcol[:, 0:1], a, AX.X, ALU.add))
            one(V.tensor_tensor(i1, i1, i2, ALU.add))
            one(V.tensor_reduce(tcol[:, 3:4], i1, AX.X, ALU.add))
            one(V.tensor_tensor(i1, i1, expert_no[:], ALU.mult))
            one(V.tensor_reduce(tcol[:, 1:2], i1, AX.X, ALU.add))
            one(V.tensor_scalar(tcol[:, 1:2], tcol[:, 1:2], 128.0, None, ALU.mult))
            one(V.tensor_scalar(tcol[:, 3:4], tcol[:, 3:4], -float(DUMMY), float(DUMMY), ALU.mult, ALU.add))
            V.tensor_tensor(tcol[:, 0:1], tcol[:, 0:1], tcol[:, 3:4], ALU.add).then_inc(map_rdy, 1)
            dve.wait_ge(mapT_rdy, 1)
            V.tensor_copy(tmap[:].rearrange("p a n -> p (a n)"), bank[5][0:1, 0:256]).then_inc(tmap_rdy, 1)

            g0, g1 = gate[:, 0], gate[:, 1]
            dve.wait_ge(ex_rdy, 2)
            one(V.tensor_reduce(gsum[:], lg[:], AX.X, ALU.add))
            one(V.reciprocal(g0, gsum[:]))
            one(V.tensor_tensor(g1, top2[:], g0, ALU.mult))
            one(V.scalar_tensor_tensor(gsum[:], g0, 1e-9, g1, ALU.add, ALU.add))
            one(V.reciprocal(gsum[:], gsum[:]))
            for k in range(2):
                one(V.tensor_tensor(gate[:, k], gate[:, k], gsum[:], ALU.mult))

            d_chain = chain("vector_split")

            def split(j, u):
                c = d_chain.begin(j, 1)
                dve.wait_ge(xr_in[u], (j - u) * 8 + 16)
                if not isinstance(j, int) or j >= 2:
                    dve.wait_ge(xt_rdy, 2 * j - 2)
                V.tensor_copy(dest_all[:, bass.ds(j, 1), :].rearrange("p a g -> p (a g)"),
                              xrow[u].bitcast(I32)[:, :, C])
                xr = xrow[u][:, :, 0:C]
                c(V.tensor_copy(hl[u][:, :, 0, :].bitcast(F32R), xr))
                V.tensor_copy(hl[u][:, :, 2, :].bitcast(F32R), xr)
                V.tensor_tensor(hl[u][:, :, 1, :], xr, hl[u][:, :, 0, :], ALU.subtract).then_inc(split_rdy, 1)
                c.end()

            def hidden(j, k):
                n = KT * j + k
                m = 128 if k < HT else HR
                dve.wait_ge(silu_rdy, n + 1)
                if k < HT:
                    dve.wait_ge(h3_rdy, HT * j + k + 1)
                    h3 = h3_ps[k % 2][:]
                else:
                    h3 = h1_ps[k % 2][TAIL3:TAIL3 + HR, :]
                dve.wait_ge(w2_rdy, n + 1)
                V.tensor_tensor(hbuf[k % 2][0:m, :], sbuf[k % 2][0:m, :], h3, ALU.mult).then_inc(mul_rdy, 1)

            def rows_out(j, u):
                dve.wait_ge(ro_rdy, j + 3)
                if not isinstance(j, int) or j >= 2:
                    dve.wait_ge(y_out[u], (j - u) * 32)
                V.tensor_copy(destc[u][:], dest_all[:, bass.ds(j, 1), :].rearrange("p a g -> p (a g)"))
                V.tensor_copy(yrow[u].rearrange("p g c -> p (g c)"), ro_ps[:, 0:4 * C]).then_inc(yr_sb, 1)

            def tile(j, u, first=False, last=False):
                hidden(j, 0)
                if not last:
                    split(j + 1, 1 - u)
                hidden(j, 1)
                if not first:
                    rows_out(j - 1, 1 - u)
                for k in range(2, KT):
                    hidden(j, k)

            split(0, 0)
            tiles(dve, tile)
            rows_out(NT - 1, 1)

            def gate1(s, u):
                dve.wait_ge(yk_in[u], (s - u) * 16 + 32)
                v = yk[0][u].rearrange("p (g c) -> p g c", g=GH)
                V.tensor_tensor(v, v, gate_of(0, s), ALU.mult).then_inc(g1_rdy, 1)

            def add(s, u):
                dve.wait_ge(fin_rdy, s + 3)
                V.tensor_tensor(stripe(xb, s), stripe(xb, s), fin_ps[u][:], ALU.add).then_inc(o_rdy, 1)

            pipelined(dve, gate1, add, NS)

        @block.tensor
        def _(pe):
            mm = nc.tensor.matmul
            for s_ in (var_rdy, bc_rdy, cv_rdy, lg_rdy, w2_rdy, ro_rdy, fin_rdy):
                pe.sem_inc(s_, 2)
            pe.wait_ge(const_p, 1)
            pe.wait_ge(const_v, 1)

            def mean(s, u):
                pe.wait_ge(x_in[u], (s - u) * 16 + 32)
                pe.wait_ge(cen_rdy, s + 1)
                mm(mean_ps[u][:], same_half[:], stripe(xb, s), start=True, stop=True).then_inc(mean_rdy, 1)

            def var(s, u):
                pe.wait_ge(sq_rdy, s + 1)
                for g in range(G):
                    ins = mm(var_ps[u][:, 2 * g:2 * g + 2], sq[u][:, 128 * g:128 * g + 128], half_col[:],
                             start=True, stop=True)
                ins.then_inc(var_rdy, 1)
                pe.wait_ge(rstd_rdy, s + 1)
                for g in range(G):
                    ins = mm(bc_ps[u][:, 128 * g:128 * g + 128],
                             wide[u][:].rearrange("p g c -> p (g c)")[:, 128 * g:128 * g + 128], ident[:],
                             start=True, stop=True)
                ins.then_inc(bc_rdy, 1)

            pipelined(pe, mean, var, NS)

            pe.wait_ge(wd_rdy, 1)
            for k in range(2):
                if k:
                    pe.wait_ge(wb_rdy, k)
                for t in range(TAPS):
                    ins = nc.tensor.transpose(w_bf[:, C * t:C * t + C],
                                              wdup[:, k, t, :, :].rearrange("o d i -> o (d i)"), ident_bf[0:C, 0:C])
                ins.then_inc(wT_rdy, 1)
            pe.wait_ge(rr_rdy, 1)
            nc.tensor.transpose(bank[3][:, 0:E], rwc[:].rearrange("e d c -> e (d c)"), ident[0:E, 0:E]).then_inc(rT2, 1)
            pe.wait_ge(wb_rdy, 2)

            def pair_up(l):
                pe.wait_ge(agg_rdy, l + 1)
                mm(bank[2][:, 0:2], pair[:], mv2[:, l, :], start=True, stop=True).then_inc(pr_rdy, 1)

            def conv(l, s, u):
                pe.wait_ge(qp_rdy, s + l * NS + 3)
                if l == 0:
                    pe.wait_ge(c1_rdy, s + 1)
                else:
                    pe.wait_ge(x1_rdy, s + 1)
                for t in range(TAPS):
                    ky, kx = divmod(t, 3)
                    ins = mm(conv_ps[u][:], wblk[:, l, t, :], qpad[u][:, :, ky:ky + H, kx:kx + W],
                             start=t == 0, stop=t == TAPS - 1)
                ins.then_inc(cv_rdy, 1)

            pair_up(0)
            pipelined(pe, lambda s, u: conv(0, s, u), lambda s, u: None, NS)
            pair_up(1)
            pe.wait_ge(rwt_rdy, 1)

            def route(s, u):
                pe.wait_ge(x1_rdy, s + 3)
                pe.wait_ge(rc_rdy, s + 1)
                for g in range(G):
                    ins = nc.tensor.transpose(rT_ps[:, 128 * g:128 * g + 128], x1[u][:, 128 * g:128 * g + 128],
                                              ident[:])
                ins.then_inc(rT_rdy, 1)
                pe.wait_ge(ch_rdy, s + 1)
                for g in range(G):
                    ins = mm(lg_ps[:, 16 * g:16 * g + 16], x1[u][:, 128 * g:128 * g + 128], rwt[:],
                             start=True, stop=True)
                ins.then_inc(lg_rdy, 1)
                pe.wait_ge(ch_rdy, s + 2)
                mm(pos_ps, before[:], chosen[:].rearrange("p g e -> p (g e)"), start=True, stop=False)
                for g in range(GH):
                    n = GH - g
                    ins = mm(pos_ps[:, E * (g + 1):E * (GH + 1)].rearrange("p (g e) -> p g e", e=E), ones_bf[:],
                             chosen[:, g, :].unsqueeze(1).broadcast_to([128, n, E]), start=False, stop=g == GH - 1)
                ins.then_inc(pos_rdy, 1)
                if u == 1:
                    e = (s - 1) // 2
                    pe.wait_ge(ws_rdy, 2 * e + 2)
                    for b in range(3):
                        if b == 2:
                            pe.wait_ge(wt_sb, 4 * e + 1)
                        for t in range(4 * b, min(4 * b + 4, 2 * HT + 1)):
                            ins = nc.tensor.transpose(w_bank(b)[:, 128 * (t % 4):128 * (t % 4) + 128],
                                                      wsp[:, t, :, :].rearrange("p d c -> p (d c)"), ident[:])
                        ins.then_inc(wt_ps, 1)
                    wait_apart(pe, wt_sb, 4 * e + 2)
                    w2v = wr2[:, 0:HT * 128].rearrange("c (p t) -> c t p", t=HT)
                    for t in range(HT):
                        nc.tensor.transpose(w_bank(3)[:, C * t:C * t + C], w2v[:, t, :], ident[0:C, 0:C])
                    nc.tensor.transpose(w_bank(3)[0:HR, C * HT:C * KT], wr2[:, HT * 128:HID],
                                        ident[0:C, 0:C]).then_inc(wt_ps, 1)

            pipelined(pe, lambda s, u: conv(1, s, u), route, NS)
            pe.wait_ge(map_rdy, 1)
            for k in range(2):
                ins = mm(bank[5][0:1, 128 * k:128 * k + 128], tcol[:, k:k + 1], ident[:], start=True, stop=True)
            ins.then_inc(mapT_rdy, 1)

            def turn(j, u, p):
                if p == 0:
                    pe.wait_ge(split_rdy, j + 3)
                pe.wait_ge(xt_sb, 2 * j + p + 1)
                for g in range(4):
                    ins = nc.tensor.transpose(xt_ps[:, 128 * g:128 * g + 128],
                                              hl[u][:, g, p:p + 2, :].rearrange("p d c -> p (d c)"), ident[:])
                ins.then_inc(xt_rdy, 1)

            def up(j, u, k):
                n = KT * j + k
                if k == 0:
                    pe.wait_ge(wt_in[u], (j - u) * 16 + 32)
                    pe.wait_ge(xt_sb, 2 * j + 3)
                pe.wait_ge(mul_rdy, n + 1)
                if k < HT:
                    for ps, c, rdy in ((h1_ps, k, h1_rdy), (h3_ps, HT + k, h3_rdy)):
                        for p in range(2):
                            ins = mm(ps[k % 2][:], wbuf[u][:, 128 * c:128 * c + 128], xT[p][u][:],
                                     start=p == 0, stop=p == 1)
                        ins.then_inc(rdy, 1)
                else:
                    for p in range(2):
                        ins = mm(h1_ps[k % 2][:], wbuf[u][:, 256 * HT:256 * HT + 128], xT[p][u][:],
                                 start=p == 0, stop=p == 1)
                    ins.then_inc(h1_rdy, 1)

            def down(j, u, k):
                n = KT * j + k
                m = 128 if k < HT else HR
                if k == 0:
                    pe.wait_ge(y_sb, j + 1)
                wait_apart(pe, mul_rdy, n + 3)
                h = 64 * (k % 2)
                ins = mm(y_ps[u][h:h + 64, :], w2buf[u][0:m, k, :], hbuf[k % 2][0:m, :],
                         start=k < 2, stop=k >= KT - 2)
                ins.then_inc(w2_rdy, 1)

            def rows_out(j, u):
                pe.wait_ge(y_sb, j + 3)
                pe.wait_ge(yr_sb, j + 1)
                for g in range(4):
                    ins = mm(ro_ps[:, C * g:C * g + C], ysb[u][:, 128 * g:128 * g + 128], fold[:],
                             start=True, stop=True)
                ins.then_inc(ro_rdy, 1)

            def tile(j, u, first=False, last=False):
                up(j, u, 1)
                down(j, u, 0)
                if not first:
                    rows_out(j - 1, 1 - u)
                up(j, u, 2)
                down(j, u, 1)
                if not last:
                    turn(j + 1, 1 - u, 0)
                up(j, u, 3)
                down(j, u, 2)
                if not last:
                    turn(j + 1, 1 - u, 1)
                up(j, u, 4)
                down(j, u, 3)
                up(j, u, 5)
                down(j, u, 4)
                if not last:
                    up(j + 1, 1 - u, 0)
                down(j, u, 5)

            turn(0, 0, 0)
            turn(0, 0, 1)
            up(0, 0, 0)
            tiles(pe, tile)
            rows_out(NT - 1, 1)

            def total(s, u):
                pe.wait_ge(g1_rdy, s + 1)
                pe.wait_ge(g2_rdy, s + 1)
                pe.wait_ge(o_rdy, s + 1)
                for g in range(G):
                    for k in range(2):
                        ins = mm(fin_ps[u][:, 128 * g:128 * g + 128], yk[k][u][:, 128 * g:128 * g + 128], ident[:],
                                 start=k == 0, stop=k == 1)
                ins.then_inc(fin_rdy, 1)

            pipelined(pe, total, lambda s, u: None, NS)


_INS = ['x', 'L0_conv_gamma1', 'L0_conv_beta1', 'L0_conv_w1', 'L0_conv_gamma2', 'L0_conv_beta2', 'L0_conv_w2',
        'L0_conv_pat', 'L0_ffn_router_w', 'L0_ffn_w1', 'L0_ffn_w2', 'L0_ffn_w3']


def kernel(**inputs):
    import numpy as np
    import concourse.bacc as bacc
    from concourse import mybir as mb
    from concourse.bass_utils import run_bass_kernel_spmd

    nc = bacc.Bacc("TRN2", target_bir_lowering=False, num_devices=1)
    arrays, args = {}, []
    for name in _INS:
        a = np.ascontiguousarray(inputs[name])
        arrays[f"in_{name}"] = a
        args.append(nc.dram_tensor(f"in_{name}", a.shape, mb.dt.from_np(a.dtype), kind="ExternalInput").ap())
    shape = inputs['x'].shape
    args.append(nc.dram_tensor("out_0", shape, mb.dt.from_np(np.dtype("float32")), kind="ExternalOutput").ap())
    conv_moe_kernel(nc, *args)
    r = run_bass_kernel_spmd(nc, [arrays], core_ids=[0])
    return r.results[0]["out_0"]
```

```python
from contextlib import ExitStack

import concourse.bass as bass
from concourse import mybir

ALU = mybir.AluOpType
ACT = mybir.ActivationFunctionType
AX = mybir.AxisListType
F32 = mybir.dt.float32
F32R = mybir.dt.float32r
BF16 = mybir.dt.bfloat16
I32 = mybir.dt.int32
RED_MAX = bass.bass_isa.ReduceOp.max

ROUND = 1.5 * 2.0 ** 23
LEVELS = 15.0
NOT_CHOSEN = -1e30


def conv_moe_kernel(nc, x, gamma1, beta1, w1, gamma2, beta2, w2, pat, router_w, ew1, ew2, ew3, out):
    N, C, H, W = x.shape
    E, HID, _ = ew1.shape
    HW = H * W
    HALF = N // 2
    S = 512
    IMG = S // HW
    NS = HALF * HW // S
    G = S // 128
    GH = 2 * G
    NP = NS // 2
    GP = 2 * GH
    TOK = N * HW
    TAPS = 9
    ROW = C + 2
    T = 512
    REG = TOK + T
    DUMMY = E * REG
    NT = 2 * TOK // T + E
    SNAPS = (6, 10, 12, NS)
    FULL = [(2 * TOK * n // NS - E * (T - 1)) // T // 2 * 2 for n in SNAPS]
    AHEAD = SNAPS[0] + 1
    NPAD = E * (T // 128)
    HT = HID // 128
    HR = HID - HT * 128
    KT = HT + 1
    WST = (2 * HT + 1) * 128
    LV = len(SNAPS) + 1
    TAIL3 = 64
    assert NS == 16 and C == 64 and E == 8 and KT == 6 and HR <= 64 and NT % 2 == 0 and NPAD % 2 == 0

    xv = x.rearrange("(h p i) c a b -> h p c i (a b)", h=2, i=2 * IMG)
    outv = out.rearrange("(h p i) c a b -> h p c i (a b)", h=2, i=2 * IMG)
    xs = nc.dram_tensor("expert_rows", [E * REG + T, ROW], F32).ap()
    yout = nc.dram_tensor("result_rows", [2 * TOK, C], F32).ap()
    wsc = nc.dram_tensor("expert_w13", [E * 128, WST], F32).ap()
    w2sc = nc.dram_tensor("expert_w2", [E * 128, KT * C], F32).ap()

    with ExitStack() as ctx:
        def sb(name, shape, dt=F32):
            return ctx.enter_context(nc.sbuf_tensor(name, shape, dt))

        def sem(name):
            return ctx.enter_context(nc.semaphore(name))

        bank = [ctx.enter_context(nc.psum_tensor(f"bank{i}", [128, 512], F32)) for i in range(8)]

        ident = sb("ident", [128, 128])
        same_half = sb("same_half", [128, 128])
        pair = sb("pair", [128, 128])
        half_col = sb("half_col", [128, 2])
        fold = sb("fold", [128, C])
        before = sb("before", [128, 128], BF16)
        ident_bf = sb("ident_bf", [128, 128], BF16)
        ones_bf = sb("ones_bf", [128, 128], BF16)
        centre = sb("centre_half", [128, 128])
        first_pref = sb("first_pref", [128, GP, E])
        expert_no = sb("expert_no", [128, LV, E])
        region = sb("region", [128, LV, E])
        tile_no = sb("tile_no", [128, 1])
        pad_off = sb("pad_off", [128, T // 128, E])
        token0 = sb("token0", [128, GP])
        pad_rows = sb("pad_rows", [128, 4, ROW])
        eps6 = sb("eps6", [128, 1])
        eps5 = sb("eps5", [128, 1])

        xb = sb("x_all", [128, NS * S])
        yb = sb("y_and_rows", [128, NS * GH * ROW])
        rows_all = yb[:, :].rearrange("p (s g r) -> p s g r", s=NS, g=GH)
        cb = sb("conv1_all", [128, NS * S])
        gb = sb("gamma_beta", [128, 4])
        bn = sb("bn_stats", [128, 2, NS, 6])
        mv = sb("bn_mean_var", [128, 2, 2])
        mv2 = sb("bn_moments", [128, 2, 2])
        bt = sb("bn_tmp", [128, 2, 4])
        aff = sb("bn_affine", [128, 2, 2])
        wc = sb("conv_w", [C, 2, C * TAPS])
        wmax = sb("conv_w_max", [C, 2])
        wmax_all = sb("conv_w_max_all", [C, 2])
        wrec = sb("conv_w_rec", [C, 2])
        patf = sb("pat_f", [C, TAPS])
        pati = sb("pat_i", [C, TAPS], I32)
        wdup = sb("conv_w_dup", [C, 2, TAPS, 2, C], BF16)
        wblk = sb("conv_w_blocks", [128, 2, TAPS, 128], BF16)
        qt = [sb(f"quant_tmp{u}", [128, S]) for u in range(2)]
        qpad = [sb(f"quant_padded{u}", [128, IMG, H + 2, W + 2], BF16) for u in range(2)]
        sq = sb("squares", [128, 2, S])
        wide = sb("rstd_wide", [128, GP, C])
        st = sb("stats", [128, 4, GP])

        x1 = [sb(f"x1_{u}", [128, S]) for u in range(2)]
        rows = [sb(f"rows_now{u}", [128, GH * ROW]) for u in range(2)]
        slot_f = sb("slot_f", [128, 2, GP])
        slot_all = sb("slot_all", [128, NS, 2 * GH], I32)
        slot = [sb(f"slot_now{u}", [128, 2 * GH], I32) for u in range(2)]
        token = sb("token_no", [128, GP])
        rw = sb("router_rows", [E, C])
        rwm = sb("router_mean", [E, 1])
        rwc = sb("router_centred", [E, 2, C])
        rwt = sb("router_T", [128, 2 * E])
        lg = sb("logits", [128, NS, GH, E])
        top2 = sb("second_minus_first", [128, NS, GH])
        ra = sb("route_a", [128, GP, E])
        rb = sb("route_b", [128, GP, E])
        rk = sb("route_slots", [128, 2, GP, E])
        m1 = sb("route_max", [128, GP])
        mm = sb("route_pref", [128, GP])
        oh = sb("one_hot", [128, 2, GP, E])
        chosen = sb("chosen", [128, GP + 1, E], BF16)
        pos = sb("positions", [128, GP + 1, E])
        base = sb("base", [128, E])
        bases = sb("base_by_pair", [128, NP, E])
        counts = sb("base_by_level", [128, LV, E])
        gate = sb("gates", [128, 2, NS, GH])
        gsum = sb("gate_sum", [128, NS, GH])
        tm = sb("tile_map_work", [128, 8, LV, E])
        run = sb("tile_map_sums", [128, 2, 2 * LV * E])
        tcol = sb("tile_map_col", [128, 4])
        twide = sb("tile_map_wide", [128, 128])
        expert_of = sb("tile_expert", [128, 128])
        tmap = sb("tile_map", [1, 2, 128], I32)
        padf = sb("pad_slot_f", [128, T // 128, E])
        padi = sb("pad_slot", [128, T // 128, E], I32)
        pads = [sb(f"pad_now{u}", [128, 1], I32) for u in range(2)]

        wr = sb("w13_rows", [128, 2, HT, C])
        wt = sb("w13_tail", [128, C])
        wr2 = sb("w2_rows", [C, HID])
        wsp = sb("w13_split", [128, 2 * HT + 1, 2, C])
        wstk = sb("w13_stacked", [128, WST])
        w2s = sb("w2_stacked", [128, KT, C])

        wbuf = [sb(f"w13_{u}", [128, WST], F32R) for u in range(2)]
        w2buf = [sb(f"w2_{u}", [128, KT, C]) for u in range(2)]
        free = [0]

        def carve(*shape):
            n = 1
            for d in shape:
                n *= d
            v = cb[:, free[0]:free[0] + n]
            free[0] += n
            assert free[0] <= NS * S
            if len(shape) == 1:
                return v
            names = "abc"[:len(shape)]
            return v.rearrange(f"p ({' '.join(names)}) -> p {' '.join(names)}",
                               **{names[i]: shape[i] for i in range(1, len(shape))})

        xrow = [carve(4, ROW) for u in range(2)]
        hl = [carve(4, 2, C) for u in range(2)]
        sbuf = [carve(T) for u in range(3)]
        hbuf = [carve(T) for u in range(4)]
        second = [carve(4) for u in range(2)]
        ysb = [carve(T) for u in range(2)]
        yrow = [carve(4, C) for u in range(2)]
        dest_all = sb("dest_all", [128, NT, 4], I32)
        destc = [sb(f"dest_now{u}", [128, 4], I32) for u in range(2)]
        xT = [[sb(f"xT_{p}_{u}", [128, T], F32R) for u in range(2)] for p in ("hi_lo", "lo_hi")]
        RING = 4
        yk = [[yb[:, (RING * k + v) * GP * C:(RING * k + v + 1) * GP * C] for v in range(RING)] for k in range(2)]

        x_in = [sem(f"x_in{u}") for u in range(2)]
        small_in = sem("small_in")
        gb_in = sem("gamma_beta_in")
        const_p = sem("const_pool")
        const_v = sem("const_vector")
        zero_p = sem("zeroed_pool")
        p_step = sem("pool_step")
        v_step = sem("vector_step")
        cen_rdy = sem("centred_ready")
        sq_rdy = sem("squares_ready")
        var_rdy = sem("var_ready")
        sd_rdy = sem("sd_ready")
        rstd_rdy = sem("rstd_ready")
        bc_rdy = sem("rstd_spread_ready")
        y_rdy = sem("y_ready")
        x_res = sem("x_plus_y_done")
        staged = sem("rows_staged")
        th_rdy = sem("tanh_ready")
        wm_rdy = sem("wmax_ready")
        wma_rdy = sem("wmax_all_ready")
        wrec_rdy = sem("wmax_reciprocal_ready")
        wd_rdy = sem("conv_w_dup_ready")
        wT_rdy = sem("conv_w_turned")
        wb_rdy = sem("conv_w_blocks_ready")
        agg_rdy = sem("moments_ready")
        pr_rdy = sem("moments_paired")
        bsd_rdy = sem("bn_sd_ready")
        bva_rdy = sem("bn_var_ready")
        aff_rdy = sem("affine_ready")
        y_cen = sem("centred_copied")
        q_rdy = sem("quant_affine_ready")
        qp_rdy = sem("quant_padded_ready")
        cv_rdy = sem("conv_ready")
        c1_rdy = sem("conv1_copied")
        x1_rdy = sem("x1_ready")
        x1_kept = sem("x1_kept")
        rT_rdy = sem("rows_turned")
        lg_rdy = sem("logits_ready")
        rn_rdy = sem("rows_normed")
        rs_rdy = sem("row_squares_ready")
        rsd_rdy = sem("row_sd_ready")
        ch_rdy = sem("chosen_ready")
        pos_rdy = sem("positions_ready")
        slot_rdy = sem("slots_ready")
        scat = [sem(f"row_scatter{u}") for u in range(2)]
        rr_rdy = sem("router_rows_centred")
        rT2 = sem("router_turned")
        rwt_rdy = sem("router_T_ready")
        w_in = sem("w13_in")
        w2_in = sem("w2_in")
        w_zero = sem("w_zeroed")
        ws_rdy = sem("w_split_ready")
        wt_ps = sem("w_turned")
        wt_sb = sem("w_stacked")
        w_out = sem("w_out")
        ex_rdy = sem("exp_ready")
        ex_go = sem("exp_go")
        dummy_out = sem("dummy_out")
        map_rdy = sem("map_cols_ready")
        mapT_rdy = sem("map_turned")
        tmap_rdy = sem("tile_map_ready")
        padi_rdy = sem("pad_slots_ready")
        pad_cp = sem("pad_slot_copied")
        pad_out = [sem(f"pad_out{u}") for u in range(2)]
        xr_in = [sem(f"tile_rows_in{u}") for u in range(2)]
        wt_in = [sem(f"tile_w_in{u}") for u in range(2)]
        split_rdy = sem("split_ready")
        xt_rdy = sem("xT_ready")
        xt_sb = sem("xT_copied")
        h1_rdy = sem("h1_ready")
        h3_rdy = sem("h3_ready")
        silu_rdy = sem("silu_ready")
        mul_rdy = sem("hidden_ready")
        w2_rdy = sem("w2_done")
        y_sb = sem("y_copied")
        ro_rdy = sem("rows_out_ready")
        yr_sb = sem("y_rows_ready")
        y_out = [sem(f"y_scatter{u}") for u in range(2)]
        yk_in = [sem(f"results_in{v}") for v in range(RING)]
        g0_rdy = sem("gated_first_ready")
        g2_rdy = sem("gated_second_ready")
        g1_rdy = sem("gated_sum_ready")
        fin_rdy = sem("sum_turned")
        o_rdy = sem("out_ready")
        o_out = sem("out_stored")
        passed = sem("passed")

        def wait_apart(eng, sem_, value):
            eng.wait_ge(sem_, value)
            eng.sem_inc(passed, 1)

        def stripe(t, s):
            return t[:, bass.ds(s * S, S)]

        def pipelined(eng, front, back, n):
            front(0, 0)
            front(1, 1)
            back(0, 0)
            front(2, 0)
            back(1, 1)
            with eng.Fori(1, n // 2 - 1) as turn:
                i = 2 * turn
                front(i + 1, 1)
                back(i, 0)
                front(i + 2, 0)
                back(i + 1, 1)
            front(n - 1, 1)
            back(n - 2, 0)
            back(n - 1, 1)

        def pairs(eng, step):
            step(0, first=True)
            with eng.Fori(1, NP - 2) as p:
                step(p)
            step(NP - 2, last=2)
            step(NP - 1, last=1)

        def tiles(eng, tile):
            tile(0, 0, first=True)
            tile(1, 1)
            tile(2, 0)
            tile(3, 1)
            with eng.Fori(2, NT // 2 - 1) as pair_:
                j = 2 * pair_
                tile(j, 0)
                tile(j + 1, 1)
            tile(NT - 2, 0, last=2)
            tile(NT - 1, 1, last=1)

        conv_ps = [bank[0], bank[1]]
        w_bf = bank[6][:, :].bitcast(BF16)

        h1_ps, h3_ps, y_ps = bank[0:3], bank[3:6], bank[6]
        turn_ps = bank[7]

        def w_bank(b):
            return bank[6 + b % 2]

        cen_ps, bc_ps, var_ps = [bank[0:2], bank[2:4]], bank[4:6], bank[6:8]
        rT_ps, lg_ps, pos_ps = bank[2:4], bank[4][:, 0:GP * E], bank[5][:, 0:(GP + 1) * E]
        fin_ps = [bank[0:2], bank[2:4]]

        def gate_of(k, p):
            return gate[:, k, bass.ds(2 * p, 2), :].rearrange("p a g -> p (a g)").unsqueeze(2).broadcast_to([128, GP, C])

        NSMALL = 2 + 1 + 1
        block = ctx.enter_context(nc.Block())

        @block.sync
        def _(sp):
            for p in range(NP):
                if p >= 2:
                    sp.wait_ge(x_in[p % 2], 32 * (p // 2))
                for h in range(2):
                    sp.dma_start(xb[64 * h:64 * h + 64, 2 * S * p:2 * S * (p + 1)]
                                 .rearrange("c (i p) -> c i p", i=2 * IMG), xv[h, p]).then_inc(x_in[p % 2], 16)
                if p == 1:
                    for k, w in enumerate((w1, w2)):
                        sp.dma_start(wc[:, k, :], w.rearrange("o i a b -> o (i a b)")).then_inc(small_in, 16)
                    sp.dma_start(pati[:], pat.rearrange("a b -> (a b)").partition_broadcast(C)).then_inc(small_in, 16)
                    sp.dma_start(rw[:], router_w).then_inc(small_in, 16)
            for k, v in enumerate((gamma1, beta1, gamma2, beta2)):
                for h in range(2):
                    sp.dma_start(gb[64 * h:64 * h + 64, k:k + 1],
                                 v.rearrange("(c a) -> c a", a=1)).then_inc(gb_in, 16)
            sp.wait_ge(const_v, 1)
            sp.dma_start(xs[DUMMY:DUMMY + T, :].rearrange("(p g) c -> p g c", g=4),
                         pad_rows[:]).then_inc(dummy_out, 16)
            sp.wait_ge(w_zero, 1)
            def weights_in(e):
                for k, w in enumerate((ew1, ew3)):
                    we = w.rearrange("e h c -> e (h c)")
                    sp.dma_start(wr[:, k, :, :].rearrange("p t c -> p (t c)"),
                                 we[bass.ds(e, 1), 0:HT * 128 * C].rearrange("a (p n) -> (a p) n", p=128)
                                 ).then_inc(w_in, 16)
                    sp.dma_start(wt[TAIL3 * k:TAIL3 * k + HR, :],
                                 we[bass.ds(e, 1), HT * 128 * C:HID * C].rearrange("a (p n) -> (a p) n", p=HR)
                                 ).then_inc(w_in, 16)

            def weights2_in(e):
                sp.dma_start(wr2[:], ew2[bass.ds(e, 1), :, :].rearrange("a c h -> (a c) h")).then_inc(w2_in, 16)

            def weights_out(e):
                sp.dma_start(wsc[bass.ds(e * 128, 128), :], wstk[:]).then_inc(w_out, 16)
                sp.dma_start(w2sc[bass.ds(e * 128, 128), :], w2s[:].rearrange("p k c -> p (k c)")).then_inc(w_out, 16)

            weights_in(0)
            weights2_in(0)
            with sp.Fori(0, E - 1) as e:
                sp.wait_ge(ws_rdy, 2 * e + 2)
                weights_in(e + 1)
                sp.wait_ge(wt_sb, 4 * e + 4)
                weights2_in(e + 1)
                weights_out(e)
            sp.wait_ge(wt_sb, 4 * E)
            weights_out(E - 1)

            sp.wait_ge(dummy_out, 16)
            sp.wait_ge(tmap_rdy, 1)
            sp.wait_ge(w_out, 32 * E)

            def scattered(stripes):
                for u in range(2):
                    sp.wait_ge(scat[u], 16 * 2 * GH * (stripes // 2))

            def load_rows(j, u):
                src = sp.value_load(tmap[0:1, 0, bass.ds(j, 1)], min_val=0, max_val=E * REG)
                sp.wait_ge(split_rdy, j + 1)
                sp.dma_start(xrow[u], xs[bass.ds(src, T), :].rearrange("(p g) c -> p g c", g=4)
                             ).then_inc(xr_in[u], 16)

            def load_weights(j, u, first=False):
                exp = sp.value_load(tmap[0:1, 1, bass.ds(j, 1)], min_val=0, max_val=(E - 1) * 128)
                if not first:
                    sp.wait_ge(h1_rdy, KT * j - KT)
                sp.dma_start(wbuf[u][:].bitcast(F32), wsc[bass.ds(exp, 128), :]).then_inc(wt_in[u], 16)
                if not first:
                    sp.wait_ge(w2_rdy, KT // 2 * j - KT // 2 + 2)
                sp.dma_start(w2buf[u][:].rearrange("p k c -> p (k c)"), w2sc[bass.ds(exp, 128), :]
                             ).then_inc(wt_in[u], 16)

            scattered(SNAPS[0])
            for u in range(2):
                load_rows(u, u)
                load_weights(u, u, first=True)
            for u in range(2):
                load_rows(2 + u, u)
            for level in range(LV):
                if 0 < level < LV - 1:
                    scattered(SNAPS[level])
                if level == LV - 1:
                    for u in range(2):
                        sp.wait_ge(pad_out[u], 16 * NPAD // 2)
                with sp.Fori(FULL[level - 1] // 2 - 1 if level else 1,
                             FULL[level] // 2 - 1 if level < LV - 1 else NT // 2 - 1) as pair_:
                    j = 2 * pair_
                    for u in range(2):
                        load_weights(j + u, u)
                        load_rows(j + u + 2, u)
            for u in range(2):
                load_weights(NT - 2 + u, u)

            for u in range(2):
                sp.wait_ge(y_out[u], 64 * (NT // 2))

            def results(p, v):
                sp.wait_ge(fin_rdy, 2 * p + 2)
                for k in range(2):
                    sp.dma_start(yk[k][v].rearrange("q (i n) -> q i n", i=2),
                                 yout[bass.ds(p * 4 * S + k * TOK, 4 * S), :]
                                 .rearrange("(i q g) c -> q i (g c)", i=2, g=GH)).then_inc(yk_in[v], 16)

            with sp.Fori(0, NP // RING) as turn:
                for v in range(RING):
                    results(RING * turn + v, v)
            sp.wait_ge(o_out, 32 * NP)

        @block.gpsimd
        def _(pool):
            def made(ins, n=[0]):
                n[0] += 1
                ins.then_inc(p_step, 1)
                pool.wait_ge(p_step, n[0])

            made(nc.gpsimd.memset(ident[:], 0.0))
            made(nc.gpsimd.affine_select(out=ident[:], in_=ident[:], compare_op=ALU.not_equal, fill=1.0,
                                         base=0, pattern=[[-1, 128]], channel_multiplier=1))
            made(nc.gpsimd.tensor_copy(ident_bf[:], ident[:]))
            made(nc.gpsimd.memset(before[:], 1.0))
            made(nc.gpsimd.affine_select(out=before[:], in_=before[:], compare_op=ALU.is_gt, fill=0.0,
                                         base=0, pattern=[[1, 128]], channel_multiplier=-1))
            iota = lambda t, pattern, base, cm: made(nc.gpsimd.iota(t, pattern=pattern, base=base,
                   channel_multiplier=cm, allow_small_or_imprecise_dtypes=True))
            iota(first_pref[:], [[0, GP], [-1, E]], E, 0)
            iota(expert_no[:], [[0, LV], [1, E]], 0, 0)
            iota(region[:], [[0, LV], [1, E]], 0, 0)
            iota(tile_no[:], [[0, 1]], 0, 1)
            iota(pad_off[:], [[128, T // 128], [0, E]], 0, 1)
            iota(token0[:], [[2 * S, 2], [1, GH]], 0, GH)
            made(nc.gpsimd.memset(ones_bf[:], 1.0))
            pool.sem_inc(const_p, 1)
            for t in (chosen, rwt, wblk, *qpad):
                ins = nc.gpsimd.memset(t[:], 0.0)
            ins.then_inc(zero_p, 1)

            pool.wait_ge(wm_rdy, 1)
            made(nc.gpsimd.partition_all_reduce(wmax_all[:], wmax[:], C, RED_MAX))
            P = nc.gpsimd
            made(P.tensor_copy(patf[:], pati[:]))
            made(P.tensor_scalar(wrec[:], wmax_all[:], 2.0, None, ALU.mult))
            pool.sem_inc(wma_rdy, 1)
            pool.wait_ge(wrec_rdy, 1)
            for k in range(2):
                made(P.tensor_scalar(wc[:, k, :], wc[:, k, :], wrec[:, k:k + 1], 0.5, ALU.mult, ALU.add))
            made(P.tensor_scalar(wc[:], wc[:], LEVELS, ROUND, ALU.mult, ALU.add))
            made(P.tensor_scalar(wc[:], wc[:], -ROUND, 2.0, ALU.add, ALU.mult))
            made(P.tensor_scalar(wc[:], wc[:], -LEVELS, None, ALU.add))
            for k in range(2):
                for d in range(2):
                    ins = P.tensor_tensor(wdup[:, k, :, d, :], wc[:, k, :].rearrange("o (i t) -> o t i", t=TAPS),
                                          patf[:].unsqueeze(2).broadcast_to([C, TAPS, C]), ALU.mult)
            ins.then_inc(wd_rdy, 1)

            with pool.Fori(0, NS) as s:
                pool.wait_ge(y_rdy, s + 2)
                nc.gpsimd.tensor_tensor(stripe(xb, s), stripe(xb, s), stripe(yb, s), ALU.add).then_inc(x_res, 1)

            def stage(s, u):
                wait_apart(pool, slot_rdy, s + 1)
                if not isinstance(s, int) or s >= 2:
                    wait_apart(pool, scat[u], (s - u) * 128)
                nc.gpsimd.tensor_copy(rows[u][:], rows_all[:, bass.ds(s, 1)].rearrange("p a g r -> p (a g r)"))
                nc.gpsimd.tensor_copy(slot[u][:], slot_all[:, bass.ds(s, 1)].rearrange("p a k -> p (a k)")
                                      ).then_inc(staged, 1)
                wait_apart(pool, staged, s + 1)

            def scatter(u, k):
                for g in range(GH):
                    nc.gpsimd.indirect_dma_start(
                        xs, bass.IndirectOffsetOnAxis(ap=slot[u][:, k * GH + g:k * GH + g + 1], axis=0),
                        rows[u][:, g * ROW:g * ROW + ROW], None).then_inc(scat[u], 16)

            def scatter_stripe(s, u):
                stage(s, u)
                scatter(u, 0)
                scatter(u, 1)

            scatter_stripe(0, 0)
            scatter_stripe(1, 1)
            with pool.Fori(1, AHEAD // 2) as pair_:
                i = 2 * pair_
                scatter_stripe(i, 0)
                scatter_stripe(i + 1, 1)
            scatter_stripe(AHEAD - 1, 0)

            def scatter_y(j, u):
                wait_apart(pool, yr_sb, j + 3)
                for g in range(4):
                    nc.gpsimd.indirect_dma_start(
                        yout, bass.IndirectOffsetOnAxis(ap=destc[u][:, g:g + 1], axis=0),
                        yrow[u][:, g, :], None, bounds_check=2 * TOK - 1, oob_is_err=False
                    ).then_inc(y_out[u], 16)

            def scatter_pad(n, u):
                if not isinstance(n, int) or n >= 2:
                    pool.wait_ge(pad_out[u], (n - u) * 8)
                nc.gpsimd.tensor_copy(pads[u][:], padi_flat[:, bass.ds(n, 1)]).then_inc(pad_cp, 1)
                wait_apart(pool, pad_cp, n + 1)
                nc.gpsimd.indirect_dma_start(
                    xs, bass.IndirectOffsetOnAxis(ap=pads[u][:], axis=0),
                    pad_rows[:, 0, :], None).then_inc(pad_out[u], 16)

            def four_tiles(j, s, u):
                stage(s, u)
                scatter(u, 0)
                scatter_y(j, 0)
                scatter_y(j + 1, 1)
                scatter(u, 1)
                scatter_y(j + 2, 0)
                scatter_y(j + 3, 1)

            late = NS - AHEAD
            four_tiles(0, AHEAD, 1)
            with pool.Fori(1, late // 2 + 1) as turn:
                four_tiles(8 * turn - 4, AHEAD - 1 + 2 * turn, 0)
                four_tiles(8 * turn, AHEAD + 2 * turn, 1)

            padi_flat = padi[:].rearrange("p i e -> p (i e)")
            pool.wait_ge(padi_rdy, 1)
            J0, J1 = 4 * late, 4 * late + NPAD // 2
            assert J1 < FULL[-1] - 2
            def pads_and_tiles(n, j):
                for v in range(2):
                    scatter_pad(n + 2 * v, 0)
                    scatter_pad(n + 2 * v + 1, 1)
                    scatter_y(j + v, v)

            pads_and_tiles(0, J0)
            with pool.Fori(1, NPAD // 4) as turn:
                pads_and_tiles(4 * turn, J0 + 2 * turn)
            with pool.Fori(J1 // 2, NT // 2) as pair_:
                j = 2 * pair_
                for u in range(2):
                    scatter_y(j + u, u)

            def gate2(p, v):
                pool.wait_ge(yk_in[v], (p - v) * (32 // RING) + 32)
                y = yk[1][v].rearrange("p (g c) -> p g c", g=GP)
                nc.gpsimd.tensor_tensor(y, y, gate_of(1, p), ALU.mult).then_inc(g2_rdy, 1)

            with pool.Fori(0, NP // RING) as turn:
                for v in range(RING):
                    gate2(RING * turn + v, v)

        @block.scalar
        def _(act):
            act.sem_inc(c1_rdy, 2)
            act.sem_inc(x1_kept, 2)
            act.sem_inc(y_sb, 1)
            act.wait_ge(small_in, 16 * NSMALL)
            nc.scalar.activation(wc[:], wc[:], ACT.Tanh).then_inc(th_rdy, 1)

            def square(p, v):
                for u in range(2):
                    s = 2 * p + u
                    act.wait_ge(cen_rdy, s + 1)
                    if u == 0:
                        act.wait_ge(var_rdy, p + 1)
                    nc.scalar.activation(sq[:, u, :], cen_ps[v][u][:], ACT.Square).then_inc(sq_rdy, 1)
                    nc.scalar.activation(stripe(yb, s), cen_ps[v][u][:], ACT.Copy).then_inc(y_cen, 1)

            def sd(p, v):
                act.wait_ge(sd_rdy, 2 * p + 1)
                nc.scalar.activation(st[:, 1, :], st[:, 0, :], ACT.Sqrt).then_inc(sd_rdy, 1)

            pipelined(act, square, sd, NP)

            def affine(l, s, u):
                act.wait_ge(qp_rdy, s + l * NS + 1)
                nc.scalar.activation(qt[u][:], stripe(cb if l else yb, s), ACT.Relu,
                                     bias=aff[:, l, 1:2], scale=aff[:, l, 0:1]).then_inc(q_rdy, 1)

            def keep_conv1(s, u):
                act.wait_ge(cv_rdy, s + 3)
                nc.scalar.activation(stripe(cb, s), conv_ps[u][:], ACT.Copy).then_inc(c1_rdy, 1)

            act.wait_ge(bva_rdy, 1)
            nc.scalar.activation(bt[:, 0, 1:2], bt[:, 0, 0:1], ACT.Sqrt).then_inc(bsd_rdy, 1)
            act.wait_ge(aff_rdy, 1)
            pipelined(act, lambda s, u: affine(0, s, u), keep_conv1, NS)
            act.wait_ge(bva_rdy, 2)
            nc.scalar.activation(bt[:, 1, 1:2], bt[:, 1, 0:1], ACT.Sqrt).then_inc(bsd_rdy, 1)
            act.wait_ge(aff_rdy, 2)

            def squares(p):
                for u in range(2):
                    s = 2 * p + u
                    act.wait_ge(x1_rdy, s + 3)
                    nc.scalar.activation(stripe(xb, s), x1[u][:], ACT.Copy).then_inc(x1_kept, 1)
                for u in range(2):
                    act.wait_ge(rT_rdy, 2 * p + u + 1)
                    nc.scalar.activation(sq[:, u, :], rT_ps[u][:], ACT.Square).then_inc(rs_rdy, 1)

            def route(p, first=False, last=0):
                act.wait_ge(rsd_rdy, 2 * p + 1)
                nc.scalar.activation(st[:, 1, :], st[:, 0, :], ACT.Sqrt).then_inc(rsd_rdy, 1)
                if not last:
                    for u in range(2):
                        affine(1, 2 * p + 4 + u, u)
                if not first:
                    wait_apart(act, w_out, 32 * p)
                for b in range(3):
                    n = min(512, WST - 512 * b)
                    act.wait_ge(wt_ps, 4 * p + b + 1)
                    nc.scalar.activation(wstk[:, 512 * b:512 * b + n].bitcast(F32R), w_bank(b)[:, 0:n],
                                         ACT.Copy).then_inc(wt_sb, 1)
                act.wait_ge(wt_ps, 4 * p + 4)
                nc.scalar.activation(w2s[:, 0:HT, :].rearrange("p k c -> p (k c)"), w_bank(3)[:, 0:HT * C],
                                     ACT.Copy)
                nc.scalar.activation(w2s[0:HR, HT, :], w_bank(3)[0:HR, HT * C:KT * C],
                                     ACT.Copy).then_inc(wt_sb, 1)
                if last != 1:
                    squares(p + 1)

            for s in range(4):
                affine(1, s, s % 2)
            squares(0)
            pairs(act, route)

            act.wait_ge(ex_go, 1)
            nc.scalar.activation(lg[:], lg[:], ACT.Exp).then_inc(ex_rdy, 1)
            nc.scalar.activation(top2[:], top2[:], ACT.Exp).then_inc(ex_rdy, 1)

            def silu(j, k):
                m = 128 if k < HT else HR
                act.wait_ge(h1_rdy, KT * j + k + 1)
                nc.scalar.activation(sbuf[k % 3][0:m, :], h1_ps[k % 3][0:m, :], ACT.Silu).then_inc(silu_rdy, 1)

            def copy_xT(j, u, part):
                if part == 0:
                    act.wait_ge(xt_rdy, j + 1)
                    nc.scalar.activation(xT[0][u][:], turn_ps[:], ACT.Copy)
                    nc.scalar.activation(xT[1][u][0:C, :], turn_ps[C:2 * C, :], ACT.Copy)
                else:
                    nc.scalar.activation(xT[1][u][C:2 * C, :], turn_ps[0:C, :], ACT.Copy).then_inc(xt_sb, 1)

            def copy_y(j, u):
                act.wait_ge(w2_rdy, KT // 2 * j + KT // 2 + 2)
                act.wait_ge(ro_rdy, j + 1)
                nc.scalar.activation(ysb[u], y_ps[:], ACT.Copy).then_inc(y_sb, 1)

            def tile(j, u, first=False, last=0):
                if not first:
                    copy_y(j - 1, 1 - u)
                if last != 1:
                    copy_xT(j + 1, 1 - u, 0)
                silu(j, 2)
                if last != 1:
                    copy_xT(j + 1, 1 - u, 1)
                for k in range(3, KT):
                    silu(j, k)
                if last != 1:
                    silu(j + 1, 0)
                    silu(j + 1, 1)

            copy_xT(0, 0, 0)
            copy_xT(0, 0, 1)
            silu(0, 0)
            silu(0, 1)
            tiles(act, tile)
            copy_y(NT - 1, 1)

            def store(p):
                act.wait_ge(o_rdy, 2 * p + 6)
                for h in range(2):
                    act.dma_start(outv[h, bass.ds(p, 1)].rearrange("a c i p -> (a c) i p"),
                                  xb[64 * h:64 * h + 64, bass.ds(2 * S * p, 2 * S)]
                                  .rearrange("c (i p) -> c i p", i=2 * IMG)).then_inc(o_out, 16)

            with act.Fori(0, NP) as p:
                store(p)

        @block.vector
        def _(dve):
            class Chain:
                base = 0

                def begin(self, n=0, per=0):
                    self.at, self.k, self.per = n, 0, per
                    return self

                def __call__(self, ins):
                    self.k += 1
                    ins.then_inc(self.sem, 1)
                    dve.wait_ge(self.sem, self.base + self.at * self.per + self.k)

                def end(self):
                    assert self.k == self.per, self.k

            def chain(name):
                c = Chain()
                c.sem = sem(name)
                return c

            V = nc.vector
            one = chain("vector_straight").begin()
            dve.sem_inc(o_rdy, 4)
            for s_ in (qp_rdy, x1_rdy, split_rdy, yr_sb):
                dve.sem_inc(s_, 2)
            dve.sem_inc(mul_rdy, 3)
            for s_ in (rn_rdy, ch_rdy, y_rdy):
                dve.sem_inc(s_, 1)

            V.memset(wt[:], 0.0)
            V.memset(w2s[:], 0.0).then_inc(w_zero, 1)
            V.memset(run[:], 0.0)
            one(V.memset(pad_rows[:], 0.0))
            one(V.memset(pad_rows[:, :, C:C + 1], float(1 << 20)))
            one(V.memset(same_half[:], 0.0))
            V.memset(same_half[0:64, 0:64], 1.0 / C)
            one(V.memset(same_half[64:128, 64:128], 1.0 / C))
            one(V.memset(half_col[:], 0.0))
            V.memset(half_col[0:64, 0:1], 1.0 / C)
            V.memset(half_col[64:128, 1:2], 1.0 / C)
            dve.wait_ge(const_p, 1)
            one(V.tensor_tensor(centre[:], ident[:], same_half[:], ALU.subtract))
            one(V.tensor_tensor(fold[:], ident[:, 0:C], ident[:, C:2 * C], ALU.add))
            for h in range(2):
                one(V.tensor_scalar(pair[:, C * h:C * h + C], fold[:], 0.5, None, ALU.mult))
            one(V.tensor_scalar(region[:], region[:], float(REG), None, ALU.mult))
            one(V.tensor_copy(base[:], region[:, 0, :]))
            V.tensor_copy(token[:], token0[:]).then_inc(const_v, 1)

            dve.wait_ge(th_rdy, 1)
            V.tensor_reduce(wmax[:], wc[:], AX.X, ALU.max, apply_absolute_value=True).then_inc(wm_rdy, 1)
            one(V.tensor_reduce(rwm[:], rw[:], AX.X, ALU.add))
            one(V.tensor_scalar(rwm[:], rwm[:], -1.0 / C, None, ALU.mult))
            V.tensor_scalar(rwc[:, 0, :], rw[:], rwm[:, 0:1], None, ALU.add)
            V.tensor_scalar(rwc[:, 1, :], rw[:], rwm[:, 0:1], None, ALU.add).then_inc(rr_rdy, 1)

            def rstd(c):
                var, sd_, r, w = (st[:, k] for k in range(4))
                c(V.reciprocal(r, sd_))
                c(V.tensor_tensor(w, var, r, ALU.mult))
                c(V.tensor_tensor(w, w, r, ALU.mult))
                c(V.tensor_scalar(w, w, -0.5, 1.5, ALU.mult, ALU.add))
                c(V.tensor_tensor(r, r, w, ALU.mult))

            ln = chain("vector_layernorm")

            def spread(p, v):
                c = ln.begin(p, 5)
                dve.wait_ge(var_rdy, p + 2)
                V.tensor_scalar(st[:, 0, :], var_ps[v][:, 0:GP], 1e-6, None, ALU.add).then_inc(sd_rdy, 1)
                dve.wait_ge(sd_rdy, 2 * p + 2)
                rstd(c)
                dve.wait_ge(bc_rdy, 2 * p + 2)
                V.tensor_copy(wide[:], st[:, 2, :].unsqueeze(2).broadcast_to([128, GP, C])).then_inc(rstd_rdy, 1)
                c.end()

            def norm(p, v):
                for u in range(2):
                    s = 2 * p + u
                    dve.wait_ge(bc_rdy, s + 3)
                    dve.wait_ge(y_cen, s + 1)
                    V.tensor_tensor(stripe(yb, s), stripe(yb, s), bc_ps[u][:], ALU.mult).then_inc(y_rdy, 1)
                for u in range(2):
                    s = 2 * p + u
                    dve.wait_ge(y_rdy, s + 2)
                    V.bn_stats(bn[:, 0, bass.ds(s, 1), :].rearrange("p a n -> p (a n)"), stripe(yb, s))

            dve.wait_ge(wma_rdy, 1)
            V.reciprocal(wrec[:], wrec[:]).then_inc(wrec_rdy, 1)
            pipelined(dve, spread, norm, NP)

            dve.wait_ge(zero_p, 1)
            for k in range(2):
                dve.wait_ge(wT_rdy, k + 1)
                turned = w_bf[:, 0:TAPS * C].rearrange("p (t c) -> p t c", t=TAPS)
                V.tensor_copy(wblk[0:64, k, :, 0:64], turned[0:64])
                V.tensor_copy(wblk[64:128, k, :, 64:128], turned[64:128]).then_inc(wb_rdy, 1)
            dve.wait_ge(rT2, 1)
            V.tensor_copy(rwt[0:64, 0:E], bank[7][0:64, 0:E])
            V.tensor_copy(rwt[64:128, E:2 * E], bank[7][64:128, 0:E]).then_inc(rwt_rdy, 1)

            def batch_norm(l, of):
                one(V.bn_aggr(mv[:, l, :], bn[:, l].rearrange("p s n -> p (s n)")))
                V.tensor_copy(mv2[:, l, 0:1], mv[:, l, 0:1])
                V.scalar_tensor_tensor(mv2[:, l, 1:2], mv[:, l, 0:1], mv[:, l, 0:1], mv[:, l, 1:2],
                                       ALU.mult, ALU.add).then_inc(agg_rdy, 1)
                dve.wait_ge(pr_rdy, l + 1)
                t = bt[:, l, :]
                mean, m2_ = mv[:, l, 0:1], mv[:, l, 1:2]
                one(V.tensor_copy(mv[:, l, :], bank[6][:, 0:2]))
                one(V.tensor_tensor(t[:, 0:1], mean, mean, ALU.mult))
                one(V.tensor_tensor(t[:, 0:1], m2_, t[:, 0:1], ALU.subtract))
                V.tensor_scalar(t[:, 0:1], t[:, 0:1], of * of, 1e-5, ALU.mult, ALU.add).then_inc(bva_rdy, 1)
                dve.wait_ge(bsd_rdy, l + 1)
                one(V.reciprocal(t[:, 2:3], t[:, 1:2]))
                one(V.tensor_tensor(t[:, 3:4], t[:, 0:1], t[:, 2:3], ALU.mult))
                one(V.tensor_tensor(t[:, 3:4], t[:, 3:4], t[:, 2:3], ALU.mult))
                one(V.tensor_scalar(t[:, 3:4], t[:, 3:4], -0.5, 1.5, ALU.mult, ALU.add))
                one(V.tensor_tensor(t[:, 2:3], t[:, 2:3], t[:, 3:4], ALU.mult))
                one(V.tensor_scalar(t[:, 2:3], t[:, 2:3], gb[:, 2 * l:2 * l + 1], LEVELS * of, ALU.mult, ALU.mult))
                V.tensor_copy(aff[:, l, 0:1], t[:, 2:3])
                one(V.tensor_tensor(t[:, 3:4], mean, t[:, 2:3], ALU.mult))
                V.scalar_tensor_tensor(aff[:, l, 1:2], gb[:, 2 * l + 1:2 * l + 2], LEVELS, t[:, 3:4],
                                       ALU.mult, ALU.subtract).then_inc(aff_rdy, 1)

            q_chain = chain("vector_quant")

            def quantise(l, s, u):
                c = q_chain.begin(s + l * NS, 1)
                dve.wait_ge(q_rdy, s + l * NS + 1)
                c(V.tensor_scalar(qt[u][:], qt[u][:], LEVELS, ROUND, ALU.min, ALU.add))
                c.end()
                dve.wait_ge(cv_rdy, s + l * NS + 1)
                V.tensor_scalar(qpad[u][:, :, 1:H + 1, 1:W + 1],
                                qt[u][:].rearrange("p (i a b) -> p i a b", i=IMG, a=H), -ROUND, None,
                                ALU.add).then_inc(qp_rdy, 1)

            b_chain = chain("vector_conv1_stats")

            def stats1(s, u):
                dve.wait_ge(c1_rdy, s + 3)
                c = b_chain.begin(s, 1)
                c(V.bn_stats(bn[:, 1, bass.ds(s, 1), :].rearrange("p a n -> p (a n)"), stripe(cb, s)))
                c.end()

            dve.wait_ge(gb_in, 16 * 8)
            batch_norm(0, 1.0)
            pipelined(dve, lambda s, u: quantise(0, s, u),
                      lambda s, u: None if isinstance(s, int) and s == 0 else stats1(s - 1, 1 - u), NS)
            stats1(NS - 1, 1)
            batch_norm(1, 1.0 / (LEVELS * LEVELS))

            r_chain = chain("vector_route")

            def add_conv(p):
                for u in range(2):
                    s = 2 * p + u
                    dve.wait_ge(cv_rdy, s + NS + 3)
                    dve.wait_ge(x_res, NS)
                    dve.wait_ge(x1_kept, s + 1)
                    dve.wait_ge(lg_rdy, p + 1)
                    V.scalar_tensor_tensor(x1[u][:], conv_ps[u][:], 1.0 / (LEVELS * LEVELS), stripe(xb, s),
                                           ALU.mult, ALU.add).then_inc(x1_rdy, 1)

            def of_pair(t, p):
                v = t[:, bass.ds(2 * p, 2)]
                return v.rearrange("p a g e -> p (a g) e") if len(t.shape) == 4 else v.rearrange("p a g -> p (a g)")

            def route(p, first=False, last=0):
                c = r_chain.begin(p, 22)
                wideof = lambda a, n: a.unsqueeze(2).broadcast_to([128, a.shape[1], n])
                dve.wait_ge(rs_rdy, 2 * p + 2)
                c(V.tensor_reduce(st[:, 0], sq[:].rearrange("p u (g c) -> p (u g) c", c=C), AX.X, ALU.add))
                V.tensor_scalar(st[:, 0], st[:, 0], 1.0 / C, 1e-5, ALU.mult, ALU.add).then_inc(rsd_rdy, 1)
                dve.wait_ge(w_in, 64 * p + 64)
                V.tensor_copy(wsp[:, 0:2 * HT, 0, :].bitcast(F32R), wr[:].rearrange("p k t c -> p (k t) c"))
                V.tensor_copy(wsp[:, 2 * HT, 0, :].bitcast(F32R), wt[:]).then_inc(ws_rdy, 1)
                dve.wait_ge(rsd_rdy, 2 * p + 2)
                rstd(c)
                for u in range(2):
                    rows_s = rows_all[:, bass.ds(2 * p + u, 1)].rearrange("p a g r -> p (a g) r")
                    ins = V.tensor_tensor(rows_s[:, :, 0:C], rT_ps[u][:].rearrange("p (g c) -> p g c", c=C),
                                          wideof(st[:, 2, GH * u:GH * u + GH], C), ALU.mult)
                ins.then_inc(rn_rdy, 1)
                rows_p = of_pair(rows_all, p)
                V.tensor_copy(rows_p[:, :, C], token[:])
                dve.wait_ge(ws_rdy, 2 * p + 1)
                V.tensor_tensor(wsp[:, 0:2 * HT, 1, :], wr[:].rearrange("p k t c -> p (k t) c"),
                                wsp[:, 0:2 * HT, 0, :], ALU.subtract)
                V.tensor_tensor(wsp[:, 2 * HT, 1, :], wt[:], wsp[:, 2 * HT, 0, :], ALU.subtract
                                ).then_inc(ws_rdy, 1)
                lgs, m2 = of_pair(lg, p), of_pair(top2, p)
                dve.wait_ge(lg_rdy, p + 2)
                c(V.tensor_tensor(ra[:], lg_ps.rearrange("p (g e) -> p g e", e=E), wideof(st[:, 2], E), ALU.mult))
                V.tensor_scalar(token[:], token[:], float(4 * S), None, ALU.add)
                c(V.tensor_reduce(m1[:], ra[:], AX.X, ALU.max))
                c(V.tensor_tensor(lgs, ra[:], wideof(m1[:], E), ALU.subtract))
                c(V.scalar_tensor_tensor(rb[:], lgs, 0.0, first_pref[:], ALU.is_equal, ALU.mult))
                c(V.tensor_reduce(mm[:], rb[:], AX.X, ALU.max))
                c(V.tensor_tensor(oh[:, 0], rb[:], wideof(mm[:], E), ALU.is_equal))
                V.tensor_copy(rows_p[:, :, C + 1], mm[:])
                c(V.scalar_tensor_tensor(ra[:], oh[:, 0], NOT_CHOSEN, lgs, ALU.mult, ALU.add))
                c(V.tensor_reduce(m2, ra[:], AX.X, ALU.max))
                c(V.tensor_tensor(rb[:], ra[:], wideof(m2, E), ALU.is_equal))
                c(V.tensor_tensor(rb[:], rb[:], first_pref[:], ALU.mult))
                c(V.tensor_reduce(mm[:], rb[:], AX.X, ALU.max))
                c(V.tensor_tensor(oh[:, 1], rb[:], wideof(mm[:], E), ALU.is_equal))
                V.tensor_tensor(chosen[:, 0:GP, :], oh[:, 0], oh[:, 1], ALU.add).then_inc(ch_rdy, 1)
                if last != 1:
                    add_conv(p + 1)
                dve.wait_ge(pos_rdy, p + 1)
                c(V.tensor_tensor(pos[:], pos_ps.rearrange("p (g e) -> p g e", e=E),
                                  base[:].unsqueeze(1).broadcast_to([128, GP + 1, E]), ALU.add))
                V.tensor_copy(base[:], pos[:, GP, :])
                V.tensor_copy(bases[:, bass.ds(p, 1)].rearrange("p a e -> p (a e)"), pos[:, GP, :])
                c(V.tensor_tensor(rk[:], oh[:], pos[:, 0:GP, :].unsqueeze(1).broadcast_to([128, 2, GP, E]), ALU.mult))
                c(V.tensor_reduce(slot_f[:], rk[:], AX.X, ALU.add))
                c(V.tensor_copy(slot_all[:, bass.ds(2 * p, 2)].rearrange("p i (k g) -> p k i g", k=2),
                                slot_f[:].rearrange("p k (i g) -> p k i g", i=2)))
                dve.sem_inc(slot_rdy, 2)
                c.end()
                if not last:
                    for u in range(2):
                        quantise(1, 2 * p + 4 + u, u)

            for u in range(2):
                quantise(1, u, u)
            add_conv(0)
            for u in range(2):
                quantise(1, 2 + u, u)
            pairs(dve, route)
            V.memset(mm[:], 0.0).then_inc(ex_go, 1)
            for level, n in enumerate((*SNAPS, NS)):
                one(V.tensor_copy(counts[:, level, :], bases[:, n // 2 - 1, :]))

            tiles_of, begin, cnt, a, in_, tmp = (tm[:, k] for k in range(6))
            flat = lambda v: v.rearrange("p l e -> p (l e)")
            cum = tm[:, 6]
            for n in range(T // 128):
                V.tensor_tensor(padf[:, n, :], pad_off[:, n, :], base[:], ALU.add)
            one(V.tensor_tensor(cnt, counts[:], region[:], ALU.subtract))
            V.tensor_copy(padi[:], padf[:]).then_inc(padi_rdy, 1)
            one(V.tensor_scalar(tmp, cnt, -(T / 2 - 0.5), 1.0 / T, ALU.add, ALU.mult))
            one(V.tensor_scalar(cum, tmp, ROUND, -ROUND, ALU.add, ALU.add))
            one(V.scalar_tensor_tensor(tmp[:, LV - 1, :], cum[:, LV - 1, :], float(T), cnt[:, LV - 1, :],
                                       ALU.mult, ALU.is_lt))
            one(V.tensor_tensor(cum[:, LV - 1, :], cum[:, LV - 1, :], tmp[:, LV - 1, :], ALU.add))
            V.memset(begin[:, 0, :], 0.0)
            one(V.tensor_copy(begin[:, 1:LV, :], cum[:, 0:LV - 1, :]))
            one(V.tensor_tensor(tiles_of, cum, begin, ALU.subtract))
            Z = M = LV * E
            one(V.tensor_copy(run[:, 0, Z:Z + M], flat(tiles_of)))
            step, at = 1, 0
            while step < M:
                one(V.tensor_tensor(run[:, 1 - at, Z:Z + M], run[:, at, Z:Z + M], run[:, at, Z - step:Z - step + M],
                                    ALU.add))
                step, at = 2 * step, 1 - at
            one(V.tensor_tensor(flat(tmp), flat(tiles_of), run[:, at, Z:Z + M], ALU.subtract))
            one(V.tensor_scalar(a, tmp, tile_no[:, 0:1], None, ALU.add))
            one(V.tensor_tensor(in_, a, tiles_of, ALU.is_lt))
            one(V.scalar_tensor_tensor(in_, a, 0.0, in_, ALU.is_ge, ALU.mult))
            one(V.tensor_tensor(a, a, begin, ALU.add))
            one(V.scalar_tensor_tensor(a, a, float(T), region[:], ALU.mult, ALU.add))
            one(V.tensor_tensor(a, a, in_, ALU.mult))
            one(V.tensor_reduce(tcol[:, 0:1], flat(a), AX.X, ALU.add))
            one(V.tensor_reduce(tcol[:, 3:4], flat(in_), AX.X, ALU.add))
            one(V.tensor_tensor(in_, in_, expert_no[:], ALU.mult))
            one(V.tensor_reduce(tcol[:, 1:2], flat(in_), AX.X, ALU.add))
            one(V.tensor_scalar(tcol[:, 3:4], tcol[:, 3:4], -float(DUMMY), float(DUMMY), ALU.mult, ALU.add))
            V.tensor_copy(twide[:], tcol[:, 1:2].broadcast_to([128, 128]))
            V.tensor_tensor(tcol[:, 0:1], tcol[:, 0:1], tcol[:, 3:4], ALU.add).then_inc(map_rdy, 1)
            dve.wait_ge(mapT_rdy, 1)
            V.tensor_scalar(expert_of[:], bank[5][:, 128:256], -1.0, float(E), ALU.mult, ALU.add)
            V.tensor_copy(tmap[:, 0, :], bank[5][0:1, 0:128])
            V.tensor_scalar(tmap[:, 1, :], bank[5][0:1, 128:256], 128.0, None, ALU.mult).then_inc(tmap_rdy, 1)

            g0, g1 = gate[:, 0], gate[:, 1]
            dve.wait_ge(ex_rdy, 2)
            one(V.tensor_reduce(gsum[:], lg[:], AX.X, ALU.add))
            one(V.reciprocal(g0, gsum[:]))
            one(V.tensor_tensor(g1, top2[:], g0, ALU.mult))
            one(V.scalar_tensor_tensor(gsum[:], g0, 1e-9, g1, ALU.add, ALU.add))
            one(V.reciprocal(gsum[:], gsum[:]))
            for k in range(2):
                one(V.tensor_tensor(gate[:, k], gate[:, k], gsum[:], ALU.mult))

            d_chain = chain("vector_split")

            def split(j, u):
                c = d_chain.begin(j, 2)
                dve.wait_ge(xr_in[u], (j - u) * 8 + 16)
                if not isinstance(j, int) or j >= 2:
                    dve.wait_ge(xt_rdy, j - 1)
                xr = xrow[u][:, :, 0:C]
                c(V.tensor_scalar(second[u][:], xrow[u][:, :, C + 1], expert_of[:, bass.ds(j, 1)], float(TOK),
                                  ALU.not_equal, ALU.mult))
                V.tensor_tensor(dest_all[:, bass.ds(j, 1), :].rearrange("p a g -> p (a g)"), second[u][:],
                                xrow[u][:, :, C], ALU.add)
                c(V.tensor_copy(hl[u][:, :, 0, :].bitcast(F32R), xr))
                V.tensor_tensor(hl[u][:, :, 1, :], xr, hl[u][:, :, 0, :], ALU.subtract).then_inc(split_rdy, 1)
                c.end()

            def hidden(j, u, k):
                n = KT * j + k
                m = 128 if k < HT else HR
                dve.wait_ge(silu_rdy, n + 1)
                if k < HT:
                    dve.wait_ge(h3_rdy, HT * j + k + 1)
                    h3 = h3_ps[k % 3][:]
                else:
                    h3 = h1_ps[k % 3][TAIL3:TAIL3 + HR, :]
                dve.wait_ge(w2_rdy, KT // 2 * j + k // 2 + 1)
                V.tensor_tensor(hbuf[(2 * u + k) % 4][0:m, :], sbuf[k % 3][0:m, :], h3, ALU.mult).then_inc(mul_rdy, 1)

            def rows_out(j, u):
                dve.wait_ge(ro_rdy, j + 3)
                if not isinstance(j, int) or j >= 2:
                    dve.wait_ge(y_out[u], (j - u) * 32)
                V.tensor_copy(destc[u][:], dest_all[:, bass.ds(j, 1), :].rearrange("p a g -> p (a g)"))
                V.tensor_reduce(yrow[u], turn_ps[:].rearrange("p (g h c) -> p g c h", g=4, h=2), AX.X, ALU.add
                                ).then_inc(yr_sb, 1)

            def tile(j, u, first=False, last=0):
                for k in range(2, KT):
                    hidden(j, u, k)
                    if k == 4:
                        if not last:
                            split(j + 2, u)
                        if not first:
                            rows_out(j - 1, 1 - u)
                if last != 1:
                    hidden(j + 1, 1 - u, 0)
                    hidden(j + 1, 1 - u, 1)

            split(0, 0)
            split(1, 1)
            hidden(0, 0, 0)
            hidden(0, 0, 1)
            tiles(dve, tile)
            rows_out(NT - 1, 1)

            def gate1(p, v):
                dve.wait_ge(yk_in[v], (p - v) * (32 // RING) + 32)
                y = yk[0][v].rearrange("p (g c) -> p g c", g=GP)
                V.tensor_tensor(y, y, gate_of(0, p), ALU.mult).then_inc(g0_rdy, 1)

            def add(p, v):
                for u in range(2):
                    s = 2 * p + u
                    dve.wait_ge(fin_rdy, s + 9)
                    V.tensor_tensor(stripe(xb, s), stripe(xb, s), fin_ps[v % 2][u][:], ALU.add).then_inc(o_rdy, 1)

            def both(p, v):
                dve.wait_ge(g2_rdy, p + 1)
                dve.wait_ge(g0_rdy, p + 1)
                V.tensor_tensor(yk[0][v], yk[0][v], yk[1][v], ALU.add).then_inc(g1_rdy, 1)

            with dve.Fori(0, NP // RING) as turn:
                for v in range(RING):
                    gate1(RING * turn + v, v)
                    both(RING * turn + v, v)
                    if v:
                        add(RING * turn + v - 1, v - 1)
                add(RING * turn + RING - 1, RING - 1)

        @block.tensor
        def _(pe):
            mm = nc.tensor.matmul
            pe.sem_inc(fin_rdy, 8)
            for s_ in (bc_rdy, cv_rdy, w2_rdy, ro_rdy):
                pe.sem_inc(s_, 2)
            for s_ in (var_rdy, lg_rdy):
                pe.sem_inc(s_, 1)
            pe.wait_ge(const_p, 1)
            pe.wait_ge(const_v, 1)

            def centred(p, v):
                for u in range(2):
                    s = 2 * p + u
                    pe.wait_ge(x_in[v], (p - v) * 16 + 32)
                    if not isinstance(p, int) or p >= 2:
                        pe.wait_ge(y_cen, s - 3)
                    mm(cen_ps[v][u][:], centre[:], stripe(xb, s), start=True, stop=True).then_inc(cen_rdy, 1)

            def var(p, v):
                pe.wait_ge(sq_rdy, 2 * p + 2)
                for g in range(2 * G):
                    ins = mm(var_ps[v][:, 2 * g:2 * g + 2],
                             sq[:].rearrange("p u n -> p (u n)")[:, 128 * g:128 * g + 128], half_col[:],
                             start=True, stop=True)
                ins.then_inc(var_rdy, 1)

            def spread(p):
                pe.wait_ge(rstd_rdy, p + 1)
                for u in range(2):
                    if not isinstance(p, int) or p >= 1:
                        pe.wait_ge(y_rdy, 2 * p + u)
                    for g in range(G):
                        ins = mm(bc_ps[u][:, 128 * g:128 * g + 128],
                                 wide[:].rearrange("p g c -> p (g c)")[:, S * u + 128 * g:S * u + 128 * g + 128],
                                 ident[:], start=True, stop=True)
                    ins.then_inc(bc_rdy, 1)

            def step(p, v):
                if not isinstance(p, int) or p < NP - 2:
                    centred(p + 2, v)
                if not isinstance(p, int) or p < NP - 1:
                    var(p + 1, 1 - v)
                spread(p)

            centred(0, 0)
            centred(1, 1)
            var(0, 0)
            step(0, 0)
            with pe.Fori(1, NP // 2 - 1) as turn_:
                step(2 * turn_ - 1, 1)
                step(2 * turn_, 0)
            step(NP - 3, 1)
            step(NP - 2, 0)
            step(NP - 1, 1)

            pe.wait_ge(wd_rdy, 1)
            for k in range(2):
                if k:
                    pe.wait_ge(wb_rdy, k)
                for t in range(TAPS):
                    ins = nc.tensor.transpose(w_bf[:, C * t:C * t + C],
                                              wdup[:, k, t, :, :].rearrange("o d i -> o (d i)"), ident_bf[0:C, 0:C])
                ins.then_inc(wT_rdy, 1)
            pe.wait_ge(rr_rdy, 1)
            nc.tensor.transpose(bank[7][:, 0:E], rwc[:].rearrange("e d c -> e (d c)"), ident[0:E, 0:E]).then_inc(rT2, 1)
            pe.wait_ge(wb_rdy, 2)

            def pair_up(l):
                pe.wait_ge(agg_rdy, l + 1)
                mm(bank[6][:, 0:2], pair[:], mv2[:, l, :], start=True, stop=True).then_inc(pr_rdy, 1)

            def conv(l, s, u):
                pe.wait_ge(qp_rdy, s + l * NS + 3)
                if l == 0:
                    pe.wait_ge(c1_rdy, s + 1)
                else:
                    pe.wait_ge(x1_rdy, s + 1)
                for t in range(TAPS):
                    ky, kx = divmod(t, 3)
                    ins = mm(conv_ps[u][:], wblk[:, l, t, :], qpad[u][:, :, ky:ky + H, kx:kx + W],
                             start=t == 0, stop=t == TAPS - 1)
                ins.then_inc(cv_rdy, 1)

            pair_up(0)
            pipelined(pe, lambda s, u: conv(0, s, u), lambda s, u: None, NS)
            pair_up(1)
            pe.wait_ge(rwt_rdy, 1)

            def turn_rows(p):
                pe.wait_ge(rn_rdy, p + 1)
                for u in range(2):
                    pe.wait_ge(x1_rdy, 2 * p + u + 3)
                    for g in range(G):
                        ins = mm(rT_ps[u][:, 128 * g:128 * g + 128], x1[u][:, 128 * g:128 * g + 128],
                                 centre[:], start=True, stop=True)
                    ins.then_inc(rT_rdy, 1)
                pe.wait_ge(ch_rdy, p + 1)
                for u in range(2):
                    for g in range(G):
                        ins = mm(lg_ps[:, 16 * (G * u + g):16 * (G * u + g) + 16], x1[u][:, 128 * g:128 * g + 128],
                                 rwt[:], start=True, stop=True)
                ins.then_inc(lg_rdy, 1)

            def conv_pair(p):
                for u in range(2):
                    conv(1, 2 * p + u, u)

            def stack_weights(p):
                pe.wait_ge(ws_rdy, 2 * p + 2)
                for b in range(3):
                    if b == 2:
                        pe.wait_ge(wt_sb, 4 * p + 1)
                    for t in range(4 * b, min(4 * b + 4, 2 * HT + 1)):
                        ins = nc.tensor.transpose(w_bank(b)[:, 128 * (t % 4):128 * (t % 4) + 128],
                                                  wsp[:, t, :, :].rearrange("p d c -> p (d c)"), ident[:])
                    ins.then_inc(wt_ps, 1)
                pe.wait_ge(w2_in, 16 * p + 16)
                wait_apart(pe, wt_sb, 4 * p + 2)
                w2v = wr2[:, 0:HT * 128].rearrange("c (p t) -> c t p", t=HT)
                for t in range(HT):
                    nc.tensor.transpose(w_bank(3)[:, C * t:C * t + C], w2v[:, t, :], ident[0:C, 0:C])
                nc.tensor.transpose(w_bank(3)[0:HR, C * HT:C * KT], wr2[:, HT * 128:HID],
                                    ident[0:C, 0:C]).then_inc(wt_ps, 1)

            def route(p, first=False, last=0):
                stack_weights(p)
                pe.wait_ge(ch_rdy, p + 2)
                mm(pos_ps, before[:], chosen[:].rearrange("p g e -> p (g e)"), start=True, stop=False)
                for g in range(GP):
                    n = GP - g
                    ins = mm(pos_ps[:, E * (g + 1):E * (GP + 1)].rearrange("p (g e) -> p g e", e=E), ones_bf[:],
                             chosen[:, g, :].unsqueeze(1).broadcast_to([128, n, E]), start=False, stop=g == GP - 1)
                ins.then_inc(pos_rdy, 1)
                if last != 1:
                    turn_rows(p + 1)
                if not last:
                    conv_pair(p + 2)

            conv_pair(0)
            turn_rows(0)
            conv_pair(1)
            pairs(pe, route)
            pe.wait_ge(map_rdy, 1)
            mm(bank[5][0:1, 0:128], tcol[:, 0:1], ident[:], start=True, stop=True)
            mm(bank[5][:, 128:256], twide[:], ident[:], start=True, stop=True).then_inc(mapT_rdy, 1)

            def turn(j, u, first=False):
                pe.wait_ge(split_rdy, j + 3)
                if not first:
                    pe.wait_ge(yr_sb, j)
                for g in range(4):
                    ins = nc.tensor.transpose(turn_ps[:, 128 * g:128 * g + 128],
                                              hl[u][:, g, :, :].rearrange("p d c -> p (d c)"), ident[:])
                ins.then_inc(xt_rdy, 1)

            def up(j, u, k):
                n = KT * j + k
                if k == 0:
                    pe.wait_ge(wt_in[u], (j - u) * 16 + 32)
                    pe.wait_ge(xt_sb, j + 1)
                pe.wait_ge(mul_rdy, n + 1)
                if k < HT:
                    for ps, c, rdy in ((h1_ps, k, h1_rdy), (h3_ps, HT + k, h3_rdy)):
                        for p in range(2):
                            ins = mm(ps[k % 3][:], wbuf[u][:, 128 * c:128 * c + 128], xT[p][u][:],
                                     start=p == 0, stop=p == 1)
                        ins.then_inc(rdy, 1)
                else:
                    for p in range(2):
                        ins = mm(h1_ps[k % 3][:], wbuf[u][:, 256 * HT:256 * HT + 128], xT[p][u][:],
                                 start=p == 0, stop=p == 1)
                    ins.then_inc(h1_rdy, 1)

            def down(j, u, k):
                if k == 0:
                    pe.wait_ge(y_sb, j + 1)
                wait_apart(pe, mul_rdy, KT * j + k + 5)
                for i in range(k, k + 2):
                    m = 128 if i < HT else HR
                    h = 64 * (i % 2)
                    ins = mm(y_ps[h:h + 64, :], w2buf[u][0:m, i, :], hbuf[(2 * u + i) % 4][0:m, :],
                             start=i < 2, stop=i >= KT - 2)
                ins.then_inc(w2_rdy, 1)

            def rows_out(j, u, last=False):
                pe.wait_ge(y_sb, j + 2)
                if not last:
                    pe.wait_ge(xt_sb, j + 3)
                else:
                    pe.wait_ge(yr_sb, j + 2)
                for g in range(4):
                    ins = nc.tensor.transpose(turn_ps[:, 128 * g:128 * g + 128], ysb[u][:, 128 * g:128 * g + 128],
                                              ident[:])
                ins.then_inc(ro_rdy, 1)

            def tile(j, u, first=False, last=0):
                if last != 1:
                    turn(j + 1, 1 - u, first)
                up(j, u, 2)
                up(j, u, 3)
                down(j, u, 0)
                up(j, u, 4)
                if not first:
                    rows_out(j - 1, 1 - u, last == 1)
                up(j, u, 5)
                down(j, u, 2)
                if last != 1:
                    up(j + 1, 1 - u, 0)
                    up(j + 1, 1 - u, 1)
                down(j, u, 4)

            turn(0, 0, True)
            up(0, 0, 0)
            up(0, 0, 1)
            tiles(pe, tile)
            rows_out(NT - 1, 1, True)

            def turn_back(p, v):
                pe.wait_ge(g1_rdy, p + 1)
                pe.wait_ge(o_rdy, 2 * p + 2)
                for u in range(2):
                    for g in range(G):
                        ins = nc.tensor.transpose(fin_ps[v % 2][u][:, 128 * g:128 * g + 128],
                                                  yk[0][v][:, S * u + 128 * g:S * u + 128 * g + 128], ident[:])
                    ins.then_inc(fin_rdy, 1)

            with pe.Fori(0, NP // RING) as turn_:
                for v in range(RING):
                    turn_back(RING * turn_ + v, v)


_INS = ['x', 'L0_conv_gamma1', 'L0_conv_beta1', 'L0_conv_w1', 'L0_conv_gamma2', 'L0_conv_beta2', 'L0_conv_w2',
        'L0_conv_pat', 'L0_ffn_router_w', 'L0_ffn_w1', 'L0_ffn_w2', 'L0_ffn_w3']


def kernel(**inputs):
    import numpy as np
    import concourse.bacc as bacc
    from concourse import mybir as mb
    from concourse.bass_utils import run_bass_kernel_spmd

    nc = bacc.Bacc("TRN2", target_bir_lowering=False, num_devices=1)
    arrays, args = {}, []
    for name in _INS:
        a = np.ascontiguousarray(inputs[name])
        arrays[f"in_{name}"] = a
        args.append(nc.dram_tensor(f"in_{name}", a.shape, mb.dt.from_np(a.dtype), kind="ExternalInput").ap())
    shape = inputs['x'].shape
    args.append(nc.dram_tensor("out_0", shape, mb.dt.from_np(np.dtype("float32")), kind="ExternalOutput").ap())
    conv_moe_kernel(nc, *args)
    r = run_bass_kernel_spmd(nc, [arrays], core_ids=[0])
    return r.results[0]["out_0"]
```

```python
from contextlib import ExitStack

import concourse.bass as bass
from concourse import mybir

ALU = mybir.AluOpType
ACT = mybir.ActivationFunctionType
AX = mybir.AxisListType
F32 = mybir.dt.float32
F32R = mybir.dt.float32r
BF16 = mybir.dt.bfloat16
I32 = mybir.dt.int32
RED_MAX = bass.bass_isa.ReduceOp.max

ROUND = 1.5 * 2.0 ** 23
LEVELS = 15.0
NOT_CHOSEN = -1e30


def conv_moe_kernel(nc, x, gamma1, beta1, w1, gamma2, beta2, w2, pat, router_w, ew1, ew2, ew3, out):
    N, C, H, W = x.shape
    E, HID, _ = ew1.shape
    HW = H * W
    HALF = N // 2
    S = 512
    IMG = S // HW
    NS = HALF * HW // S
    G = S // 128
    GH = 2 * G
    NP = NS // 2
    GP = 2 * GH
    TOK = N * HW
    TAPS = 9
    ROW = C + 2
    T = 512
    TH = T // 2
    REG = TOK + T
    DUMMY = E * REG
    SNAPS = (4, 6, 8, 10, 12, 14, NS)
    FULL = [(2 * TOK * n // NS - E * (T - 1)) // T // 2 * 2 for n in SNAPS]
    AHEAD = SNAPS[0] + 2
    NF = FULL[-1]
    NH = ((2 * TOK - NF * T) // TH + E - 1 + 1) // 2 * 2
    NT = NF + NH // 2
    NPAD = E * (TH // 128)
    HT = HID // 128
    HR = HID - HT * 128
    KT = HT + 1
    WST = (2 * HT + 1) * 128
    LV = len(SNAPS)
    TAIL3 = 64
    assert NS == 16 and C == 64 and E == 8 and KT == 6 and HR <= 64 and NT % 2 == 0 and NPAD % 4 == 0

    xv = x.rearrange("(h p i) c a b -> h p c i (a b)", h=2, i=2 * IMG)
    outv = out.rearrange("(h p i) c a b -> h p c i (a b)", h=2, i=2 * IMG)
    xs = nc.dram_tensor("expert_rows", [E * REG + TH, ROW], F32).ap()
    yout = nc.dram_tensor("result_rows", [2 * TOK, C], F32).ap()
    wsc = nc.dram_tensor("expert_w13", [E * 128, WST], F32).ap()
    w2sc = nc.dram_tensor("expert_w2", [E * 128, KT * C], F32).ap()

    with ExitStack() as ctx:
        def sb(name, shape, dt=F32):
            return ctx.enter_context(nc.sbuf_tensor(name, shape, dt))

        def sem(name):
            return ctx.enter_context(nc.semaphore(name))

        bank = [ctx.enter_context(nc.psum_tensor(f"bank{i}", [128, 512], F32)) for i in range(8)]

        ident = sb("ident", [128, 128])
        same_half = sb("same_half", [128, 128])
        pair = sb("pair", [128, 128])
        half_col = sb("half_col", [128, 2])
        fold = sb("fold", [128, C])
        before = sb("before", [128, 128], BF16)
        ident_bf = sb("ident_bf", [128, 128], BF16)
        ones_bf = sb("ones_bf", [128, 128], BF16)
        centre = sb("centre_half", [128, 128])
        first_pref = sb("first_pref", [128, GP, E])
        expert_no = sb("expert_no", [128, LV, E])
        region = sb("region", [128, LV, E])
        tile_no = sb("tile_no", [128, 1])
        pad_off = sb("pad_off", [128, TH // 128, E])
        token0 = sb("token0", [128, GP])
        pad_rows = sb("pad_rows", [128, 2, ROW])
        silu_first = sb("silu_first", [128, 1])

        xb = sb("x_all", [128, NS * S])
        yb = sb("y_and_rows", [128, NS * GH * ROW])
        rows_all = yb[:, :].rearrange("p (s g r) -> p s g r", s=NS, g=GH)
        cb = sb("conv1_all", [128, NS * S])
        gb = sb("gamma_beta", [128, 4])
        bn = sb("bn_stats", [128, 2, NS, 6])
        mv = sb("bn_mean_var", [128, 2, 2])
        mv2 = sb("bn_moments", [128, 2, 2])
        bt = sb("bn_tmp", [128, 2, 4])
        aff = sb("bn_affine", [128, 2, 2])
        wc = sb("conv_w", [C, 2, C * TAPS])
        wmax = sb("conv_w_max", [C, 2])
        wmax_all = sb("conv_w_max_all", [C, 2])
        wrec = sb("conv_w_rec", [C, 2])
        patf = sb("pat_f", [C, TAPS])
        pati = sb("pat_i", [C, TAPS], I32)
        wdup = sb("conv_w_dup", [C, 2, TAPS, 2, C], BF16)
        wblk = sb("conv_w_blocks", [128, 2, TAPS, 128], BF16)
        qt = [sb(f"quant_tmp{u}", [128, S]) for u in range(2)]
        qpad = [sb(f"quant_padded{u}", [128, IMG, H + 2, W + 2], BF16) for u in range(2)]
        sq = sb("squares", [128, 2, S])
        wide = sb("rstd_wide", [128, GP, C])
        st = sb("stats", [128, 4, GP])

        x1 = [sb(f"x1_{u}", [128, S]) for u in range(2)]
        rows = [sb(f"rows_now{u}", [128, GH * ROW]) for u in range(2)]
        slot_f = sb("slot_f", [128, 2, GP])
        slot_all = sb("slot_all", [128, NS, 2 * GH], I32)
        slot = [sb(f"slot_now{u}", [128, 2 * GH], I32) for u in range(2)]
        token = sb("token_no", [128, GP])
        rw = sb("router_rows", [E, C])
        rwm = sb("router_mean", [E, 1])
        rwc = sb("router_centred", [E, 2, C])
        rwt = sb("router_T", [128, 2 * E])
        lg = sb("logits", [128, NS, GH, E])
        top2 = sb("second_minus_first", [128, NS, GH])
        ra = sb("route_a", [128, GP, E])
        rb = sb("route_b", [128, GP, E])
        rk = sb("route_slots", [128, 2, GP, E])
        m1 = sb("route_max", [128, GP])
        mm = sb("route_pref", [128, GP])
        oh = sb("one_hot", [128, 2, GP, E])
        chosen = sb("chosen", [128, GP + 1, E], BF16)
        pos = sb("positions", [128, GP + 1, E])
        base = sb("base", [128, E])
        bases = sb("base_by_pair", [128, NP, E])
        counts = sb("base_by_level", [128, LV, E])
        gate = sb("gates", [128, 2, NS, GH])
        gsum = sb("gate_sum", [128, NS, GH])
        tm = sb("tile_map_work", [128, 8, LV, E])
        run = sb("tile_map_sums", [128, 2, 2 * LV * E])
        th = sb("half_map_work", [128, 6, E])
        tcol = sb("tile_map_col", [128, 5])
        twide = sb("tile_map_wide", [128, 2, 128])
        expert_of = sb("tile_expert", [128, 2, 128])
        tmap = sb("tile_map", [1, 4, 128], I32)
        padf = sb("pad_slot_f", [128, TH // 128, E])
        padi = sb("pad_slot", [128, TH // 128, E], I32)
        pads = [sb(f"pad_now{u}", [128, 1], I32) for u in range(2)]

        wr = sb("w13_rows", [128, 2, HT, C])
        wt = sb("w13_tail", [128, C])
        wr2 = sb("w2_rows", [C, HID])
        wsp = sb("w13_split", [128, 2 * HT + 1, 2, C], F32R)
        wstk = sb("w13_stacked", [128, WST], F32R)
        w2s = sb("w2_stacked", [128, KT, C])

        wbuf = [[sb(f"w13_{u}", [128, WST], F32R)[:, :] for u in range(2)]]
        w2buf = [[sb(f"w2_{u}", [128, KT, C])[:, :, :] for u in range(2)]]
        wbuf.append([wsp[:, :, :, :].rearrange("p t d c -> p (t d c)"), wstk[:, :]])
        w2buf.append([yb[:, u * KT * C:(u + 1) * KT * C].rearrange("p (k c) -> p k c", k=KT) for u in range(2)])
        free = [0]

        def carve(*shape):
            n = 1
            for d in shape:
                n *= d
            v = cb[:, free[0]:free[0] + n]
            free[0] += n
            assert free[0] <= NS * S
            if len(shape) == 1:
                return v
            names = "abc"[:len(shape)]
            return v.rearrange(f"p ({' '.join(names)}) -> p {' '.join(names)}",
                               **{names[i]: shape[i] for i in range(1, len(shape))})

        xrow = [carve(4, ROW) for u in range(2)]
        hl = [carve(4, 2, C) for u in range(2)]
        sbuf = [carve(T) for u in range(3)]
        hbuf = [carve(T) for u in range(4)]
        second = [carve(4) for u in range(2)]
        ysb = [carve(T) for u in range(2)]
        yrow = [carve(4, C) for u in range(2)]
        dest_all = sb("dest_all", [128, NT, 4], I32)
        destc = [sb(f"dest_now{u}", [128, 4], I32) for u in range(2)]
        xT = [[sb(f"xT_{p}_{u}", [128, T], F32R) for u in range(2)] for p in ("hi_lo", "lo_hi")]
        RING = 4
        yk = [[yb[:, (RING * k + v) * GP * C:(RING * k + v + 1) * GP * C] for v in range(RING)] for k in range(2)]

        x_in = [sem(f"x_in{u}") for u in range(2)]
        small_in = sem("small_in")
        gb_in = sem("gamma_beta_in")
        const_p = sem("const_pool")
        const_v = sem("const_vector")
        zero_p = sem("zeroed_pool")
        p_step = sem("pool_step")
        v_step = sem("vector_step")
        cen_rdy = sem("centred_ready")
        sq_rdy = sem("squares_ready")
        var_rdy = sem("var_ready")
        sd_rdy = sem("sd_ready")
        rstd_rdy = sem("rstd_ready")
        bc_rdy = sem("rstd_spread_ready")
        y_rdy = sem("y_ready")
        x_res = sem("x_plus_y_done")
        staged = sem("rows_staged")
        th_rdy = sem("tanh_ready")
        wm_rdy = sem("wmax_ready")
        wma_rdy = sem("wmax_all_ready")
        wrec_rdy = sem("wmax_reciprocal_ready")
        wd_rdy = sem("conv_w_dup_ready")
        wT_rdy = sem("conv_w_turned")
        wb_rdy = sem("conv_w_blocks_ready")
        agg_rdy = sem("moments_ready")
        pr_rdy = sem("moments_paired")
        bsd_rdy = sem("bn_sd_ready")
        bva_rdy = sem("bn_var_ready")
        aff_rdy = sem("affine_ready")
        y_cen = sem("centred_copied")
        q_rdy = sem("quant_affine_ready")
        qp_rdy = sem("quant_padded_ready")
        cv_rdy = sem("conv_ready")
        c1_rdy = sem("conv1_copied")
        x1_rdy = sem("x1_ready")
        x1_kept = sem("x1_kept")
        rT_rdy = sem("rows_turned")
        lg_rdy = sem("logits_ready")
        rn_rdy = sem("rows_normed")
        rs_rdy = sem("row_squares_ready")
        rsd_rdy = sem("row_sd_ready")
        ch_rdy = sem("chosen_ready")
        pos_rdy = sem("positions_ready")
        slot_rdy = sem("slots_ready")
        scat = [sem(f"row_scatter{u}") for u in range(2)]
        rr_rdy = sem("router_rows_centred")
        rT2 = sem("router_turned")
        rwt_rdy = sem("router_T_ready")
        w_in = sem("w13_in")
        w2_in = sem("w2_in")
        w_zero = sem("w_zeroed")
        ws_rdy = sem("w_split_ready")
        wt_ps = sem("w_turned")
        wt_sb = sem("w_stacked")
        w_out = sem("w_out")
        ex_rdy = sem("exp_ready")
        ex_go = sem("exp_go")
        dummy_out = sem("dummy_out")
        map_rdy = sem("map_cols_ready")
        mapT_rdy = sem("map_turned")
        tmap_rdy = sem("tile_map_ready")
        padi_rdy = sem("pad_slots_ready")
        pad_cp = sem("pad_slot_copied")
        pad_out = [sem(f"pad_out{u}") for u in range(2)]
        xr_in = [[sem(f"{n}_rows_in{u}") for u in range(2)] for n in ("tile", "second")]
        wt_in = [[sem(f"{n}_w_in{u}") for u in range(2)] for n in ("tile", "second")]
        split_rdy = sem("split_ready")
        xt_rdy = sem("xT_ready")
        xt_sb = sem("xT_copied")
        h1_rdy = sem("h1_ready")
        h3_rdy = sem("h3_ready")
        silu_rdy = sem("silu_ready")
        mul_rdy = sem("hidden_ready")
        w2_rdy = sem("w2_done")
        y_sb = sem("y_copied")
        ro_rdy = sem("rows_out_ready")
        yr_sb = sem("y_rows_ready")
        y_out = [sem(f"y_scatter{u}") for u in range(2)]
        yk_in = [sem(f"results_in{v}") for v in range(RING)]
        gate_rdy = sem("gates_ready")
        g0_rdy = sem("gated_first_ready")
        g2_rdy = sem("gated_second_ready")
        g1_rdy = sem("gated_sum_ready")
        fin_rdy = sem("sum_turned")
        o_rdy = sem("out_ready")
        o_out = sem("out_stored")
        passed = sem("passed")

        def wait_apart(eng, sem_, value):
            eng.wait_ge(sem_, value)
            eng.sem_inc(passed, 1)

        def stripe(t, s):
            return t[:, bass.ds(s * S, S)]

        def pipelined(eng, front, back, n):
            front(0, 0)
            front(1, 1)
            back(0, 0)
            front(2, 0)
            back(1, 1)
            with eng.Fori(1, n // 2 - 1) as turn:
                i = 2 * turn
                front(i + 1, 1)
                back(i, 0)
                front(i + 2, 0)
                back(i + 1, 1)
            front(n - 1, 1)
            back(n - 2, 0)
            back(n - 1, 1)

        def pairs(eng, step):
            step(0, first=True)
            with eng.Fori(1, NP - 2) as p:
                step(p)
            step(NP - 2, last=2)
            step(NP - 1, last=1)

        def tiles(eng, tile):
            tile(0, 0, (0, 0, 0), first=True)
            tile(1, 1, (0, 0, 0))
            tile(2, 0, (0, 0, 0))
            tile(3, 1, (0, 0, 0))
            with eng.Fori(2, NF // 2 - 1) as pair_:
                j = 2 * pair_
                tile(j, 0, (0, 0, 0))
                tile(j + 1, 1, (0, 0, 0))
            tile(NF - 2, 0, (0, 0, 1))
            tile(NF - 1, 1, (0, 1, 1))
            with eng.Fori(NF // 2, NT // 2 - 1) as pair_:
                j = 2 * pair_
                tile(j, 0, (1, 1, 1))
                tile(j + 1, 1, (1, 1, 1))
            tile(NT - 2, 0, (1, 1, 1), last=2)
            tile(NT - 1, 1, (1, 1, 1), last=1)

        conv_ps = [bank[0], bank[1]]
        w_bf = bank[6][:, :].bitcast(BF16)

        h1_ps, h3_ps, y_ps = bank[0:3], bank[3:6], bank[6]
        turn_ps = bank[7]

        def w_bank(b):
            return bank[6 + b % 2]

        cen_ps, bc_ps, var_ps = [bank[0:2], bank[2:4]], bank[4:6], bank[6:8]
        rT_ps, lg_ps, pos_ps = bank[2:4], bank[4][:, 0:GP * E], bank[5][:, 0:(GP + 1) * E]
        fin_ps = [bank[0:2], bank[2:4]]

        def gate_of(k, p):
            return gate[:, k, bass.ds(2 * p, 2), :].rearrange("p a g -> p (a g)").unsqueeze(2).broadcast_to([128, GP, C])

        NSMALL = 2 + 1 + 1
        block = ctx.enter_context(nc.Block())

        @block.sync
        def _(sp):
            for p in range(NP):
                if p >= 2:
                    sp.wait_ge(x_in[p % 2], 32 * (p // 2))
                for h in range(2):
                    sp.dma_start(xb[64 * h:64 * h + 64, 2 * S * p:2 * S * (p + 1)]
                                 .rearrange("c (i p) -> c i p", i=2 * IMG), xv[h, p]).then_inc(x_in[p % 2], 16)
                if p == 1:
                    for k, w in enumerate((w1, w2)):
                        sp.dma_start(wc[:, k, :], w.rearrange("o i a b -> o (i a b)")).then_inc(small_in, 16)
                    sp.dma_start(pati[:], pat.rearrange("a b -> (a b)").partition_broadcast(C)).then_inc(small_in, 16)
                    sp.dma_start(rw[:], router_w).then_inc(small_in, 16)
            for k, v in enumerate((gamma1, beta1, gamma2, beta2)):
                for h in range(2):
                    sp.dma_start(gb[64 * h:64 * h + 64, k:k + 1],
                                 v.rearrange("(c a) -> c a", a=1)).then_inc(gb_in, 16)
            sp.wait_ge(const_v, 1)
            sp.dma_start(xs[DUMMY:DUMMY + TH, :].rearrange("(p g) c -> p g c", g=2),
                         pad_rows[:]).then_inc(dummy_out, 16)
            sp.wait_ge(w_zero, 1)
            def weights_in(e):
                for k, w in enumerate((ew1, ew3)):
                    we = w.rearrange("e h c -> e (h c)")
                    sp.dma_start(wr[:, k, :, :].rearrange("p t c -> p (t c)"),
                                 we[bass.ds(e, 1), 0:HT * 128 * C].rearrange("a (p n) -> (a p) n", p=128)
                                 ).then_inc(w_in, 16)
                    sp.dma_start(wt[TAIL3 * k:TAIL3 * k + HR, :],
                                 we[bass.ds(e, 1), HT * 128 * C:HID * C].rearrange("a (p n) -> (a p) n", p=HR)
                                 ).then_inc(w_in, 16)

            def weights2_in(e):
                sp.dma_start(wr2[:], ew2[bass.ds(e, 1), :, :].rearrange("a c h -> (a c) h")).then_inc(w2_in, 16)

            def weights_out(e):
                sp.dma_start(wsc[bass.ds(e * 128, 128), :], wstk[:].bitcast(F32)).then_inc(w_out, 16)
                sp.dma_start(w2sc[bass.ds(e * 128, 128), :], w2s[:].rearrange("p k c -> p (k c)")).then_inc(w_out, 16)

            weights_in(0)
            weights2_in(0)
            with sp.Fori(0, E - 1) as e:
                sp.wait_ge(ws_rdy, 2 * e + 2)
                weights_in(e + 1)
                sp.wait_ge(wt_sb, 4 * e + 4)
                weights2_in(e + 1)
                weights_out(e)
            sp.wait_ge(wt_sb, 4 * E)
            weights_out(E - 1)

            sp.wait_ge(dummy_out, 16)
            sp.wait_ge(tmap_rdy, 1)
            sp.wait_ge(w_out, 32 * E)

            def scattered(stripes):
                for u in range(2):
                    sp.wait_ge(scat[u], 16 * 2 * GH * (stripes // 2))

            def load_rows(j, u, two=0):
                sp.wait_ge(split_rdy, j + 1)
                n = T >> two
                for i in range(1 + two):
                    at = tmap[0:1, two, bass.ds(2 * j - 2 * NF + i if two else j, 1)]
                    src = sp.value_load(at, min_val=0, max_val=DUMMY if two else DUMMY - T)
                    sp.dma_start(xrow[u][:, 2 * i:2 * i + n // 128, :],
                                 xs[bass.ds(src, n), :].rearrange("(p g) c -> p g c", g=n // 128)
                                 ).then_inc(xr_in[i][u], 16)

            def load_weights(j, u, two=0, first=False):
                for i in range(1 + two):
                    at = tmap[0:1, 2 + two, bass.ds(2 * j - 2 * NF + i if two else j, 1)]
                    exp = sp.value_load(at, min_val=0, max_val=(E - 1) * 128)
                    if not first and i == 0:
                        sp.wait_ge(h1_rdy, KT * j - KT)
                    sp.dma_start(wbuf[i][u].bitcast(F32), wsc[bass.ds(exp, 128), :]).then_inc(wt_in[i][u], 16)
                    if not first and i == 0:
                        sp.wait_ge(w2_rdy, KT // 2 * j - KT // 2 + 2)
                    sp.dma_start(w2buf[i][u].rearrange("p k c -> p (k c)"), w2sc[bass.ds(exp, 128), :]
                                 ).then_inc(wt_in[i][u], 16)

            scattered(SNAPS[0])
            for u in range(2):
                load_rows(u, u)
                load_weights(u, u, first=True)
            for u in range(2):
                load_rows(2 + u, u)
            for level in range(LV):
                if level:
                    scattered(SNAPS[level])
                with sp.Fori(FULL[level - 1] // 2 - 1 if level else 1, FULL[level] // 2 - 1) as pair_:
                    j = 2 * pair_
                    for u in range(2):
                        load_weights(j + u, u)
                        load_rows(j + u + 2, u)
            sp.wait_ge(tmap_rdy, 2)
            for u in range(2):
                sp.wait_ge(pad_out[u], 16 * NPAD // 2)
            for u in range(2):
                load_weights(NF - 2 + u, u)
                load_rows(NF + u, u, two=1)
            with sp.Fori(NF // 2, NT // 2 - 1) as pair_:
                j = 2 * pair_
                for u in range(2):
                    load_weights(j + u, u, two=1)
                    load_rows(j + u + 2, u, two=1)
            for u in range(2):
                load_weights(NT - 2 + u, u, two=1)

            for u in range(2):
                sp.wait_ge(y_out[u], 64 * (NT // 2))

            def results(p, v):
                sp.wait_ge(fin_rdy, 2 * p + 2)
                for k in range(2):
                    sp.dma_start(yk[k][v].rearrange("q (i n) -> q i n", i=2),
                                 yout[bass.ds(p * 4 * S + k * TOK, 4 * S), :]
                                 .rearrange("(i q g) c -> q i (g c)", i=2, g=GH)).then_inc(yk_in[v], 16)

            with sp.Fori(0, NP // RING) as turn:
                for v in range(RING):
                    results(RING * turn + v, v)
            sp.wait_ge(o_out, 32 * NP)

        @block.gpsimd
        def _(pool):
            def made(ins, n=[0]):
                n[0] += 1
                ins.then_inc(p_step, 1)
                pool.wait_ge(p_step, n[0])

            made(nc.gpsimd.memset(ident[:], 0.0))
            made(nc.gpsimd.affine_select(out=ident[:], in_=ident[:], compare_op=ALU.not_equal, fill=1.0,
                                         base=0, pattern=[[-1, 128]], channel_multiplier=1))
            made(nc.gpsimd.tensor_copy(ident_bf[:], ident[:]))
            made(nc.gpsimd.memset(before[:], 1.0))
            made(nc.gpsimd.affine_select(out=before[:], in_=before[:], compare_op=ALU.is_gt, fill=0.0,
                                         base=0, pattern=[[1, 128]], channel_multiplier=-1))
            iota = lambda t, pattern, base, cm: made(nc.gpsimd.iota(t, pattern=pattern, base=base,
                   channel_multiplier=cm, allow_small_or_imprecise_dtypes=True))
            iota(first_pref[:], [[0, GP], [-1, E]], E, 0)
            iota(expert_no[:], [[0, LV], [1, E]], 0, 0)
            iota(region[:], [[0, LV], [1, E]], 0, 0)
            iota(tile_no[:], [[0, 1]], 0, 1)
            iota(pad_off[:], [[128, TH // 128], [0, E]], 0, 1)
            iota(token0[:], [[2 * S, 2], [1, GH]], 0, GH)
            made(nc.gpsimd.memset(ones_bf[:], 1.0))
            pool.sem_inc(const_p, 1)
            for t in (chosen, rwt, wblk, *qpad):
                ins = nc.gpsimd.memset(t[:], 0.0)
            ins.then_inc(zero_p, 1)

            pool.wait_ge(wm_rdy, 1)
            made(nc.gpsimd.partition_all_reduce(wmax_all[:], wmax[:], C, RED_MAX))
            P = nc.gpsimd
            made(P.tensor_copy(patf[:], pati[:]))
            made(P.tensor_scalar(wrec[:], wmax_all[:], 2.0, None, ALU.mult))
            pool.sem_inc(wma_rdy, 1)
            pool.wait_ge(wrec_rdy, 1)
            for k in range(2):
                made(P.tensor_scalar(wc[:, k, :], wc[:, k, :], wrec[:, k:k + 1], 0.5, ALU.mult, ALU.add))
            made(P.tensor_scalar(wc[:], wc[:], LEVELS, ROUND, ALU.mult, ALU.add))
            made(P.tensor_scalar(wc[:], wc[:], -ROUND, 2.0, ALU.add, ALU.mult))
            made(P.tensor_scalar(wc[:], wc[:], -LEVELS, None, ALU.add))
            for k in range(2):
                for d in range(2):
                    ins = P.tensor_tensor(wdup[:, k, :, d, :], wc[:, k, :].rearrange("o (i t) -> o t i", t=TAPS),
                                          patf[:].unsqueeze(2).broadcast_to([C, TAPS, C]), ALU.mult)
            ins.then_inc(wd_rdy, 1)

            with pool.Fori(0, NS) as s:
                pool.wait_ge(y_rdy, s + 2)
                nc.gpsimd.tensor_tensor(stripe(xb, s), stripe(xb, s), stripe(yb, s), ALU.add).then_inc(x_res, 1)

            def stage(s, u):
                wait_apart(pool, slot_rdy, s + 1)
                if not isinstance(s, int) or s >= 2:
                    wait_apart(pool, scat[u], (s - u) * 128)
                nc.gpsimd.tensor_copy(rows[u][:], rows_all[:, bass.ds(s, 1)].rearrange("p a g r -> p (a g r)"))
                nc.gpsimd.tensor_copy(slot[u][:], slot_all[:, bass.ds(s, 1)].rearrange("p a k -> p (a k)")
                                      ).then_inc(staged, 1)
                wait_apart(pool, staged, s + 1)

            def scatter(u, k, groups=range(GH)):
                for g in groups:
                    nc.gpsimd.indirect_dma_start(
                        xs, bass.IndirectOffsetOnAxis(ap=slot[u][:, k * GH + g:k * GH + g + 1], axis=0),
                        rows[u][:, g * ROW:g * ROW + ROW], None).then_inc(scat[u], 16)

            def scatter_stripe(s, u):
                stage(s, u)
                scatter(u, 0)
                scatter(u, 1)

            scatter_stripe(0, 0)
            scatter_stripe(1, 1)
            with pool.Fori(1, AHEAD // 2) as pair_:
                i = 2 * pair_
                scatter_stripe(i, 0)
                scatter_stripe(i + 1, 1)

            def scatter_y(j, u):
                wait_apart(pool, yr_sb, j + 3)
                for g in range(4):
                    nc.gpsimd.indirect_dma_start(
                        yout, bass.IndirectOffsetOnAxis(ap=destc[u][:, g:g + 1], axis=0),
                        yrow[u][:, g, :], None, bounds_check=2 * TOK - 1, oob_is_err=False
                    ).then_inc(y_out[u], 16)

            def scatter_pad(n, u):
                if not isinstance(n, int) or n >= 2:
                    pool.wait_ge(pad_out[u], (n - u) * 8)
                nc.gpsimd.tensor_copy(pads[u][:], padi_flat[:, bass.ds(n, 1)]).then_inc(pad_cp, 1)
                wait_apart(pool, pad_cp, n + 1)
                nc.gpsimd.indirect_dma_start(
                    xs, bass.IndirectOffsetOnAxis(ap=pads[u][:], axis=0),
                    pad_rows[:, 0, :], None).then_inc(pad_out[u], 16)

            def four_tiles(j, s, u):
                stage(s, u)
                for i in range(4):
                    scatter(u, i // 2, range(i % 2 * G, i % 2 * G + G))
                    scatter_y(j + i, i % 2)

            late = NS - AHEAD
            assert AHEAD % 2 == 0
            with pool.Fori(0, late // 2) as turn:
                four_tiles(8 * turn, AHEAD + 2 * turn, 0)
                four_tiles(8 * turn + 4, AHEAD + 2 * turn + 1, 1)

            padi_flat = padi[:].rearrange("p i e -> p (i e)")
            pool.wait_ge(padi_rdy, 1)
            J0, J1 = 4 * late, 4 * late + NPAD // 2
            assert J1 < NF - 2
            def pads_and_tiles(n, j):
                for v in range(2):
                    scatter_pad(n + 2 * v, 0)
                    scatter_pad(n + 2 * v + 1, 1)
                    scatter_y(j + v, v)

            pads_and_tiles(0, J0)
            with pool.Fori(1, NPAD // 4) as turn:
                pads_and_tiles(4 * turn, J0 + 2 * turn)
            with pool.Fori(J1 // 2, NT // 2) as pair_:
                j = 2 * pair_
                for u in range(2):
                    scatter_y(j + u, u)

            def gate2(p, v):
                pool.wait_ge(yk_in[v], (p - v) * (32 // RING) + 32)
                y = yk[1][v].rearrange("p (g c) -> p g c", g=GP)
                nc.gpsimd.tensor_tensor(y, y, gate_of(1, p), ALU.mult).then_inc(g2_rdy, 1)

            pool.wait_ge(gate_rdy, 1)
            with pool.Fori(0, NP // RING) as turn:
                for v in range(RING):
                    gate2(RING * turn + v, v)

        @block.scalar
        def _(act):
            act.sem_inc(c1_rdy, 2)
            act.sem_inc(x1_kept, 2)
            act.sem_inc(y_sb, 1)
            act.wait_ge(small_in, 16 * NSMALL)
            nc.scalar.activation(wc[:], wc[:], ACT.Tanh).then_inc(th_rdy, 1)

            def square(p, v):
                for u in range(2):
                    s = 2 * p + u
                    act.wait_ge(cen_rdy, s + 1)
                    if u == 0:
                        act.wait_ge(var_rdy, p + 1)
                    nc.scalar.activation(sq[:, u, :], cen_ps[v][u][:], ACT.Square).then_inc(sq_rdy, 1)
                    nc.scalar.activation(stripe(yb, s), cen_ps[v][u][:], ACT.Copy).then_inc(y_cen, 1)

            def sd(p, v):
                act.wait_ge(sd_rdy, 2 * p + 1)
                nc.scalar.activation(st[:, 1, :], st[:, 0, :], ACT.Sqrt).then_inc(sd_rdy, 1)

            pipelined(act, square, sd, NP)

            def affine(l, s, u):
                act.wait_ge(qp_rdy, s + l * NS + 1)
                nc.scalar.activation(qt[u][:], stripe(cb if l else yb, s), ACT.Relu,
                                     bias=aff[:, l, 1:2], scale=aff[:, l, 0:1]).then_inc(q_rdy, 1)

            def keep_conv1(s, u):
                act.wait_ge(cv_rdy, s + 3)
                nc.scalar.activation(stripe(cb, s), conv_ps[u][:], ACT.Copy).then_inc(c1_rdy, 1)

            act.wait_ge(bva_rdy, 1)
            nc.scalar.activation(bt[:, 0, 1:2], bt[:, 0, 0:1], ACT.Sqrt).then_inc(bsd_rdy, 1)
            act.wait_ge(aff_rdy, 1)
            pipelined(act, lambda s, u: affine(0, s, u), keep_conv1, NS)
            act.wait_ge(bva_rdy, 2)
            nc.scalar.activation(bt[:, 1, 1:2], bt[:, 1, 0:1], ACT.Sqrt).then_inc(bsd_rdy, 1)
            act.wait_ge(aff_rdy, 2)

            def squares(p):
                for u in range(2):
                    s = 2 * p + u
                    act.wait_ge(x1_rdy, s + 3)
                    nc.scalar.activation(stripe(xb, s), x1[u][:], ACT.Copy).then_inc(x1_kept, 1)
                for u in range(2):
                    act.wait_ge(rT_rdy, 2 * p + u + 1)
                    nc.scalar.activation(sq[:, u, :], rT_ps[u][:], ACT.Square).then_inc(rs_rdy, 1)

            def route(p, first=False, last=0):
                act.wait_ge(rsd_rdy, 2 * p + 1)
                nc.scalar.activation(st[:, 1, :], st[:, 0, :], ACT.Sqrt).then_inc(rsd_rdy, 1)
                if not last:
                    for u in range(2):
                        affine(1, 2 * p + 4 + u, u)
                if not first:
                    wait_apart(act, w_out, 32 * p)
                for b in range(3):
                    n = min(512, WST - 512 * b)
                    act.wait_ge(wt_ps, 4 * p + b + 1)
                    nc.scalar.activation(wstk[:, 512 * b:512 * b + n], w_bank(b)[:, 0:n],
                                         ACT.Copy).then_inc(wt_sb, 1)
                act.wait_ge(wt_ps, 4 * p + 4)
                nc.scalar.activation(w2s[:, 0:HT, :].rearrange("p k c -> p (k c)"), w_bank(3)[:, 0:HT * C],
                                     ACT.Copy)
                nc.scalar.activation(w2s[0:HR, HT, :], w_bank(3)[0:HR, HT * C:KT * C],
                                     ACT.Copy).then_inc(wt_sb, 1)
                if last != 1:
                    squares(p + 1)

            for s in range(4):
                affine(1, s, s % 2)
            squares(0)
            pairs(act, route)

            act.wait_ge(ex_go, 1)
            nc.scalar.activation(lg[:], lg[:], ACT.Exp).then_inc(ex_rdy, 1)
            nc.scalar.activation(top2[:], top2[:], ACT.Exp).then_inc(ex_rdy, 1)
            nc.scalar.activation(silu_first[:], half_col[:, 0:1], ACT.Silu)

            def silu(j, k):
                m = 128 if k < HT else HR
                act.wait_ge(h1_rdy, KT * j + k + 1)
                nc.scalar.activation(sbuf[k % 3][0:m, :], h1_ps[k % 3][0:m, :], ACT.Silu).then_inc(silu_rdy, 1)

            def copy_xT(j, u, part):
                if part == 0:
                    act.wait_ge(xt_rdy, j + 1)
                    nc.scalar.activation(xT[0][u][:], turn_ps[:], ACT.Copy)
                    nc.scalar.activation(xT[1][u][0:C, :], turn_ps[C:2 * C, :], ACT.Copy)
                else:
                    nc.scalar.activation(xT[1][u][C:2 * C, :], turn_ps[0:C, :], ACT.Copy).then_inc(xt_sb, 1)

            def copy_y(j, u):
                act.wait_ge(w2_rdy, KT // 2 * j + KT // 2 + 2)
                act.wait_ge(ro_rdy, j + 1)
                nc.scalar.activation(ysb[u], y_ps[:], ACT.Copy).then_inc(y_sb, 1)

            def tile(j, u, two, first=False, last=0):
                if not first:
                    copy_y(j - 1, 1 - u)
                if last != 1:
                    copy_xT(j + 1, 1 - u, 0)
                silu(j, 2)
                if last != 1:
                    copy_xT(j + 1, 1 - u, 1)
                for k in range(3, KT):
                    silu(j, k)
                if last != 1:
                    silu(j + 1, 0)
                    silu(j + 1, 1)

            copy_xT(0, 0, 0)
            copy_xT(0, 0, 1)
            silu(0, 0)
            silu(0, 1)
            tiles(act, tile)
            copy_y(NT - 1, 1)

            def store(p):
                act.wait_ge(o_rdy, 2 * p + 6)
                for h in range(2):
                    act.dma_start(outv[h, bass.ds(p, 1)].rearrange("a c i p -> (a c) i p"),
                                  xb[64 * h:64 * h + 64, bass.ds(2 * S * p, 2 * S)]
                                  .rearrange("c (i p) -> c i p", i=2 * IMG)).then_inc(o_out, 16)

            with act.Fori(0, NP) as p:
                store(p)

        @block.vector
        def _(dve):
            class Chain:
                base = 0

                def begin(self, n=0, per=0):
                    self.at, self.k, self.per = n, 0, per
                    return self

                def __call__(self, ins, *between):
                    self.k += 1
                    ins.then_inc(self.sem, 1)
                    for work in between:
                        work()
                    dve.wait_ge(self.sem, self.base + self.at * self.per + self.k)

                def end(self):
                    assert self.k == self.per, self.k

            def chain(name):
                c = Chain()
                c.sem = sem(name)
                return c

            V = nc.vector
            one = chain("vector_straight").begin()
            dve.sem_inc(o_rdy, 4)
            for s_ in (qp_rdy, x1_rdy, split_rdy, yr_sb):
                dve.sem_inc(s_, 2)
            dve.sem_inc(mul_rdy, 3)
            for s_ in (rn_rdy, ch_rdy, y_rdy):
                dve.sem_inc(s_, 1)

            V.memset(wt[:], 0.0)
            V.memset(w2s[:], 0.0).then_inc(w_zero, 1)
            V.memset(run[:], 0.0)
            one(V.memset(pad_rows[:], 0.0))
            one(V.memset(pad_rows[:, :, C:C + 1], float(1 << 20)))
            one(V.memset(same_half[:], 0.0))
            V.memset(same_half[0:64, 0:64], 1.0 / C)
            one(V.memset(same_half[64:128, 64:128], 1.0 / C))
            one(V.memset(half_col[:], 0.0))
            V.memset(half_col[0:64, 0:1], 1.0 / C)
            V.memset(half_col[64:128, 1:2], 1.0 / C)
            dve.wait_ge(const_p, 1)
            one(V.tensor_tensor(centre[:], ident[:], same_half[:], ALU.subtract))
            one(V.tensor_tensor(fold[:], ident[:, 0:C], ident[:, C:2 * C], ALU.add))
            for h in range(2):
                one(V.tensor_scalar(pair[:, C * h:C * h + C], fold[:], 0.5, None, ALU.mult))
            one(V.tensor_scalar(region[:], region[:], float(REG), None, ALU.mult))
            one(V.tensor_copy(base[:], region[:, 0, :]))
            V.tensor_copy(token[:], token0[:]).then_inc(const_v, 1)

            dve.wait_ge(th_rdy, 1)
            V.tensor_reduce(wmax[:], wc[:], AX.X, ALU.max, apply_absolute_value=True).then_inc(wm_rdy, 1)
            one(V.tensor_reduce(rwm[:], rw[:], AX.X, ALU.add))
            one(V.tensor_scalar(rwm[:], rwm[:], -1.0 / C, None, ALU.mult))
            V.tensor_scalar(rwc[:, 0, :], rw[:], rwm[:, 0:1], None, ALU.add)
            V.tensor_scalar(rwc[:, 1, :], rw[:], rwm[:, 0:1], None, ALU.add).then_inc(rr_rdy, 1)

            def rstd(c, *between):
                var, sd_, r, w = (st[:, k] for k in range(4))
                fill = [(f,) for f in between] + [()] * (4 - len(between))
                c(V.reciprocal(r, sd_), *fill[0])
                c(V.tensor_tensor(w, var, r, ALU.mult), *fill[1])
                c(V.tensor_tensor(w, w, r, ALU.mult), *fill[2])
                c(V.tensor_scalar(w, w, -0.5, 1.5, ALU.mult, ALU.add), *fill[3])
                c(V.tensor_tensor(r, r, w, ALU.mult))

            ln = chain("vector_layernorm")

            def spread(p, v):
                c = ln.begin(p, 5)
                dve.wait_ge(var_rdy, p + 2)
                V.tensor_scalar(st[:, 0, :], var_ps[v][:, 0:GP], 1e-6, None, ALU.add).then_inc(sd_rdy, 1)
                dve.wait_ge(sd_rdy, 2 * p + 2)
                rstd(c)
                dve.wait_ge(bc_rdy, 2 * p + 2)
                V.tensor_copy(wide[:], st[:, 2, :].unsqueeze(2).broadcast_to([128, GP, C])).then_inc(rstd_rdy, 1)
                c.end()

            def norm(p, v):
                for u in range(2):
                    s = 2 * p + u
                    dve.wait_ge(bc_rdy, s + 3)
                    dve.wait_ge(y_cen, s + 1)
                    V.tensor_tensor(stripe(yb, s), stripe(yb, s), bc_ps[u][:], ALU.mult).then_inc(y_rdy, 1)
                for u in range(2):
                    s = 2 * p + u
                    dve.wait_ge(y_rdy, s + 2)
                    V.bn_stats(bn[:, 0, bass.ds(s, 1), :].rearrange("p a n -> p (a n)"), stripe(yb, s))

            dve.wait_ge(wma_rdy, 1)
            V.reciprocal(wrec[:], wrec[:]).then_inc(wrec_rdy, 1)
            pipelined(dve, spread, norm, NP)

            dve.wait_ge(zero_p, 1)
            for k in range(2):
                dve.wait_ge(wT_rdy, k + 1)
                turned = w_bf[:, 0:TAPS * C].rearrange("p (t c) -> p t c", t=TAPS)
                V.tensor_copy(wblk[0:64, k, :, 0:64], turned[0:64])
                V.tensor_copy(wblk[64:128, k, :, 64:128], turned[64:128]).then_inc(wb_rdy, 1)
            dve.wait_ge(rT2, 1)
            V.tensor_copy(rwt[0:64, 0:E], bank[7][0:64, 0:E])
            V.tensor_copy(rwt[64:128, E:2 * E], bank[7][64:128, 0:E]).then_inc(rwt_rdy, 1)

            def batch_norm(l, of):
                one(V.bn_aggr(mv[:, l, :], bn[:, l].rearrange("p s n -> p (s n)")))
                V.tensor_copy(mv2[:, l, 0:1], mv[:, l, 0:1])
                V.scalar_tensor_tensor(mv2[:, l, 1:2], mv[:, l, 0:1], mv[:, l, 0:1], mv[:, l, 1:2],
                                       ALU.mult, ALU.add).then_inc(agg_rdy, 1)
                dve.wait_ge(pr_rdy, l + 1)
                t = bt[:, l, :]
                mean, m2_ = mv[:, l, 0:1], mv[:, l, 1:2]
                one(V.tensor_copy(mv[:, l, :], bank[6][:, 0:2]))
                one(V.tensor_tensor(t[:, 0:1], mean, mean, ALU.mult))
                one(V.tensor_tensor(t[:, 0:1], m2_, t[:, 0:1], ALU.subtract))
                V.tensor_scalar(t[:, 0:1], t[:, 0:1], of * of, 1e-5, ALU.mult, ALU.add).then_inc(bva_rdy, 1)
                dve.wait_ge(bsd_rdy, l + 1)
                one(V.reciprocal(t[:, 2:3], t[:, 1:2]))
                one(V.tensor_tensor(t[:, 3:4], t[:, 0:1], t[:, 2:3], ALU.mult))
                one(V.tensor_tensor(t[:, 3:4], t[:, 3:4], t[:, 2:3], ALU.mult))
                one(V.tensor_scalar(t[:, 3:4], t[:, 3:4], -0.5, 1.5, ALU.mult, ALU.add))
                one(V.tensor_tensor(t[:, 2:3], t[:, 2:3], t[:, 3:4], ALU.mult))
                one(V.tensor_scalar(t[:, 2:3], t[:, 2:3], gb[:, 2 * l:2 * l + 1], LEVELS * of, ALU.mult, ALU.mult))
                V.tensor_copy(aff[:, l, 0:1], t[:, 2:3])
                one(V.tensor_tensor(t[:, 3:4], mean, t[:, 2:3], ALU.mult))
                V.scalar_tensor_tensor(aff[:, l, 1:2], gb[:, 2 * l + 1:2 * l + 2], LEVELS, t[:, 3:4],
                                       ALU.mult, ALU.subtract).then_inc(aff_rdy, 1)

            q_chain = chain("vector_quant")

            def quant_round(l, s, u):
                dve.wait_ge(q_rdy, s + l * NS + 1)
                V.tensor_scalar(qt[u][:], qt[u][:], LEVELS, ROUND, ALU.min, ALU.add).then_inc(q_chain.sem, 1)

            def quant_pad(l, s, u):
                dve.wait_ge(q_chain.sem, s + l * NS + 1)
                dve.wait_ge(cv_rdy, s + l * NS + 1)
                V.tensor_scalar(qpad[u][:, :, 1:H + 1, 1:W + 1],
                                qt[u][:].rearrange("p (i a b) -> p i a b", i=IMG, a=H), -ROUND, None,
                                ALU.add).then_inc(qp_rdy, 1)

            def quantise(l, s, u):
                quant_round(l, s, u)
                quant_pad(l, s, u)

            b_chain = chain("vector_conv1_stats")

            def stats1(s, u):
                dve.wait_ge(c1_rdy, s + 3)
                c = b_chain.begin(s, 1)
                c(V.bn_stats(bn[:, 1, bass.ds(s, 1), :].rearrange("p a n -> p (a n)"), stripe(cb, s)))
                c.end()

            dve.wait_ge(gb_in, 16 * 8)
            batch_norm(0, 1.0)
            pipelined(dve, lambda s, u: quantise(0, s, u),
                      lambda s, u: None if isinstance(s, int) and s == 0 else stats1(s - 1, 1 - u), NS)
            stats1(NS - 1, 1)
            batch_norm(1, 1.0 / (LEVELS * LEVELS))

            r_chain = chain("vector_route")

            def add_conv(p, u):
                s = 2 * p + u
                dve.wait_ge(cv_rdy, s + NS + 3)
                dve.wait_ge(x_res, NS)
                dve.wait_ge(x1_kept, s + 1)
                dve.wait_ge(lg_rdy, p + 1)
                V.scalar_tensor_tensor(x1[u][:], conv_ps[u][:], 1.0 / (LEVELS * LEVELS), stripe(xb, s),
                                       ALU.mult, ALU.add).then_inc(x1_rdy, 1)

            def of_pair(t, p):
                v = t[:, bass.ds(2 * p, 2)]
                return v.rearrange("p a g e -> p (a g) e") if len(t.shape) == 4 else v.rearrange("p a g -> p (a g)")

            def route(p, first=False, last=0):
                c = r_chain.begin(p, 21)
                wideof = lambda a, n: a.unsqueeze(2).broadcast_to([128, a.shape[1], n])
                wr_ = wr[:].rearrange("p k t c -> p (k t) c")
                rows_p = of_pair(rows_all, p)
                lgs, m2 = of_pair(lg, p), of_pair(top2, p)

                def high():
                    dve.wait_ge(w_in, 64 * p + 64)
                    V.tensor_copy(wsp[:, 0:2 * HT, 0, :], wr_)
                    V.tensor_copy(wsp[:, 2 * HT, 0, :], wt[:]).then_inc(ws_rdy, 1)

                def low(n):
                    def work():
                        dve.wait_ge(ws_rdy, 2 * p + 1)
                        a = slice(4 * n, min(4 * n + 4, 2 * HT))
                        ins = V.tensor_tensor(wsp[:, a, 1, :], wr_[:, a], wsp[:, a, 0, :].bitcast(F32), ALU.subtract)
                        if 4 * n + 4 >= 2 * HT:
                            V.tensor_tensor(wsp[:, 2 * HT, 1, :], wt[:], wsp[:, 2 * HT, 0, :].bitcast(F32), ALU.subtract
                                            ).then_inc(ws_rdy, 1)
                    return work

                def norm_rows(u):
                    def work():
                        rows_s = rows_all[:, bass.ds(2 * p + u, 1)].rearrange("p a g r -> p (a g) r")
                        ins = V.tensor_tensor(rows_s[:, :, 0:C], rT_ps[u][:].rearrange("p (g c) -> p g c", c=C),
                                              wideof(st[:, 2, GH * u:GH * u + GH], C), ALU.mult)
                        if u == 1:
                            ins.then_inc(rn_rdy, 1)
                    return work

                next_conv = [lambda u=u: add_conv(p + 1, u) if last != 1 else None for u in range(2)]
                quant = [lambda f=f, u=u: f(1, 2 * p + 4 + u, u) if not last else None
                         for f in (quant_round, quant_pad) for u in range(2)]
                assert 2 * HT <= 12

                dve.wait_ge(rs_rdy, 2 * p + 2)
                c(V.tensor_reduce(st[:, 0], sq[:].rearrange("p u (g c) -> p (u g) c", c=C), AX.X, ALU.add))
                V.tensor_scalar(st[:, 0], st[:, 0], 1.0 / C, 1e-5, ALU.mult, ALU.add).then_inc(rsd_rdy, 1)
                high()
                dve.wait_ge(rsd_rdy, 2 * p + 2)
                rstd(c, low(0), low(1), low(2))
                dve.wait_ge(lg_rdy, p + 2)
                c(V.tensor_tensor(ra[:], lg_ps.rearrange("p (g e) -> p g e", e=E), wideof(st[:, 2], E), ALU.mult),
                  norm_rows(0))
                c(V.tensor_reduce(m1[:], ra[:], AX.X, ALU.max), norm_rows(1))
                c(V.tensor_tensor(lgs, ra[:], wideof(m1[:], E), ALU.subtract),
                  lambda: V.tensor_copy(rows_p[:, :, C], token[:]))
                c(V.scalar_tensor_tensor(rb[:], lgs, 0.0, first_pref[:], ALU.is_equal, ALU.mult), next_conv[0])
                c(V.tensor_reduce(mm[:], rb[:], AX.X, ALU.max), next_conv[1])
                c(V.tensor_tensor(oh[:, 0], rb[:], wideof(mm[:], E), ALU.is_equal),
                  lambda: V.tensor_copy(rows_p[:, :, C + 1], mm[:]))
                c(V.scalar_tensor_tensor(ra[:], oh[:, 0], NOT_CHOSEN, lgs, ALU.mult, ALU.add), quant[0])
                c(V.tensor_reduce(m2, ra[:], AX.X, ALU.max), quant[1])
                c(V.tensor_tensor(rb[:], ra[:], wideof(m2, E), ALU.is_equal),
                  lambda: V.tensor_scalar(token[:], token[:], float(4 * S), None, ALU.add))
                c(V.tensor_tensor(rb[:], rb[:], first_pref[:], ALU.mult))
                c(V.tensor_reduce(mm[:], rb[:], AX.X, ALU.max))
                c(V.tensor_tensor(oh[:, 1], rb[:], wideof(mm[:], E), ALU.is_equal))
                V.tensor_tensor(chosen[:, 0:GP, :], oh[:, 0], oh[:, 1], ALU.add).then_inc(ch_rdy, 1)
                quant[2]()
                quant[3]()
                dve.wait_ge(pos_rdy, p + 1)
                c(V.tensor_tensor(pos[:], pos_ps.rearrange("p (g e) -> p g e", e=E),
                                  base[:].unsqueeze(1).broadcast_to([128, GP + 1, E]), ALU.add))
                c(V.tensor_tensor(rk[:], oh[:], pos[:, 0:GP, :].unsqueeze(1).broadcast_to([128, 2, GP, E]), ALU.mult),
                  lambda: V.tensor_copy(base[:], pos[:, GP, :]),
                  lambda: V.tensor_copy(bases[:, bass.ds(p, 1)].rearrange("p a e -> p (a e)"), pos[:, GP, :]))
                c(V.tensor_reduce(slot_f[:], rk[:], AX.X, ALU.add))
                V.tensor_copy(slot_all[:, bass.ds(2 * p, 2)].rearrange("p i (k g) -> p k i g", k=2),
                              slot_f[:].rearrange("p k (i g) -> p k i g", i=2)).then_inc(slot_rdy, 2)
                c.end()

            for u in range(2):
                quantise(1, u, u)
            for u in range(2):
                add_conv(0, u)
            for u in range(2):
                quantise(1, 2 + u, u)
            pairs(dve, route)
            V.memset(mm[:], 0.0).then_inc(ex_go, 1)
            for level, n in enumerate(SNAPS):
                one(V.tensor_copy(counts[:, level, :], bases[:, n // 2 - 1, :]))

            tiles_of, begin, cnt, a, in_, tmp = (tm[:, k] for k in range(6))
            flat = lambda v: v.rearrange("p l e -> p (l e)")
            cum = tm[:, 6]
            for n in range(TH // 128):
                V.tensor_tensor(padf[:, n, :], pad_off[:, n, :], base[:], ALU.add)
            one(V.tensor_tensor(cnt, counts[:], region[:], ALU.subtract))
            V.tensor_copy(padi[:], padf[:]).then_inc(padi_rdy, 1)
            one(V.tensor_scalar(tmp, cnt, -(T / 2 - 0.5), 1.0 / T, ALU.add, ALU.mult))
            one(V.tensor_scalar(cum, tmp, ROUND, -ROUND, ALU.add, ALU.add))
            V.memset(begin[:, 0, :], 0.0)
            one(V.tensor_copy(begin[:, 1:LV, :], cum[:, 0:LV - 1, :]))
            one(V.tensor_tensor(tiles_of, cum, begin, ALU.subtract))
            Z = LV * E

            def less_before(out_, of):
                n = of.shape[1]
                one(V.tensor_copy(run[:, 0, Z:Z + n], of))
                step, at = 1, 0
                while step < n:
                    one(V.tensor_tensor(run[:, 1 - at, Z:Z + n], run[:, at, Z:Z + n],
                                        run[:, at, Z - step:Z - step + n], ALU.add))
                    step, at = 2 * step, 1 - at
                one(V.tensor_tensor(out_, of, run[:, at, Z:Z + n], ALU.subtract))

            less_before(flat(tmp), flat(tiles_of))

            def place(a_, in_t, less_, n_of, start, rows_, reg, exps, col):
                one(V.tensor_scalar(a_, less_, tile_no[:, 0:1], None, ALU.add))
                one(V.tensor_tensor(in_t, a_, n_of, ALU.is_lt))
                one(V.scalar_tensor_tensor(in_t, a_, 0.0, in_t, ALU.is_ge, ALU.mult))
                one(V.scalar_tensor_tensor(a_, a_, float(rows_), start, ALU.mult, ALU.add))
                one(V.tensor_tensor(a_, a_, reg, ALU.add))
                one(V.tensor_tensor(a_, a_, in_t, ALU.mult))
                one(V.tensor_reduce(tcol[:, col:col + 1], a_, AX.X, ALU.add))
                if col:
                    one(V.tensor_reduce(tcol[:, 4:5], in_t, AX.X, ALU.add))
                one(V.tensor_tensor(in_t, in_t, exps, ALU.mult))
                one(V.tensor_reduce(tcol[:, 2 + col:3 + col], in_t, AX.X, ALU.add))

            one(V.tensor_scalar(begin, begin, float(T), None, ALU.mult))
            place(flat(a), flat(in_), flat(tmp), flat(tiles_of), flat(begin), T, flat(region[:]),
                  flat(expert_no[:]), 0)
            V.tensor_copy(twide[:, 0, :], tcol[:, 2:3].broadcast_to([128, 128])).then_inc(map_rdy, 1)
            dve.wait_ge(mapT_rdy, 1)
            V.tensor_scalar(expert_of[:, 0, :], bank[5][:, 128:256], -1.0, float(E), ALU.mult, ALU.add)
            V.tensor_copy(tmap[:, 0, :], bank[5][0:1, 0:128])
            V.tensor_scalar(tmap[:, 2, :], bank[5][0:1, 128:256], 128.0, None, ALU.mult).then_inc(tmap_rdy, 1)

            rest, first, nh, ah, inh, less = (th[:, k] for k in range(6))
            one(V.tensor_scalar(first, tmp[:, LV - 1, :], float(NF), 0.0, ALU.add, ALU.max))
            one(V.tensor_tensor(first, first, tiles_of[:, LV - 1, :], ALU.min))
            one(V.scalar_tensor_tensor(first, first, float(T), begin[:, LV - 1, :], ALU.mult, ALU.add))
            one(V.tensor_tensor(rest, cnt[:, LV - 1, :], first, ALU.subtract))
            one(V.tensor_scalar(nh, rest, TH / 2 - 0.5, 1.0 / TH, ALU.add, ALU.mult))
            one(V.tensor_scalar(nh, nh, ROUND, -ROUND, ALU.add, ALU.add))
            less_before(less, nh)
            place(ah, inh, less, nh, first, TH, region[:, 0, :], expert_no[:, 0, :], 1)
            one(V.tensor_scalar(tcol[:, 4:5], tcol[:, 4:5], -float(DUMMY), float(DUMMY), ALU.mult, ALU.add))
            V.tensor_tensor(tcol[:, 1:2], tcol[:, 1:2], tcol[:, 4:5], ALU.add)
            V.tensor_copy(twide[:, 1, :], tcol[:, 3:4].broadcast_to([128, 128])).then_inc(map_rdy, 1)
            dve.wait_ge(mapT_rdy, 2)
            V.tensor_scalar(expert_of[:, 1, :], bank[5][:, 384:512], -1.0, float(E), ALU.mult, ALU.add)
            V.tensor_copy(tmap[:, 1, :], bank[5][0:1, 256:384])
            V.tensor_scalar(tmap[:, 3, :], bank[5][0:1, 384:512], 128.0, None, ALU.mult).then_inc(tmap_rdy, 1)

            d_chain = chain("vector_split")

            def split(j, u, two=0):
                c = d_chain.begin(j, 2)
                dve.wait_ge(xr_in[0][u], (j - u) * 8 + 16)
                if two:
                    dve.wait_ge(xr_in[1][u], (j - NF - u) * 8 + 16)
                if not isinstance(j, int) or j >= 2:
                    dve.wait_ge(xt_rdy, j - 1)
                xr = xrow[u][:, :, 0:C]
                n = 4 >> two
                for i in range(1 + two):
                    at = bass.ds(2 * j - 2 * NF + i if two else j, 1)
                    ins = V.tensor_scalar(second[u][:, n * i:n * i + n], xrow[u][:, n * i:n * i + n, C + 1],
                                          expert_of[:, two, at], float(TOK), ALU.not_equal, ALU.mult)
                c(ins)
                V.tensor_tensor(dest_all[:, bass.ds(j, 1), :].rearrange("p a g -> p (a g)"), second[u][:],
                                xrow[u][:, :, C], ALU.add)
                c(V.tensor_copy(hl[u][:, :, 0, :].bitcast(F32R), xr))
                V.tensor_tensor(hl[u][:, :, 1, :], xr, hl[u][:, :, 0, :], ALU.subtract).then_inc(split_rdy, 1)
                c.end()

            def hidden(j, u, k):
                n = KT * j + k
                m = 128 if k < HT else HR
                dve.wait_ge(silu_rdy, n + 1)
                if k < HT:
                    dve.wait_ge(h3_rdy, HT * j + k + 1)
                    h3 = h3_ps[k % 3][:]
                else:
                    h3 = h1_ps[k % 3][TAIL3:TAIL3 + HR, :]
                dve.wait_ge(w2_rdy, KT // 2 * j + k // 2 + 1)
                V.tensor_tensor(hbuf[(2 * u + k) % 4][0:m, :], sbuf[k % 3][0:m, :], h3, ALU.mult).then_inc(mul_rdy, 1)

            def rows_out(j, u):
                dve.wait_ge(ro_rdy, j + 3)
                if not isinstance(j, int) or j >= 2:
                    dve.wait_ge(y_out[u], (j - u) * 32)
                V.tensor_copy(destc[u][:], dest_all[:, bass.ds(j, 1), :].rearrange("p a g -> p (a g)"))
                V.tensor_reduce(yrow[u], turn_ps[:].rearrange("p (g h c) -> p g c h", g=4, h=2), AX.X, ALU.add
                                ).then_inc(yr_sb, 1)

            def tile(j, u, two, first=False, last=0):
                if not last:
                    split(j + 2, u, two[2])
                for k in range(2, KT):
                    hidden(j, u, k)
                    if k == 4 and not first:
                        rows_out(j - 1, 1 - u)
                if last != 1:
                    hidden(j + 1, 1 - u, 0)
                    hidden(j + 1, 1 - u, 1)

            split(0, 0)
            split(1, 1)
            hidden(0, 0, 0)
            hidden(0, 0, 1)
            tiles(dve, tile)
            rows_out(NT - 1, 1)

            g0, g1 = gate[:, 0], gate[:, 1]
            dve.wait_ge(ex_rdy, 2)
            one(V.tensor_reduce(gsum[:], lg[:], AX.X, ALU.add))
            one(V.reciprocal(g0, gsum[:]))
            one(V.tensor_tensor(g1, top2[:], g0, ALU.mult))
            one(V.scalar_tensor_tensor(gsum[:], g0, 1e-9, g1, ALU.add, ALU.add))
            one(V.reciprocal(gsum[:], gsum[:]))
            for k in range(2):
                ins = V.tensor_tensor(gate[:, k], gate[:, k], gsum[:], ALU.mult)
            ins.then_inc(gate_rdy, 1)
            dve.wait_ge(gate_rdy, 1)

            def gate1(p, v):
                dve.wait_ge(yk_in[v], (p - v) * (32 // RING) + 32)
                y = yk[0][v].rearrange("p (g c) -> p g c", g=GP)
                V.tensor_tensor(y, y, gate_of(0, p), ALU.mult).then_inc(g0_rdy, 1)

            def add(p, v):
                for u in range(2):
                    s = 2 * p + u
                    dve.wait_ge(fin_rdy, s + 9)
                    V.tensor_tensor(stripe(xb, s), stripe(xb, s), fin_ps[v % 2][u][:], ALU.add).then_inc(o_rdy, 1)

            def both(p, v):
                dve.wait_ge(g2_rdy, p + 1)
                dve.wait_ge(g0_rdy, p + 1)
                V.tensor_tensor(yk[0][v], yk[0][v], yk[1][v], ALU.add).then_inc(g1_rdy, 1)

            with dve.Fori(0, NP // RING) as turn:
                for v in range(RING):
                    gate1(RING * turn + v, v)
                    both(RING * turn + v, v)
                    if v:
                        add(RING * turn + v - 1, v - 1)
                add(RING * turn + RING - 1, RING - 1)

        @block.tensor
        def _(pe):
            mm = nc.tensor.matmul
            pe.sem_inc(fin_rdy, 8)
            for s_ in (bc_rdy, cv_rdy, w2_rdy, ro_rdy):
                pe.sem_inc(s_, 2)
            for s_ in (var_rdy, lg_rdy):
                pe.sem_inc(s_, 1)
            pe.wait_ge(const_p, 1)
            pe.wait_ge(const_v, 1)

            def centred(p, v):
                for u in range(2):
                    s = 2 * p + u
                    pe.wait_ge(x_in[v], (p - v) * 16 + 32)
                    if not isinstance(p, int) or p >= 2:
                        pe.wait_ge(y_cen, s - 3)
                    mm(cen_ps[v][u][:], centre[:], stripe(xb, s), start=True, stop=True).then_inc(cen_rdy, 1)

            def var(p, v):
                pe.wait_ge(sq_rdy, 2 * p + 2)
                for g in range(2 * G):
                    ins = mm(var_ps[v][:, 2 * g:2 * g + 2],
                             sq[:].rearrange("p u n -> p (u n)")[:, 128 * g:128 * g + 128], half_col[:],
                             start=True, stop=True)
                ins.then_inc(var_rdy, 1)

            def spread(p):
                pe.wait_ge(rstd_rdy, p + 1)
                for u in range(2):
                    if not isinstance(p, int) or p >= 1:
                        pe.wait_ge(y_rdy, 2 * p + u)
                    for g in range(G):
                        ins = mm(bc_ps[u][:, 128 * g:128 * g + 128],
                                 wide[:].rearrange("p g c -> p (g c)")[:, S * u + 128 * g:S * u + 128 * g + 128],
                                 ident[:], start=True, stop=True)
                    ins.then_inc(bc_rdy, 1)

            def step(p, v):
                if not isinstance(p, int) or p < NP - 2:
                    centred(p + 2, v)
                if not isinstance(p, int) or p < NP - 1:
                    var(p + 1, 1 - v)
                spread(p)

            centred(0, 0)
            centred(1, 1)
            var(0, 0)
            step(0, 0)
            with pe.Fori(1, NP // 2 - 1) as turn_:
                step(2 * turn_ - 1, 1)
                step(2 * turn_, 0)
            step(NP - 3, 1)
            step(NP - 2, 0)
            step(NP - 1, 1)

            pe.wait_ge(wd_rdy, 1)
            for k in range(2):
                if k:
                    pe.wait_ge(wb_rdy, k)
                for t in range(TAPS):
                    ins = nc.tensor.transpose(w_bf[:, C * t:C * t + C],
                                              wdup[:, k, t, :, :].rearrange("o d i -> o (d i)"), ident_bf[0:C, 0:C])
                ins.then_inc(wT_rdy, 1)
            pe.wait_ge(rr_rdy, 1)
            nc.tensor.transpose(bank[7][:, 0:E], rwc[:].rearrange("e d c -> e (d c)"), ident[0:E, 0:E]).then_inc(rT2, 1)
            pe.wait_ge(wb_rdy, 2)

            def pair_up(l):
                pe.wait_ge(agg_rdy, l + 1)
                mm(bank[6][:, 0:2], pair[:], mv2[:, l, :], start=True, stop=True).then_inc(pr_rdy, 1)

            def conv(l, s, u):
                pe.wait_ge(qp_rdy, s + l * NS + 3)
                if l == 0:
                    pe.wait_ge(c1_rdy, s + 1)
                else:
                    pe.wait_ge(x1_rdy, s + 1)
                for t in range(TAPS):
                    ky, kx = divmod(t, 3)
                    ins = mm(conv_ps[u][:], wblk[:, l, t, :], qpad[u][:, :, ky:ky + H, kx:kx + W],
                             start=t == 0, stop=t == TAPS - 1)
                ins.then_inc(cv_rdy, 1)

            pair_up(0)
            pipelined(pe, lambda s, u: conv(0, s, u), lambda s, u: None, NS)
            pair_up(1)
            pe.wait_ge(rwt_rdy, 1)

            def turn_rows(p):
                pe.wait_ge(rn_rdy, p + 1)
                for u in range(2):
                    pe.wait_ge(x1_rdy, 2 * p + u + 3)
                    for g in range(G):
                        ins = mm(rT_ps[u][:, 128 * g:128 * g + 128], x1[u][:, 128 * g:128 * g + 128],
                                 centre[:], start=True, stop=True)
                    ins.then_inc(rT_rdy, 1)
                for u in range(2):
                    for g in range(G):
                        ins = mm(lg_ps[:, 16 * (G * u + g):16 * (G * u + g) + 16], x1[u][:, 128 * g:128 * g + 128],
                                 rwt[:], start=True, stop=True)
                ins.then_inc(lg_rdy, 1)

            def conv_pair(p):
                for u in range(2):
                    conv(1, 2 * p + u, u)

            def stack_weights(p):
                pe.wait_ge(ws_rdy, 2 * p + 2)
                for b in range(3):
                    if b == 2:
                        pe.wait_ge(wt_sb, 4 * p + 1)
                    for t in range(4 * b, min(4 * b + 4, 2 * HT + 1)):
                        ins = nc.tensor.transpose(w_bank(b)[:, 128 * (t % 4):128 * (t % 4) + 128],
                                                  wsp[:, t, :, :].bitcast(F32).rearrange("p d c -> p (d c)"), ident[:])
                    ins.then_inc(wt_ps, 1)
                pe.wait_ge(w2_in, 16 * p + 16)
                wait_apart(pe, wt_sb, 4 * p + 2)
                w2v = wr2[:, 0:HT * 128].rearrange("c (p t) -> c t p", t=HT)
                for t in range(HT):
                    nc.tensor.transpose(w_bank(3)[:, C * t:C * t + C], w2v[:, t, :], ident[0:C, 0:C])
                nc.tensor.transpose(w_bank(3)[0:HR, C * HT:C * KT], wr2[:, HT * 128:HID],
                                    ident[0:C, 0:C]).then_inc(wt_ps, 1)

            def route(p, first=False, last=0):
                stack_weights(p)
                if last != 1:
                    turn_rows(p + 1)
                pe.wait_ge(ch_rdy, p + 2)
                mm(pos_ps, before[:], chosen[:].rearrange("p g e -> p (g e)"), start=True, stop=False)
                for g in range(GP):
                    n = GP - g
                    ins = mm(pos_ps[:, E * (g + 1):E * (GP + 1)].rearrange("p (g e) -> p g e", e=E), ones_bf[:],
                             chosen[:, g, :].unsqueeze(1).broadcast_to([128, n, E]), start=False, stop=g == GP - 1)
                ins.then_inc(pos_rdy, 1)
                if not last:
                    conv_pair(p + 2)

            conv_pair(0)
            turn_rows(0)
            conv_pair(1)
            pairs(pe, route)
            for i in range(2):
                pe.wait_ge(map_rdy, i + 1)
                mm(bank[5][0:1, 256 * i:256 * i + 128], tcol[:, i:i + 1], ident[:], start=True, stop=True)
                mm(bank[5][:, 256 * i + 128:256 * i + 256], twide[:, i, :], ident[:], start=True, stop=True
                   ).then_inc(mapT_rdy, 1)

            def turn(j, u, first=False):
                pe.wait_ge(split_rdy, j + 3)
                if not first:
                    pe.wait_ge(yr_sb, j)
                for g in range(4):
                    ins = nc.tensor.transpose(turn_ps[:, 128 * g:128 * g + 128],
                                              hl[u][:, g, :, :].rearrange("p d c -> p (d c)"), ident[:])
                ins.then_inc(xt_rdy, 1)

            def up(j, u, k, two=0):
                n = KT * j + k
                if k == 0:
                    pe.wait_ge(wt_in[0][u], (j - u) * 16 + 32)
                    if two:
                        pe.wait_ge(wt_in[1][u], (j - NF - u) * 16 + 32)
                    pe.wait_ge(xt_sb, j + 1)
                pe.wait_ge(mul_rdy, n + 1)
                if k < HT:
                    parts = ((h1_ps, k, h1_rdy), (h3_ps, HT + k, h3_rdy))
                else:
                    parts = ((h1_ps, 2 * HT, h1_rdy),)
                for ps, c, rdy in parts:
                    for i in range(1 + two):
                        rows_ = slice(TH * i, TH * i + (T >> two))
                        for p in range(2):
                            ins = mm(ps[k % 3][:, rows_], wbuf[i][u][:, 128 * c:128 * c + 128], xT[p][u][:, rows_],
                                     start=p == 0, stop=p == 1)
                    ins.then_inc(rdy, 1)

            def down(j, u, k, two=0):
                if k == 0:
                    pe.wait_ge(y_sb, j + 1)
                wait_apart(pe, mul_rdy, KT * j + k + 5)
                for e in range(1 + two):
                    rows_ = slice(TH * e, TH * e + (T >> two))
                    for i in range(k, k + 2):
                        m = 128 if i < HT else HR
                        h = 64 * (i % 2)
                        ins = mm(y_ps[h:h + 64, rows_], w2buf[e][u][0:m, i, :], hbuf[(2 * u + i) % 4][0:m, rows_],
                                 start=i < 2 and e == 0, stop=i >= KT - 2 and e == two)
                ins.then_inc(w2_rdy, 1)

            def rows_out(j, u, last=False):
                pe.wait_ge(y_sb, j + 2)
                if not last:
                    pe.wait_ge(xt_sb, j + 3)
                else:
                    pe.wait_ge(yr_sb, j + 2)
                for g in range(4):
                    ins = nc.tensor.transpose(turn_ps[:, 128 * g:128 * g + 128], ysb[u][:, 128 * g:128 * g + 128],
                                              ident[:])
                ins.then_inc(ro_rdy, 1)

            def tile(j, u, two, first=False, last=0):
                if last != 1:
                    turn(j + 1, 1 - u, first)
                up(j, u, 2, two[0])
                up(j, u, 3, two[0])
                down(j, u, 0, two[0])
                up(j, u, 4, two[0])
                if not first:
                    rows_out(j - 1, 1 - u, last == 1)
                up(j, u, 5, two[0])
                down(j, u, 2, two[0])
                if last != 1:
                    up(j + 1, 1 - u, 0, two[1])
                    up(j + 1, 1 - u, 1, two[1])
                down(j, u, 4, two[0])

            turn(0, 0, True)
            up(0, 0, 0)
            up(0, 0, 1)
            tiles(pe, tile)
            rows_out(NT - 1, 1, True)

            def turn_back(p, v):
                pe.wait_ge(g1_rdy, p + 1)
                pe.wait_ge(o_rdy, 2 * p + 2)
                for u in range(2):
                    for g in range(G):
                        ins = nc.tensor.transpose(fin_ps[v % 2][u][:, 128 * g:128 * g + 128],
                                                  yk[0][v][:, S * u + 128 * g:S * u + 128 * g + 128], ident[:])
                    ins.then_inc(fin_rdy, 1)

            with pe.Fori(0, NP // RING) as turn_:
                for v in range(RING):
                    turn_back(RING * turn_ + v, v)


_INS = ['x', 'L0_conv_gamma1', 'L0_conv_beta1', 'L0_conv_w1', 'L0_conv_gamma2', 'L0_conv_beta2', 'L0_conv_w2',
        'L0_conv_pat', 'L0_ffn_router_w', 'L0_ffn_w1', 'L0_ffn_w2', 'L0_ffn_w3']


def kernel(**inputs):
    import numpy as np
    import concourse.bacc as bacc
    from concourse import mybir as mb
    from concourse.bass_utils import run_bass_kernel_spmd

    nc = bacc.Bacc("TRN2", target_bir_lowering=False, num_devices=1)
    arrays, args = {}, []
    for name in _INS:
        a = np.ascontiguousarray(inputs[name])
        arrays[f"in_{name}"] = a
        args.append(nc.dram_tensor(f"in_{name}", a.shape, mb.dt.from_np(a.dtype), kind="ExternalInput").ap())
    shape = inputs['x'].shape
    args.append(nc.dram_tensor("out_0", shape, mb.dt.from_np(np.dtype("float32")), kind="ExternalOutput").ap())
    conv_moe_kernel(nc, *args)
    r = run_bass_kernel_spmd(nc, [arrays], core_ids=[0])
    return r.results[0]["out_0"]
```
